# Optimizing a Trainium2 kernel written in Bass

```python
import numpy as np
import jax
import jax.numpy as jnp

def _softmax(x, axis=-1):
    return jax.nn.softmax(x, axis=axis)

def _gelu(x):
    return jax.nn.gelu(x, approximate=True)

def _silu(x):
    return jax.nn.silu(x)

def _sigmoid(x):
    return jax.nn.sigmoid(x)

def _layernorm(x, axis=-1, eps=1e-05):
    m = jnp.mean(x, axis=axis, keepdims=True)
    v = jnp.var(x, axis=axis, keepdims=True)
    return (x - m) / jnp.sqrt(v + eps)

def _scatter_add(tgt, idx, src, axis=0):
    return tgt.at[idx].add(src)

def _segment_sum(src, seg, n):
    return jax.ops.segment_sum(src, seg, n)
kernel_name = 'mk_macaron_d1_jaxref_r4_e2ba7e'

def setup_inputs(seed: int=0):
    np.random.seed(seed)
    _w = jnp.asarray

    def _L0_attn_setup():
        import jax, jax.numpy as jnp
        import numpy as np
        B, S, D = (8, 1024, 256)
        H, DK, DV, L = (8, 64, 64, 64)
        key = jax.random.key(seed)
        ks = jax.random.split(key, 6)
        x = jax.random.normal(ks[0], (B, S, D), dtype=jnp.float32)
        sd = 1.0 / np.sqrt(D)
        Wq = jax.random.normal(ks[1], (D, H * DK), dtype=jnp.float32) * sd
        Wk = jax.random.normal(ks[2], (D, H * DK), dtype=jnp.float32) * sd
        Wv = jax.random.normal(ks[3], (D, H * DV), dtype=jnp.float32) * sd
        betas = jax.random.normal(ks[4], (1, H, 1, DV), dtype=jnp.float32)
        Wo = jax.random.normal(ks[5], (H * DV, D), dtype=jnp.float32) * (1.0 / np.sqrt(H * DV))
        return {'x': x, 'Wq': Wq, 'Wk': Wk, 'Wv': Wv, 'betas': betas, 'Wo': Wo}
    _L0_attn_in = _L0_attn_setup()

    def _L0_ffn_setup():
        import jax, jax.numpy as jnp
        import numpy as np
        import math
        D = 256
        H = 16
        E = 8
        TOPK = 2
        LAT = D // 2
        KPH = LAT // H
        HD = D // H

        def _forward(hs, q_w, q_b, k_w, k_b, v_w, v_b, o_w, o_b, router_w, router_b, w1, b1, w2, b2):
            B, S, _ = hs.shape
            Q = (hs @ q_w + q_b).reshape(B, S, H, HD).transpose(0, 2, 1, 3)
            K = (hs @ k_w + k_b).reshape(B, S, H, KPH).transpose(0, 2, 1, 3)
            V = (hs @ v_w + v_b).reshape(B, S, H, KPH).transpose(0, 2, 1, 3)
            scores = jnp.einsum('bhsk,bhtk->bhst', Q[..., :KPH], K) / math.sqrt(KPH)
            attn = jax.nn.softmax(scores, axis=-1)
            ao = jnp.einsum('bhst,bhtv->bhsv', attn, V)
            ao = ao.transpose(0, 2, 1, 3).reshape(B, S, H * KPH)
            ao = jnp.concatenate([ao, jnp.zeros((B, S, D - LAT), ao.dtype)], axis=-1)
            mla_out = ao @ o_w + o_b
            probs = jax.nn.softmax(mla_out @ router_w + router_b, axis=-1)
            topw, topi = jax.lax.top_k(probs, TOPK)
            topw = topw / (topw.sum(-1, keepdims=True) + 1e-08)
            combine = jnp.sum(jax.nn.one_hot(topi, E, dtype=probs.dtype) * topw[..., None], axis=-2)
            h1 = jnp.einsum('bsd,edf->ebsf', mla_out, w1) + b1[:, None, None, :]
            h1 = jax.nn.gelu(h1, approximate=False)
            h2 = jnp.einsum('ebsf,efd->ebsd', h1, w2) + b2[:, None, None, :]
            moe_out = jnp.einsum('bse,ebsd->bsd', combine, h2)
            return hs + 0.3 * moe_out
        key = jax.random.key(seed)
        ks = jax.random.split(key, 16)
        s = 0.02
        inp = {'hidden_states': jax.random.normal(ks[0], (2, 512, D), jnp.float32), 'q_w': jax.random.normal(ks[1], (D, D), jnp.float32) * s, 'q_b': jnp.zeros((D,), jnp.float32), 'k_w': jax.random.normal(ks[2], (D, LAT), jnp.float32) * s, 'k_b': jnp.zeros((LAT,), jnp.float32), 'v_w': jax.random.normal(ks[3], (D, LAT), jnp.float32) * s, 'v_b': jnp.zeros((LAT,), jnp.float32), 'o_w': jax.random.normal(ks[4], (D, D), jnp.float32) * s, 'o_b': jnp.zeros((D,), jnp.float32), 'router_w': jax.random.normal(ks[5], (D, E), jnp.float32) * s, 'router_b': jnp.zeros((E,), jnp.float32), 'w1': jax.random.normal(ks[6], (E, D, 2 * D), jnp.float32) * s, 'b1': jnp.zeros((E, 2 * D), jnp.float32), 'w2': jax.random.normal(ks[7], (E, 2 * D, D), jnp.float32) * s, 'b2': jnp.zeros((E, D), jnp.float32)}
        return inp
    _L0_ffn_in = _L0_ffn_setup()
    _d = {'L0_attn_x': _L0_attn_in['x'], 'L0_attn_Wq': _L0_attn_in['Wq'], 'L0_attn_Wk': _L0_attn_in['Wk'], 'L0_attn_Wv': _L0_attn_in['Wv'], 'L0_attn_betas': _L0_attn_in['betas'], 'L0_attn_Wo': _L0_attn_in['Wo'], 'L0_ffn_q_w': _L0_ffn_in['q_w'], 'L0_ffn_q_b': _L0_ffn_in['q_b'], 'L0_ffn_k_w': _L0_ffn_in['k_w'], 'L0_ffn_k_b': _L0_ffn_in['k_b'], 'L0_ffn_v_w': _L0_ffn_in['v_w'], 'L0_ffn_v_b': _L0_ffn_in['v_b'], 'L0_ffn_o_w': _L0_ffn_in['o_w'], 'L0_ffn_o_b': _L0_ffn_in['o_b'], 'L0_ffn_router_w': _L0_ffn_in['router_w'], 'L0_ffn_router_b': _L0_ffn_in['router_b'], 'L0_ffn_w1': _L0_ffn_in['w1'], 'L0_ffn_b1': _L0_ffn_in['b1'], 'L0_ffn_w2': _L0_ffn_in['w2'], 'L0_ffn_b2': _L0_ffn_in['b2']}
    _x0 = _d['L0_attn_x']
    _d['L0_attn_x'] = jax.random.normal(jax.random.fold_in(jax.random.key(seed), 1), (8, 512, 256), dtype=_x0.dtype)
    del _x0
    return _d

def reference(L0_attn_x, L0_attn_Wq, L0_attn_Wk, L0_attn_Wv, L0_attn_betas, L0_attn_Wo, L0_ffn_q_w, L0_ffn_q_b, L0_ffn_k_w, L0_ffn_k_b, L0_ffn_v_w, L0_ffn_v_b, L0_ffn_o_w, L0_ffn_o_b, L0_ffn_router_w, L0_ffn_router_b, L0_ffn_w1, L0_ffn_b1, L0_ffn_w2, L0_ffn_b2):

    def _L0_attn_ref(x, Wq, Wk, Wv, betas, Wo):
        import jax, jax.numpy as jnp
        import numpy as np
        B, S, D = (8, 1024, 256)
        H, DK, DV, L = (8, 64, 64, 64)
        b, s, d = x.shape
        n_seq = s // L
        xs = x.reshape(b, n_seq, L, d)

        def proj(W, dh):
            p = xs @ W
            return p.reshape(b, n_seq, L, H, dh).transpose(1, 0, 3, 2, 4)
        q = proj(Wq, DK)
        k = proj(Wk, DK)
        v = proj(Wv, DV)
        scale = 1.0 / np.sqrt(DK)
        gate = jax.nn.sigmoid(betas)
        mem0 = jnp.zeros((b, H, DK, DV), dtype=x.dtype)
        z0 = jnp.ones((b, H, DK, 1), dtype=x.dtype) / DK

        def step(carry, inp):
            mem, z = carry
            q_s, k_s, v_s = inp
            sq = jax.nn.elu(q_s) + 1.0
            att_mem = sq @ mem / (sq @ z)
            sk = jax.nn.elu(k_s) + 1.0
            mem = mem + jnp.einsum('bhlk,bhlv->bhkv', sk, v_s)
            z = z + sk.sum(axis=-2, keepdims=True).transpose(0, 1, 3, 2)
            att_dot = jax.nn.softmax(jnp.einsum('bhik,bhjk->bhij', q_s, k_s) * scale, axis=-1)
            att = att_dot @ v_s
            att = gate * att_mem + (1.0 - gate) * att
            return ((mem, z), att)
        _, outs = jax.lax.scan(step, (mem0, z0), (q, k, v))
        out = outs.transpose(1, 0, 3, 2, 4).reshape(b, s, H * DV)
        return out @ Wo

    def _L0_ffn_ref(hidden_states, q_w, q_b, k_w, k_b, v_w, v_b, o_w, o_b, router_w, router_b, w1, b1, w2, b2):
        import jax, jax.numpy as jnp
        import numpy as np
        import math
        D = 256
        H = 16
        E = 8
        TOPK = 2
        LAT = D // 2
        KPH = LAT // H
        HD = D // H

        def _forward(hs, q_w, q_b, k_w, k_b, v_w, v_b, o_w, o_b, router_w, router_b, w1, b1, w2, b2):
            B, S, _ = hs.shape
            Q = (hs @ q_w + q_b).reshape(B, S, H, HD).transpose(0, 2, 1, 3)
            K = (hs @ k_w + k_b).reshape(B, S, H, KPH).transpose(0, 2, 1, 3)
            V = (hs @ v_w + v_b).reshape(B, S, H, KPH).transpose(0, 2, 1, 3)
            scores = jnp.einsum('bhsk,bhtk->bhst', Q[..., :KPH], K) / math.sqrt(KPH)
            attn = jax.nn.softmax(scores, axis=-1)
            ao = jnp.einsum('bhst,bhtv->bhsv', attn, V)
            ao = ao.transpose(0, 2, 1, 3).reshape(B, S, H * KPH)
            ao = jnp.concatenate([ao, jnp.zeros((B, S, D - LAT), ao.dtype)], axis=-1)
            mla_out = ao @ o_w + o_b
            probs = jax.nn.softmax(mla_out @ router_w + router_b, axis=-1)
            topw, topi = jax.lax.top_k(probs, TOPK)
            topw = topw / (topw.sum(-1, keepdims=True) + 1e-08)
            combine = jnp.sum(jax.nn.one_hot(topi, E, dtype=probs.dtype) * topw[..., None], axis=-2)
            h1 = jnp.einsum('bsd,edf->ebsf', mla_out, w1) + b1[:, None, None, :]
            h1 = jax.nn.gelu(h1, approximate=False)
            h2 = jnp.einsum('ebsf,efd->ebsd', h1, w2) + b2[:, None, None, :]
            moe_out = jnp.einsum('bse,ebsd->bsd', combine, h2)
            return hs + 0.3 * moe_out
        return _forward(hidden_states, q_w, q_b, k_w, k_b, v_w, v_b, o_w, o_b, router_w, router_b, w1, b1, w2, b2)
    x = L0_attn_x
    x = x + 0.5 * _L0_ffn_ref(_layernorm(x, axis=-1), L0_ffn_q_w, L0_ffn_q_b, L0_ffn_k_w, L0_ffn_k_b, L0_ffn_v_w, L0_ffn_v_b, L0_ffn_o_w, L0_ffn_o_b, L0_ffn_router_w, L0_ffn_router_b, L0_ffn_w1, L0_ffn_b1, L0_ffn_w2, L0_ffn_b2)
    x = x + _L0_attn_ref(_layernorm(x, axis=-1), L0_attn_Wq, L0_attn_Wk, L0_attn_Wv, L0_attn_betas, L0_attn_Wo)
    x = x + 0.5 * _L0_ffn_ref(_layernorm(x, axis=-1), L0_ffn_q_w, L0_ffn_q_b, L0_ffn_k_w, L0_ffn_k_b, L0_ffn_v_w, L0_ffn_v_b, L0_ffn_o_w, L0_ffn_o_b, L0_ffn_router_w, L0_ffn_router_b, L0_ffn_w1, L0_ffn_b1, L0_ffn_w2, L0_ffn_b2)
    return x

_drawn_inputs = setup_inputs


def setup_inputs(seed=0):
    import zlib

    import numpy as np

    out = dict(_drawn_inputs(seed))
    spreads = {'L0_ffn_q_b': (0.0, 0.8),
     'L0_ffn_k_b': (0.0, 0.8),
     'L0_ffn_v_b': (0.0, 0.8),
     'L0_ffn_o_b': (0.0, 0.604),
     'L0_ffn_router_b': (0.0, 0.596),
     'L0_ffn_b1': (0.0, 0.8),
     'L0_ffn_b2': (0.0, 0.589)}
    factors = {'L0_ffn_q_w': 8.0,
     'L0_ffn_k_w': 8.0,
     'L0_ffn_v_w': 8.0,
     'L0_ffn_o_w': 8.0,
     'L0_ffn_router_w': 5.931,
     'L0_ffn_w1': 8.0,
     'L0_ffn_w2': 8.0}
    for name, (base, spread) in spreads.items():
        noise = np.random.default_rng([zlib.crc32(name.encode()), seed]).standard_normal(out[name].shape)
        drawn = base * np.exp(spread * noise) if base else spread * noise
        out[name] = jnp.asarray(drawn.astype(out[name].dtype))
    for name, factor in factors.items():
        out[name] = (out[name] * factor).astype(out[name].dtype)
    return out
```

```python
from contextlib import ExitStack

import numpy as np

import concourse.bass as bass
from concourse import mybir

ALU = mybir.AluOpType
ACT = mybir.ActivationFunctionType
F32 = mybir.dt.float32
BF16 = mybir.dt.bfloat16
AX = mybir.AxisListType

P = 128
EPS = 1e-5


def wait(eng, sem, value):
    if not (isinstance(value, int) and value <= 0):
        eng.wait_ge(sem, value)


class Steps:

    def __init__(self, eng, sem, unit, per_unit):
        self.eng, self.sem, self.base, self.per_unit, self.n = eng, sem, unit * per_unit, per_unit, 0

    def own(self, instruction):
        instruction.then_inc(self.sem, 1)
        self.n += 1
        self.eng.wait_ge(self.sem, self.base + self.n)

    def end(self):
        assert self.n == self.per_unit, (self.n, self.per_unit)


def over_batches(eng, first, middle, last, start, n):
    first(start)
    with eng.Fori(start, start + n - 1) as b:
        middle(b)
    last(start + n - 1)


LN_STEPS = 7


def layernorm(dve, s, X, HS, stats, mv, ve, sd, rs, T, var_ready, sd_ready, hs_ready, unit, carrier):
    for t in range(T):
        last = dve.bn_stats(stats[:, t, :], X[:, t, :])
    s.own(last)
    dve.memset(carrier, 0.0)
    for t in range(T):
        last = dve.bn_aggr(mv[:, t, :], stats[:, t, :])
    s.own(last)
    dve.tensor_scalar(ve[:, :], mv[:, :, 1], EPS, None, ALU.add).then_inc(var_ready, 1)
    dve.wait_ge(sd_ready, unit + 1)
    s.own(dve.reciprocal(rs[:, :], sd[:, :]))
    s.own(dve.tensor_tensor(sd[:, :], rs[:, :], rs[:, :], ALU.mult))
    s.own(dve.tensor_tensor(sd[:, :], sd[:, :], ve[:, :], ALU.mult))
    s.own(dve.tensor_scalar(sd[:, :], sd[:, :], -0.5, 1.5, ALU.mult, ALU.add))
    s.own(dve.tensor_tensor(rs[:, :], rs[:, :], sd[:, :], ALU.mult))
    for t in range(T):
        last = dve.tensor_scalar(HS[:, t, :], X[:, t, :], mv[:, t, 0:1], rs[:, t:t + 1],
                                 ALU.subtract, ALU.mult)
    last.then_inc(hs_ready, 1)


def ffn_pass(nc, new_sem, tag, nth, x_in, x_out, bank, ident, tri, w, scratch, dims):
    B, S, D, H, HD, KPH, E, F = dims
    T, DC, FC = S // P, D // P, F // P
    QUARTERS = 4
    HQ = H // QUARTERS
    PARTS = 3
    TERMS = [(0, 0), (1, 0), (2, 0), (0, 1), (1, 1), (0, 2)]
    K_MAX = 96
    K_EXP = K_MAX + PARTS
    PV_W = 32
    SC = H * T
    PER_Q = SC // QUARTERS
    NF = E * FC
    SCORE_SCALE = 1.0 / float(np.sqrt(KPH))
    OUT_SCALE = 0.5 * 0.3
    START = nth * B
    A_FRONT, A_SCM, A_POST = LN_STEPS + 3, 3 * QUARTERS, T + 14
    q_scr, k_scr, m_scr = scratch

    with ExitStack() as ctx:
        def sb(name, shape, dt=F32):
            return ctx.enter_context(nc.sbuf_tensor(f"{tag}_{name}", shape, dt))

        def sem(name):
            return new_sem(f"ffn_{name}")

        X = sb("x", [P, T, D])
        HS = sb("hs", [P, T, D])
        XR = sb("xr", [P, T, D])
        Y = sb("y", [P, T, D])
        stats = sb("stats", [P, T, 6])
        mv = sb("mv", [P, T, 2])
        ve, sd, rs = sb("ve", [P, T]), sb("sd", [P, T]), sb("rs", [P, T])
        carrier = sb("carrier", [P, 1])
        hsT = sb("hsT", [P, DC, S])
        qf, kf = sb("qf", [P, S]), sb("kf", [P, S])
        qres, kres = sb("qres", [P, S]), sb("kres", [P, S])
        q3, k3 = sb("q3", [P, PARTS, S], BF16), sb("k3", [P, PARTS, S], BF16)
        QS, KS = sb("QS", [K_EXP, H, S], BF16), sb("KS", [K_EXP, H, S], BF16)
        V = sb("V", [P, T, H, PV_W])
        M = sb("M", [P, T, H])
        mres = sb("mres", [P, T, HQ])
        m3 = sb("m3", [P, T, PARTS, HQ], BF16)
        mT = sb("mT", [PARTS * HQ, S], BF16)
        PT = sb("PT", [P, 8, S])
        PVS = sb("PVS", [P, QUARTERS, S])
        rec = sb("rec", [P, T, H])
        AO = sb("AO", [P, T, H * KPH])
        aoT = sb("aoT", [P, S])
        mlaT = sb("mlaT", [P, DC, S])
        L = sb("L", [P, T, E])
        pr = sb("pr", [P, T, E])
        small = sb("small", [P, T])
        gt, eq = sb("gt", [P, T, E, E]), sb("eq", [P, T, E, E])
        rank = sb("rank", [P, T, E])
        comb = sb("comb", [P, T, E])
        cT = sb("cT", [P, S])
        Cb = sb("Cb", [P, 2, S])
        Gt = sb("Gt", [P, 2, S])
        G = sb("G", [P, 2, S])
        OT = sb("OT", [P, DC, S])
        zero = sb("zero", [P, 1])

        x_loaded, xr_ready, y_ready, y_stored = sem("x_loaded"), sem("xr_ready"), sem("y_ready"), sem("y_stored")
        var_ready, sd_ready, hs_ready = sem("var_ready"), sem("sd_ready"), sem("hs_ready")
        hsT_filled, hsT_ready = sem("hsT_filled"), sem("hsT_ready")
        q_filled, k_filled, v_filled = sem("q_filled"), sem("k_filled"), sem("v_filled")
        q_ready, k_ready, v_ready = sem("q_ready"), sem("k_ready"), sem("v_ready")
        q3_ready, k3_ready = sem("q3_ready"), sem("k3_ready")
        split_stored, stacks_loaded = sem("split_stored"), sem("stacks_loaded")
        scm_filled, scm_drained = sem("scm_filled"), sem("scm_drained")
        m3_ready, mT_filled = sem("m3_ready"), sem("mT_filled")
        m_stored, m_loaded = sem("m_stored"), [sem(f"m_loaded{q}") for q in range(QUARTERS)]
        sce_filled, probs_ready = sem("sce_filled"), sem("probs_ready")
        pv_used, pvs_ready = sem("pv_used"), sem("pvs_ready")
        pvT_filled, ao_ready = sem("pvT_filled"), sem("ao_ready")
        aoT_filled, aoT_ready = sem("aoT_filled"), sem("aoT_ready")
        mla_filled, mlaT_ready = sem("mla_filled"), sem("mlaT_ready")
        router_filled, logits_ready, ex_ready = sem("router_filled"), sem("logits_ready"), sem("ex_ready")
        comb_ready, cT_filled, cT_ready = sem("comb_ready"), sem("cT_filled"), sem("cT_ready")
        c_filled, cb_ready = sem("c_filled"), sem("cb_ready")
        h1_filled, gelu_ready, g_ready, g_used = sem("h1_filled"), sem("gelu_ready"), sem("g_ready"), sem("g_used")
        out_filled, ot_ready, nat_filled = sem("out_filled"), sem("ot_ready"), sem("nat_filled")
        dve_front, dve_scm, dve_post, pool_front = sem("dve_front"), sem("dve_scm"), sem("dve_post"), sem("pool_front")
        init = sem("init")
        INIT = 8 * (nth + 1)

        H1, C_BANK, OUT, SCM = bank[0:3], bank[3], bank[4:6], bank[6:8]
        SCE = [bank[2], bank[3], bank[6], bank[7]]
        PVB = bank[4:6]

        def scm_ring(a, n):
            return SCM[n % 2], a * QUARTERS * (PER_Q + 1) + n - 1

        block = ctx.enter_context(nc.Block())

        @block.sync
        def _(sp):
            def load(a):
                wait(sp, xr_ready, a)
                sp.dma_start(X[:, :, :], x_in[a - START].rearrange("(t p) d -> p t d", p=P)).then_inc(x_loaded, 16)

            def stacks(a):
                sp.wait_ge(q3_ready, a + 1)
                sp.dma_start(q_scr.rearrange("c r t -> r c t"), q3[:, :, :]).then_inc(split_stored, 16)
                sp.wait_ge(k3_ready, a + 1)
                sp.dma_start(k_scr.rearrange("c r t -> r c t"), k3[:, :, :]).then_inc(split_stored, 16)
                wait(sp, sce_filled, a * SC)
                sp.wait_ge(split_stored, a * 32 + 32)
                sp.wait_ge(init, INIT)
                for n, (i, j) in enumerate(TERMS):
                    at = slice(n * KPH, (n + 1) * KPH)
                    sp.dma_start(QS[at, :, :], q_scr[i].rearrange("(h k) t -> k h t", k=KPH)).then_inc(stacks_loaded, 16)
                    sp.dma_start(KS[at, :, :], k_scr[j].rearrange("(h k) t -> k h t", k=KPH)).then_inc(stacks_loaded, 16)

            def maxima(a):
                for q in range(QUARTERS):
                    sp.wait_ge(scm_drained, (a * QUARTERS + q + 1) * (PER_Q + 1))
                    sp.dma_start(m_scr[q], mT[:, :]).then_inc(m_stored, 16)
                    sp.wait_ge(m_stored, (a * QUARTERS + q) * 16 + 16)
                    sp.dma_start(QS[K_MAX:K_EXP, q * HQ:(q + 1) * HQ, :],
                                 m_scr[q].rearrange("(c h) t -> c h t", h=HQ)).then_inc(m_loaded[q], 16)

            def store(m):
                wait(sp, y_ready, 2 * m + 2)
                sp.dma_start(x_out[m - START].rearrange("(t p) d -> p t d", p=P), Y[:, :, :]).then_inc(y_stored, 16)

            def first(a):
                load(a)
                stacks(a)
                maxima(a)

            def middle(b):
                first(b + 1)
                store(b)

            over_batches(sp, first, middle, store, START, B)
            sp.wait_ge(y_stored, 16 * (START + B + 1))
            sp.wait_ge(m_stored, 16 * QUARTERS * (START + B))
            sp.wait_ge(split_stored, 32 * (START + B))

        @block.gpsimd
        def _(pool):
            pool.memset(QS[0:K_MAX, :, :], 0.0).then_inc(init, 1)
            pool.memset(KS[0:K_MAX, :, :], 0.0).then_inc(init, 1)
            pool.wait_ge(init, INIT - 6)
            pool.memset(KS[K_MAX:K_EXP, :, :], 1.0).then_inc(init, 1)
            pool.wait_ge(init, INIT - 5)
            pool.memset(V[:, :, :, :], 0.0).then_inc(init, 1)
            pool.memset(cT[:, :], 0.0).then_inc(init, 1)
            pool.memset(zero[:, :], 0.0).then_inc(init, 1)
            if nth == 0:
                pool.memset(Y[:, 0, 0:1], 0.0).then_inc(y_stored, 16)
            pool.wait_ge(init, INIT - 2)
            nothing = zero[:, :].to_broadcast([P, S])
            pool.memset(V[:, :, :, KPH:KPH + 1], 1.0).then_inc(init, 2)

            def split_k(a):
                s = Steps(pool, pool_front, a, 3)
                pool.wait_ge(k_ready, a + 1)
                wait(pool, split_stored, a * 32)
                s.own(pool.tensor_tensor(k3[:, 0, :], kf[:, :], nothing, ALU.add))
                s.own(pool.tensor_tensor(kres[:, :], kf[:, :], k3[:, 0, :], ALU.subtract))
                s.own(pool.tensor_tensor(k3[:, 1, :], kres[:, :], nothing, ALU.add))
                pool.tensor_tensor(k3[:, 2, :], kres[:, :], k3[:, 1, :], ALU.subtract).then_inc(k3_ready, 1)
                s.end()

            over_batches(pool, split_k, lambda b: split_k(b + 1), lambda m: None, START, B)

        @block.scalar
        def _(act):
            def front(a):
                act.wait_ge(var_ready, a + 1)
                act.activation(sd[:, :], ve[:, :], ACT.Sqrt).then_inc(sd_ready, 1)
                for c in range(DC):
                    act.wait_ge(hsT_filled, a * DC + c + 1)
                    act.activation(hsT[:, c, :], bank[c], ACT.Copy).then_inc(hsT_ready, 1)
                wait(act, q3_ready, a)
                act.wait_ge(q_filled, a + 1)
                act.activation(qf[:, :], bank[2][:, :], ACT.Identity, bias=w["q_bs"][:, 0:1],
                               scale=SCORE_SCALE).then_inc(q_ready, 1)
                wait(act, k3_ready, a)
                act.wait_ge(k_filled, a + 1)
                act.activation(kf[:, :], bank[3][:, :], ACT.Identity, bias=w["k_b"][:, 0:1]).then_inc(k_ready, 1)

            def moe(m):
                for e in range(E):
                    act.wait_ge(c_filled, m * E + e + 1)
                    wait(act, g_ready, m * NF + (e - 1) * FC) if e >= 2 else None
                    act.activation(Cb[:, e % 2, :], C_BANK[:, :], ACT.Copy).then_inc(cb_ready, 1)
                    for f in range(FC):
                        i = e * FC + f
                        act.wait_ge(h1_filled, m * NF + i + 1)
                        if i >= 2:
                            act.wait_ge(g_ready, m * NF + i - 1)
                        act.activation(Gt[:, i % 2, :], H1[i % 3][:, :], ACT.Gelu,
                                       bias=w["b1"][:, e, f:f + 1]).then_inc(gelu_ready, 1)
                act.wait_ge(out_filled, m + 1)
                for c in range(DC):
                    act.activation(OT[:, c, :], OUT[c][:, :], ACT.Copy).then_inc(ot_ready, 1)

            def exponentials(a):
                for i in range(SC):
                    act.wait_ge(sce_filled, a * SC + i + 1)
                    if i >= 8:
                        act.wait_ge(pv_used, a * SC + i - 7)
                    act.activation(PT[:, i % 8, :], SCE[i % 4][:, :], ACT.Exp).then_inc(probs_ready, 1)

            def post(a):
                act.wait_ge(aoT_filled, a + 1)
                act.activation(aoT[:, :], bank[4][:, :], ACT.Copy).then_inc(aoT_ready, 1)
                for c in range(DC):
                    act.wait_ge(mla_filled, a * DC + c + 1)
                    act.activation(mlaT[:, c, :], bank[6 + c][:, :], ACT.Identity,
                                   bias=w["o_b"][:, c:c + 1]).then_inc(mlaT_ready, 1)
                act.wait_ge(logits_ready, a + 1)
                act.activation(L[:, :, :], L[:, :, :], ACT.Exp).then_inc(ex_ready, 1)
                act.wait_ge(cT_filled, a + 1)
                act.activation(cT[0:E, :], bank[0][0:E, :], ACT.Copy).then_inc(cT_ready, 1)

            def first(a):
                front(a)
                exponentials(a)
                post(a)

            def middle(b):
                front(b + 1)
                moe(b)
                exponentials(b + 1)
                post(b + 1)

            act.wait_ge(init, INIT)
            over_batches(act, first, middle, moe, START, B)

        @block.vector
        def _(dve):
            def front(a):
                s = Steps(dve, dve_front, a, A_FRONT)
                dve.wait_ge(x_loaded, a * 16 + 16)
                layernorm(dve, s, X, HS, stats, mv, ve, sd, rs, T, var_ready, sd_ready, hs_ready, a, carrier[:, :])
                dve.wait_ge(q_ready, a + 1)
                wait(dve, split_stored, a * 32)
                s.own(dve.tensor_copy(q3[:, 0, :], qf[:, :]))
                s.own(dve.tensor_tensor(qres[:, :], qf[:, :], q3[:, 0, :], ALU.subtract))
                s.own(dve.tensor_copy(q3[:, 1, :], qres[:, :]))
                dve.tensor_tensor(q3[:, 2, :], qres[:, :], q3[:, 1, :], ALU.subtract).then_inc(q3_ready, 1)
                dve.wait_ge(v_filled, a + 1)
                for t in range(T):
                    last = dve.tensor_tensor(V[:, t, :, 0:KPH],
                                             bank[4][:, t * P:(t + 1) * P].rearrange("p (h k) -> p h k", k=KPH),
                                             w["v_b"][:, :].rearrange("p (h k) -> p h k", k=KPH), ALU.add)
                last.then_inc(v_ready, 1)
                s.end()

            def maximum(a, q, j):
                n = q * (PER_Q + 1) + j
                scores, _ = scm_ring(a, n)
                dve.wait_ge(scm_filled, a * SC + q * PER_Q + j + 1)
                h, t = q * HQ + j // T, j % T
                dve.tensor_reduce(M[:, t, h:h + 1], scores[:, :], AX.X, ALU.max).then_inc(scm_drained, 1)

            def split_maxima(a, q, s):
                mq = M[:, :, q * HQ:(q + 1) * HQ]
                dve.wait_ge(scm_drained, a * QUARTERS * (PER_Q + 1) + q * (PER_Q + 1) + PER_Q)
                wait(dve, mT_filled, a * QUARTERS + q)
                s.own(dve.tensor_scalar(m3[:, :, 0, :], mq, -1.0, None, ALU.mult))
                s.own(dve.scalar_tensor_tensor(mres[:, :, :], mq, -1.0, m3[:, :, 0, :], ALU.mult, ALU.subtract))
                s.own(dve.tensor_copy(m3[:, :, 1, :], mres[:, :, :]))
                dve.tensor_tensor(m3[:, :, 2, :], mres[:, :, :], m3[:, :, 1, :], ALU.subtract).then_inc(m3_ready, 1)

            def evacuate_mT(a, q):
                n = q * (PER_Q + 1) + PER_Q
                scores, _ = scm_ring(a, n)
                dve.wait_ge(mT_filled, a * QUARTERS + q + 1)
                wait(dve, m_stored, (a * QUARTERS + q) * 16)
                dve.tensor_copy(mT[:, :], scores.bitcast(BF16)[0:PARTS * HQ, 0:S]).then_inc(scm_drained, 1)

            def quarter_step(a, q, j, s):
                if j < PER_Q:
                    maximum(a, q, j)
                else:
                    split_maxima(a, q, s)
                    evacuate_mT(a, q)

            def scale(m, i):
                if i % FC == 0:
                    dve.wait_ge(cb_ready, m * E + i // FC + 1)
                dve.wait_ge(gelu_ready, m * NF + i + 1)
                if i >= 2:
                    dve.wait_ge(g_used, m * NF + i - 1)
                dve.tensor_tensor(G[:, i % 2, :], Gt[:, i % 2, :], Cb[:, (i // FC) % 2, :],
                                  ALU.mult).then_inc(g_ready, 1)

            def moe(m, a):
                s = Steps(dve, dve_scm, a, A_SCM) if a is not None else None
                for i in range(NF):
                    scale(m, i)
                    if a is not None:
                        q, j = divmod(2 * i, PER_Q)
                        quarter_step(a, q, j, s)
                        quarter_step(a, q, j + 1, s)
                        if j + 2 == PER_Q:
                            quarter_step(a, q, PER_Q, s)
                if a is not None:
                    s.end()
                dve.wait_ge(y_stored, 16 * m + 16)
                dve.wait_ge(xr_ready, m + 1)
                for n in range(2):
                    dve.wait_ge(nat_filled, 2 * m + n + 1)
                    dve.scalar_tensor_tensor(Y[:, 2 * n:2 * n + 2, :].rearrange("p t d -> p (t d)"), bank[n][:, :],
                                             OUT_SCALE, XR[:, 2 * n:2 * n + 2, :].rearrange("p t d -> p (t d)"),
                                             ALU.mult, ALU.add).then_inc(y_ready, 1)

            def pv_out(a):
                for q in range(QUARTERS):
                    dve.wait_ge(pv_used, a * SC + (q + 1) * PER_Q)
                    dve.tensor_copy(PVS[:, q, :], PVB[q % 2][:, :]).then_inc(pvs_ready, 1)

            def post(a):
                s = Steps(dve, dve_post, a, A_POST)
                for t in range(T):
                    dve.wait_ge(pvT_filled, a * T + t + 1)
                    out = bank[t][:, :].rearrange("p (h c) -> p h c", c=PV_W)
                    s.own(dve.reciprocal(rec[:, t, :], out[:, :, KPH]))
                    dve.tensor_tensor(AO[:, t, :].rearrange("p (h k) -> p h k", k=KPH), out[:, :, 0:KPH],
                                      rec[:, t, :].unsqueeze(2).to_broadcast([P, H, KPH]),
                                      ALU.mult).then_inc(ao_ready, 1)
                dve.scalar_tensor_tensor(XR[:, :, :], HS[:, :, :], 0.5, X[:, :, :],
                                         ALU.mult, ALU.add).then_inc(xr_ready, 1)
                per_token = small[:, :].unsqueeze(2).to_broadcast([P, T, E])
                dve.wait_ge(router_filled, a + 1)
                s.own(dve.tensor_tensor(L[:, :, :], bank[5][:, 0:T * E].rearrange("p (t e) -> p t e", e=E),
                                        w["router_b"][:, :].unsqueeze(1).to_broadcast([P, T, E]), ALU.add))
                s.own(dve.tensor_reduce(small[:, :], L[:, :, :], AX.X, ALU.max))
                dve.tensor_tensor(L[:, :, :], L[:, :, :], per_token, ALU.subtract).then_inc(logits_ready, 1)
                dve.wait_ge(ex_ready, a + 1)
                s.own(dve.tensor_reduce(small[:, :], L[:, :, :], AX.X, ALU.add))
                s.own(dve.reciprocal(small[:, :], small[:, :]))
                s.own(dve.tensor_tensor(pr[:, :, :], L[:, :, :], per_token, ALU.mult))
                other = pr[:, :, :].unsqueeze(2).to_broadcast([P, T, E, E])
                this = pr[:, :, :].unsqueeze(3).to_broadcast([P, T, E, E])
                s.own(dve.tensor_tensor(gt[:, :, :, :], other, this, ALU.is_gt))
                s.own(dve.tensor_tensor(eq[:, :, :, :], other, this, ALU.is_equal))
                s.own(dve.tensor_tensor(eq[:, :, :, :], eq[:, :, :, :],
                                        tri[:, :, :].unsqueeze(1).to_broadcast([P, T, E, E]), ALU.mult))
                s.own(dve.tensor_tensor(gt[:, :, :, :], gt[:, :, :, :], eq[:, :, :, :], ALU.add))
                s.own(dve.tensor_reduce(rank[:, :, :], gt[:, :, :, :], AX.X, ALU.add))
                s.own(dve.scalar_tensor_tensor(comb[:, :, :], rank[:, :, :], 1.5, pr[:, :, :], ALU.is_lt, ALU.mult))
                s.own(dve.tensor_reduce(small[:, :], comb[:, :, :], AX.X, ALU.add))
                s.own(dve.tensor_scalar(small[:, :], small[:, :], 1e-8, None, ALU.add))
                s.own(dve.reciprocal(small[:, :], small[:, :]))
                dve.tensor_tensor(comb[:, :, :], comb[:, :, :], per_token, ALU.mult).then_inc(comb_ready, 1)
                s.end()

            def first(a):
                front(a)
                s = Steps(dve, dve_scm, a, A_SCM)
                for q in range(QUARTERS):
                    for j in range(PER_Q + 1):
                        quarter_step(a, q, j, s)
                s.end()
                pv_out(a)
                post(a)

            def middle(b):
                front(b + 1)
                moe(b, b + 1)
                pv_out(b + 1)
                post(b + 1)

            dve.wait_ge(init, INIT)
            over_batches(dve, first, middle, lambda m: moe(m, None), START, B)

        @block.tensor
        def _(pe):
            def front(a):
                pe.wait_ge(hs_ready, a + 1)
                for c in range(DC):
                    for t in range(T):
                        last = pe.transpose(bank[c][:, t * P:(t + 1) * P], HS[:, t, c * P:(c + 1) * P], ident[:, :])
                    last.then_inc(hsT_filled, 1)
                pe.wait_ge(hsT_ready, (a + 1) * DC)
                for filled, to, weight in ((q_filled, bank[2], w["q_w"]), (k_filled, bank[3], w["k_w"])):
                    for c in range(DC):
                        last = pe.matmul(to[:, :], weight[:, c, :], hsT[:, c, :], start=(c == 0), stop=(c == DC - 1))
                    last.then_inc(filled, 1)
                for t in range(T):
                    for c in range(DC):
                        last = pe.matmul(bank[4][:, t * P:(t + 1) * P], hsT[:, c, t * P:(t + 1) * P],
                                         w["v_w"][:, c, :], start=(c == 0), stop=(c == DC - 1))
                last.then_inc(v_filled, 1)
                pe.wait_ge(q_ready, a + 1)
                pe.wait_ge(k_ready, a + 1)
                pe.wait_ge(v_ready, a + 1)

            def score_for_max(a, q, j):
                n = q * (PER_Q + 1) + j
                scores, freed = scm_ring(a, n)
                if j == 0 and q == 0:
                    pe.wait_ge(stacks_loaded, (a + 1) * 2 * len(TERMS) * 16)
                if n >= 2:
                    pe.wait_ge(scm_drained, freed)
                h, t = q * HQ + j // T, j % T
                pe.matmul(scores[:, :], QS[0:K_MAX, h, t * P:(t + 1) * P], KS[0:K_MAX, h, :],
                          start=True, stop=True).then_inc(scm_filled, 1)

            def turn_maxima(a, q):
                n = q * (PER_Q + 1) + PER_Q
                scores, freed = scm_ring(a, n)
                pe.wait_ge(scm_drained, freed)
                pe.wait_ge(m3_ready, a * QUARTERS + q + 1)
                rows = scores.bitcast(BF16)
                for t in range(T):
                    last = pe.transpose(rows[0:PARTS * HQ, t * P:(t + 1) * P],
                                        m3[:, t, :, :].rearrange("p c h -> p (c h)"), w["ident_b"][:, :])
                last.then_inc(mT_filled, 1)

            def quarter_step(a, q, j):
                if j < PER_Q:
                    score_for_max(a, q, j)
                else:
                    turn_maxima(a, q)

            def moe(m, a):
                pe.wait_ge(mlaT_ready, (m + 1) * DC)
                pe.wait_ge(cT_ready, m + 1)

                def second(i):
                    e, f = divmod(i, FC)
                    pe.wait_ge(g_ready, m * NF + i + 1)
                    for c in range(DC):
                        last = pe.matmul(OUT[c][:, :], w["w2"][:, e, f, c * P:(c + 1) * P], G[:, i % 2, :],
                                         start=(i == 0), stop=False)
                    last.then_inc(g_used, 1)

                for i in range(NF):
                    e, f = divmod(i, FC)
                    if f == 0:
                        if e >= 1:
                            pe.wait_ge(cb_ready, m * E + e)
                        pe.matmul(C_BANK[:, :], w["sel"][:, e, :], cT[:, :], start=True, stop=True).then_inc(c_filled, 1)
                    if i >= 3:
                        pe.wait_ge(gelu_ready, m * NF + i - 2)
                    for c in range(DC):
                        last = pe.matmul(H1[i % 3][:, :], w["w1"][:, e, c, f * P:(f + 1) * P], mlaT[:, c, :],
                                         start=(c == 0), stop=(c == DC - 1))
                    last.then_inc(h1_filled, 1)
                    if i >= 1:
                        second(i - 1)
                    if a is not None:
                        q, j = divmod(2 * i, PER_Q)
                        quarter_step(a, q, j)
                        quarter_step(a, q, j + 1)
                        if j + 2 == PER_Q:
                            quarter_step(a, q, PER_Q)
                second(NF - 1)
                for c in range(DC):
                    last = pe.matmul(OUT[c][:, :], w["b2"][:, c * P:(c + 1) * P], cT[:, :], start=False, stop=True)
                last.then_inc(out_filled, 1)
                pe.wait_ge(ot_ready, (m + 1) * DC)
                pe.wait_ge(gelu_ready, (m + 1) * NF)
                for t in range(T):
                    for c in range(DC):
                        last = pe.transpose(bank[t // 2][:, (t % 2) * D + c * P:(t % 2) * D + (c + 1) * P],
                                            OT[:, c, t * P:(t + 1) * P], ident[:, :])
                    if t % 2:
                        last.then_inc(nat_filled, 1)

            def exponentials(a):
                def score(i):
                    q, j = divmod(i, PER_Q)
                    t, h = j // HQ, q * HQ + j % HQ
                    if j == 0:
                        pe.wait_ge(m_loaded[q], a * 16 + 16)
                    if i >= 4:
                        pe.wait_ge(probs_ready, a * SC + i - 3)
                    pe.matmul(SCE[i % 4][:, :], KS[0:K_EXP, h, t * P:(t + 1) * P], QS[0:K_EXP, h, :],
                              start=True, stop=True).then_inc(sce_filled, 1)

                def weigh(i):
                    q, j = divmod(i, PER_Q)
                    t, hq = j // HQ, j % HQ
                    if j == 0 and q >= 2:
                        pe.wait_ge(pvs_ready, a * QUARTERS + q - 1)
                    pe.wait_ge(probs_ready, a * SC + i + 1)
                    last = pe.matmul(PVB[q % 2][hq * PV_W:(hq + 1) * PV_W, :], V[:, t, q * HQ + hq, :],
                                     PT[:, i % 8, :], start=(t == 0), stop=(t == T - 1))
                    last.then_inc(pv_used, 1)

                pe.wait_ge(v_ready, a + 1)
                pe.wait_ge(scm_drained, (a + 1) * QUARTERS * (PER_Q + 1))
                for g in range(SC // HQ + 1):
                    for n in range(HQ):
                        if g < SC // HQ:
                            score(g * HQ + n)
                    for n in range(HQ):
                        if g >= 1:
                            weigh((g - 1) * HQ + n)

            def post(a, m):
                pe.wait_ge(pvs_ready, (a + 1) * QUARTERS)
                if m is not None:
                    pe.wait_ge(y_ready, 2 * m + 2)
                for t in range(T):
                    for q in range(QUARTERS):
                        last = pe.transpose(bank[t][:, q * P:(q + 1) * P], PVS[:, q, t * P:(t + 1) * P], ident[:, :])
                    last.then_inc(pvT_filled, 1)
                for t in range(T):
                    pe.wait_ge(ao_ready, a * T + t + 1)
                    last = pe.transpose(bank[4][:, t * P:(t + 1) * P], AO[:, t, :], ident[:, :])
                last.then_inc(aoT_filled, 1)
                pe.wait_ge(aoT_ready, a + 1)
                for c in range(DC):
                    pe.matmul(bank[6 + c][:, :], w["o_w"][:, c * P:(c + 1) * P], aoT[:, :],
                              start=True, stop=True).then_inc(mla_filled, 1)
                pe.wait_ge(mlaT_ready, (a + 1) * DC)
                for t in range(T):
                    for c in range(DC):
                        last = pe.matmul(bank[5][:, t * E:(t + 1) * E], mlaT[:, c, t * P:(t + 1) * P],
                                         w["router_w"][:, c, :], start=(c == 0), stop=(c == DC - 1))
                last.then_inc(router_filled, 1)
                pe.wait_ge(comb_ready, a + 1)
                for t in range(T):
                    last = pe.transpose(bank[0][0:E, t * P:(t + 1) * P], comb[:, t, :], ident[:, :])
                last.then_inc(cT_filled, 1)
                pe.wait_ge(cT_ready, a + 1)

            def first(a):
                front(a)
                for q in range(QUARTERS):
                    for j in range(PER_Q + 1):
                        quarter_step(a, q, j)
                exponentials(a)
                post(a, None)

            def middle(b):
                front(b + 1)
                moe(b, b + 1)
                exponentials(b + 1)
                post(b + 1, b)

            pe.wait_ge(init, INIT)
            over_batches(pe, first, middle, lambda m: moe(m, None), START, B)


def attention_pass(nc, new_sem, tag, x_in, x_out, bank, ident, ident_b, w, B, S, D, H, DK, LSEG):
    T, DC, NSEG, PAIRS = S // P, D // P, S // LSEG, H // 2
    HK = H * DK
    KC = HK // P
    VW = DK + 1
    SCALE = 1.0 / float(np.sqrt(DK))
    QK = 2 * PAIRS
    FRONT, PER_TILE = LN_STEPS, 9

    with ExitStack() as ctx:
        def sb(name, shape, dt=F32):
            return ctx.enter_context(nc.sbuf_tensor(f"{tag}_{name}", shape, dt))

        def sem(name):
            return new_sem(f"{tag}_{name}")

        X, HS, Y = sb("x", [P, T, D]), sb("hs", [P, T, D]), sb("y", [P, T, D])
        stats, mv = sb("stats", [P, T, 6]), sb("mv", [P, T, 2])
        ve, sd, rs = sb("ve", [P, T]), sb("sd", [P, T]), sb("rs", [P, T])
        carrier = sb("carrier", [P, 1])
        hsT = sb("hsT", [P, DC, S])
        qk = sb("qk", [P, QK, S])
        low = sb("low", [P, 2, S])
        ex = sb("ex", [P, 2, S])
        sqk = sb("sqk", [P, QK, S])
        sk = sb("sk", [P, T, HK])
        V = sb("V", [P, T, H, VW])
        MEM = sb("MEM", [P, NSEG, PAIRS, VW])
        SS = sb("SS", [P, 2, H, LSEG])
        mx, rr = sb("mx", [P, H]), sb("rr", [P, H])
        PB = sb("PB", [P, H, P])
        PBT = sb("PBT", [P, H, P])
        rz = sb("rz", [P, 2, PAIRS])
        AM = sb("AM", [P, HK])
        AL = sb("AL", [P, HK])
        AT = sb("AT", [P, HK])
        attT = sb("attT", [P, KC, P])

        x_loaded, y_ready, y_stored = sem("x_loaded"), sem("y_ready"), sem("y_stored")
        var_ready, sd_ready, hs_ready = sem("var_ready"), sem("sd_ready"), sem("hs_ready")
        hsT_filled, hsT_ready = sem("hsT_filled"), sem("hsT_ready")
        qk_filled, qk_ready, low_ready, ex_ready, sqk_ready = (
            sem("qk_filled"), sem("qk_ready"), sem("low_ready"), sem("ex_ready"), sem("sqk_ready"))
        v_filled, v_ready, sk_filled, sk_ready = sem("v_filled"), sem("v_ready"), sem("sk_filled"), sem("sk_ready")
        u_filled, mem_ready = sem("u_filled"), sem("mem_ready")
        s_filled, s_ready, e_ready, pb_ready = sem("s_filled"), sem("s_ready"), sem("e_ready"), sem("pb_ready")
        pbT_filled, pbT_ready = sem("pbT_filled"), sem("pbT_ready")
        l_filled, am_filled, at_ready = sem("l_filled"), sem("am_filled"), sem("at_ready")
        attT_filled, attT_ready, o_filled = sem("attT_filled"), sem("attT_ready"), sem("o_filled")
        dve_front, dve_tile = sem("dve_front"), sem("dve_tile")
        init = sem("init")
        INIT = 4

        RING = bank[2:6]
        block = ctx.enter_context(nc.Block())

        @block.sync
        def _(sp):
            with sp.Fori(0, B) as a:
                sp.dma_start(X[:, :, :], x_in[a].rearrange("(t p) d -> p t d", p=P)).then_inc(x_loaded, 16)
                wait(sp, y_ready, a * T + T)
                sp.dma_start(x_out[a].rearrange("(t p) d -> p t d", p=P), Y[:, :, :]).then_inc(y_stored, 16)
            sp.wait_ge(y_stored, 16 * (B + 1))

        @block.gpsimd
        def _(pool):
            pool.memset(PB[:, :, :], 0.0).then_inc(init, 1)
            pool.memset(Y[:, 0, 0:1], 0.0).then_inc(y_stored, 16)
            pool.memset(V[:, :, :, DK:VW], 1.0).then_inc(init, 1)
            pool.memset(MEM[:, 0, :, 0:DK], 0.0).then_inc(init, 1)
            pool.memset(MEM[:, 0, :, DK:VW], 1.0 / DK).then_inc(init, 1)

        @block.scalar
        def _(act):
            act.wait_ge(init, INIT)
            with act.Fori(0, B) as a:
                act.wait_ge(var_ready, a + 1)
                act.activation(sd[:, :], ve[:, :], ACT.Sqrt).then_inc(sd_ready, 1)
                for c in range(DC):
                    act.wait_ge(hsT_filled, a * DC + c + 1)
                    act.activation(hsT[:, c, :], bank[c], ACT.Copy).then_inc(hsT_ready, 1)
                for i in range(QK + 1):
                    if i < QK:
                        act.wait_ge(qk_filled, a * QK + i + 1)
                        act.activation(qk[:, i, :], RING[i % 4], ACT.Copy).then_inc(qk_ready, 1)
                    if i >= 1:
                        act.wait_ge(low_ready, a * QK + i)
                        if i >= 3:
                            act.wait_ge(sqk_ready, a * QK + i - 2)
                        act.activation(ex[:, (i - 1) % 2, :], low[:, (i - 1) % 2, :], ACT.Exp).then_inc(ex_ready, 1)
                for t in range(T):
                    act.wait_ge(v_filled, a * T + t + 1)
                    act.activation(V[:, t, :, 0:DK], RING[t].rearrange("p (h v) -> p h v", v=DK),
                                   ACT.Copy).then_inc(v_ready, 1)
                for t in range(T):
                    act.wait_ge(sk_filled, a * T + t + 1)
                    act.activation(sk[:, t, :], RING[t], ACT.Copy).then_inc(sk_ready, 1)
                for t in range(T):
                    act.wait_ge(s_ready, a * T + t + 1)
                    act.activation(SS[:, t % 2, :, :], SS[:, t % 2, :, :], ACT.Exp, scale=SCALE).then_inc(e_ready, 1)
                    act.wait_ge(pbT_filled, a * T + t + 1)
                    for n in range(2):
                        act.activation(PBT[:, n * PAIRS:(n + 1) * PAIRS, :].rearrange("p h i -> p (h i)"),
                                       bank[2 + n], ACT.Copy).then_inc(pbT_ready, 1)
                    act.wait_ge(attT_filled, a * T + t + 1)
                    act.activation(attT[:, :, :].rearrange("p c i -> p (c i)"), bank[5], ACT.Copy).then_inc(attT_ready, 1)

        @block.vector
        def _(dve):
            dve.wait_ge(init, INIT)
            with dve.Fori(0, B) as a:
                s = Steps(dve, dve_front, a, FRONT)
                dve.wait_ge(x_loaded, a * 16 + 16)
                layernorm(dve, s, X, HS, stats, mv, ve, sd, rs, T, var_ready, sd_ready, hs_ready, a, carrier[:, :])
                s.end()
                for i in range(QK + 1):
                    if i < QK:
                        dve.wait_ge(qk_ready, a * QK + i + 1)
                        if i >= 2:
                            dve.wait_ge(ex_ready, a * QK + i - 1)
                        dve.tensor_scalar(low[:, i % 2, :], qk[:, i, :], 0.0, None, ALU.min).then_inc(low_ready, 1)
                    if i >= 1:
                        dve.wait_ge(ex_ready, a * QK + i)
                        dve.scalar_tensor_tensor(sqk[:, i - 1, :], qk[:, i - 1, :], 0.0, ex[:, (i - 1) % 2, :],
                                                 ALU.max, ALU.add).then_inc(sqk_ready, 1)
                for n in range(NSEG - 1):
                    dve.wait_ge(u_filled, a * (NSEG - 1) + n + 1)
                    if n >= 1:
                        dve.wait_ge(mem_ready, a * (NSEG - 1) + n)
                    dve.tensor_tensor(MEM[:, n + 1, :, :], MEM[:, n, :, :],
                                      bank[2 + n % 2][:, 0:PAIRS * VW].rearrange("p (h v) -> p h v", v=VW),
                                      ALU.add).then_inc(mem_ready, 1)
                s = Steps(dve, dve_tile, a, PER_TILE * T)
                for t in range(T):
                    dve.wait_ge(s_filled, a * T + t + 1)
                    if t >= 1:
                        dve.wait_ge(pbT_filled, a * T + t)
                    for n in range(2):
                        sc = bank[6 + n][:, 0:PAIRS * LSEG].rearrange("p (h j) -> p h j", j=LSEG)
                        last = dve.tensor_reduce(mx[:, n * PAIRS:(n + 1) * PAIRS], sc, AX.X, ALU.max)
                    s.own(last)
                    for n in range(2):
                        sc = bank[6 + n][:, 0:PAIRS * LSEG].rearrange("p (h j) -> p h j", j=LSEG)
                        last = dve.tensor_tensor(SS[:, t % 2, n * PAIRS:(n + 1) * PAIRS, :], sc,
                                                 mx[:, n * PAIRS:(n + 1) * PAIRS].unsqueeze(2).to_broadcast([P, PAIRS, LSEG]),
                                                 ALU.subtract)
                    last.then_inc(s_ready, 1)
                    dve.wait_ge(e_ready, a * T + t + 1)
                    s.own(dve.tensor_reduce(rr[:, :], SS[:, t % 2, :, :], AX.X, ALU.add))
                    s.own(dve.reciprocal(rr[:, :], rr[:, :]))
                    for n in range(2):
                        half = slice(n * LSEG, (n + 1) * LSEG)
                        last = dve.tensor_tensor(PB[half, :, half], SS[half, t % 2, :, :],
                                                 rr[half, :].unsqueeze(2).to_broadcast([LSEG, H, LSEG]), ALU.mult)
                    last.then_inc(pb_ready, 1)
                    dve.wait_ge(am_filled, a * T + t + 1)
                    by_head = AM[:, :].rearrange("p (c two v) -> p two c v", two=2, v=DK)
                    for n in range(2):
                        am = bank[n][:, 0:PAIRS * VW].rearrange("p (c v) -> p c v", v=VW)
                        last = dve.reciprocal(rz[:, n, :], am[:, :, DK])
                    s.own(last)
                    for n in range(2):
                        am = bank[n][:, 0:PAIRS * VW].rearrange("p (c v) -> p c v", v=VW)
                        last = dve.tensor_tensor(by_head[:, n, :, :], am[:, :, 0:DK],
                                                 rz[:, n, :].unsqueeze(2).to_broadcast([P, PAIRS, DK]), ALU.mult)
                    s.own(last)
                    s.own(dve.tensor_tensor(AM[:, :], AM[:, :], w["gate"][:, :], ALU.mult))
                    dve.wait_ge(l_filled, a * T + t + 1)
                    s.own(dve.tensor_tensor(AL[:, :], bank[4], w["omg"][:, :], ALU.mult))
                    if t >= 1:
                        dve.wait_ge(attT_filled, a * T + t)
                    dve.tensor_tensor(AT[:, :], AM[:, :], AL[:, :], ALU.add).then_inc(at_ready, 1)
                    if t == 0:
                        dve.wait_ge(y_stored, a * 16 + 16)
                    dve.wait_ge(o_filled, a * T + t + 1)
                    s.own(dve.tensor_copy(Y[:, t, :], bank[5][:, 0:D]))
                    s.own(dve.memset(rz[:, :, 0:1], 0.0))
                    dve.tensor_tensor(Y[:, t, :], Y[:, t, :], X[:, t, :], ALU.add).then_inc(y_ready, 1)
                s.end()

        @block.tensor
        def _(pe):
            def carry(free):
                pe.matmul(free[:, 510:512], ident_b[:, :], ident_b[:, 0:2], start=True, stop=True)

            pe.wait_ge(init, INIT)
            with pe.Fori(0, B) as a:
                pe.wait_ge(hs_ready, a + 1)
                for c in range(DC):
                    for t in range(T):
                        last = pe.transpose(bank[c][:, t * P:(t + 1) * P], HS[:, t, c * P:(c + 1) * P], ident[:, :])
                    last.then_inc(hsT_filled, 1)
                pe.wait_ge(hsT_ready, (a + 1) * DC)
                for i in range(QK):
                    weight = w["la_q"] if i < PAIRS else w["la_k"]
                    pair = i % PAIRS
                    if i >= 4:
                        pe.wait_ge(qk_ready, a * QK + i - 3)
                    for c in range(DC):
                        last = pe.matmul(RING[i % 4], weight[:, c, pair * P:(pair + 1) * P], hsT[:, c, :],
                                         start=(c == 0), stop=(c == DC - 1))
                    last.then_inc(qk_filled, 1)
                for t in range(T):
                    pe.wait_ge(qk_ready, a * QK + QK - 4 + t + 1)
                    for c in range(DC):
                        last = pe.matmul(RING[t], hsT[:, c, t * P:(t + 1) * P], w["la_v"][:, c, :],
                                         start=(c == 0), stop=(c == DC - 1))
                    last.then_inc(v_filled, 1)
                pe.wait_ge(sqk_ready, (a + 1) * QK)
                for t in range(T):
                    pe.wait_ge(v_ready, a * T + t + 1)
                    for pair in range(PAIRS):
                        last = pe.transpose(RING[t][:, pair * P:(pair + 1) * P],
                                            sqk[:, PAIRS + pair, t * P:(t + 1) * P], ident[:, :])
                    last.then_inc(sk_filled, 1)
                pe.wait_ge(sk_ready, (a + 1) * T)
                carry(bank[2])
                for n in range(NSEG - 1):
                    t, rows = n // 2, slice((n % 2) * LSEG, (n % 2 + 1) * LSEG)
                    if n >= 2:
                        pe.wait_ge(mem_ready, a * (NSEG - 1) + n - 1)
                        carry(bank[2 + n % 2])
                    for h in range(H):
                        pair, one = h // 2, h % 2
                        last = pe.matmul(bank[2 + n % 2][one * DK:(one + 1) * DK, pair * VW:(pair + 1) * VW],
                                         sk[rows, t, h * DK:(h + 1) * DK], V[rows, t, h, :], start=True, stop=True)
                    last.then_inc(u_filled, 1)
                pe.wait_ge(mem_ready, (a + 1) * (NSEG - 1))
                carry(bank[6])
                for t in range(T):
                    if t >= 1:
                        pe.wait_ge(s_ready, a * T + t)
                        carry(bank[6])
                    for h in range(H):
                        pair, one = h // 2, h % 2
                        part = slice(one * DK, (one + 1) * DK)
                        for n in range(2):
                            seg = slice((2 * t + n) * LSEG, (2 * t + n + 1) * LSEG)
                            last = pe.matmul(bank[6 + one][n * LSEG:(n + 1) * LSEG, pair * LSEG:(pair + 1) * LSEG],
                                             qk[part, pair, seg], qk[part, PAIRS + pair, seg], start=True, stop=True)
                    last.then_inc(s_filled, 1)
                    for h in range(H):
                        pair, one = h // 2, h % 2
                        part = slice(one * DK, (one + 1) * DK)
                        for n in range(2):
                            seg = slice((2 * t + n) * LSEG, (2 * t + n + 1) * LSEG)
                            last = pe.matmul(bank[one][n * LSEG:(n + 1) * LSEG, pair * VW:(pair + 1) * VW],
                                             sqk[part, pair, seg], MEM[part, 2 * t + n, pair, :], start=True, stop=True)
                    last.then_inc(am_filled, 1)
                    pe.wait_ge(pb_ready, a * T + t + 1)
                    for h in range(H):
                        last = pe.transpose(bank[2 + h // PAIRS][:, (h % PAIRS) * P:(h % PAIRS + 1) * P],
                                            PB[:, h, :], ident[:, :])
                    last.then_inc(pbT_filled, 1)
                    pe.wait_ge(pbT_ready, (a * T + t + 1) * 2)
                    for h in range(H):
                        last = pe.matmul(bank[4][:, h * DK:(h + 1) * DK], PBT[:, (h % 2) * PAIRS + h // 2, :],
                                         V[:, t, h, 0:DK], start=True, stop=True)
                    last.then_inc(l_filled, 1)
                    pe.wait_ge(at_ready, a * T + t + 1)
                    for c in range(KC):
                        last = pe.transpose(bank[5][:, c * P:(c + 1) * P], AT[:, c * P:(c + 1) * P], ident[:, :])
                    last.then_inc(attT_filled, 1)
                    pe.wait_ge(attT_ready, a * T + t + 1)
                    for c in range(KC):
                        last = pe.matmul(bank[5][:, 0:D], attT[:, c, :], w["la_o"][:, c, :],
                                         start=(c == 0), stop=(c == KC - 1))
                    last.then_inc(o_filled, 1)
                    pe.wait_ge(y_ready, a * T + t + 1)


def macaron(nc, x, Wq, Wk, Wv, betas, Wo, q_w, q_b, k_w, k_b, v_w, v_b, o_w, o_b,
            router_w, router_b, w1, b1, w2, b2, out):
    B, S, D = x.shape
    E, _, F = w1.shape
    H = 16
    LAT = k_w.shape[1]
    KPH, HD = LAT // H, D // H
    AH, ADK = betas.shape[1], betas.shape[3]
    LSEG = 64
    DC, FC = D // P, F // P
    assert LAT == P and AH * ADK == Wq.shape[1]

    with ExitStack() as ctx:
        def sb(name, shape, dt=F32):
            return ctx.enter_context(nc.sbuf_tensor(name, shape, dt))

        semaphores = {}

        def sem(name):
            if name not in semaphores:
                semaphores[name] = ctx.enter_context(nc.semaphore(name))
            return semaphores[name]

        bank = [ctx.enter_context(nc.psum_tensor(f"bank{i}", [P, 512], F32))[:, :] for i in range(8)]
        ident = sb("ident", [P, P])
        tri = sb("tri", [P, E, E])
        w = {
            "q_w": sb("q_w", [P, DC, LAT]), "k_w": sb("k_w", [P, DC, LAT]), "v_w": sb("v_w", [P, DC, LAT]),
            "q_bs": sb("q_bs", [P, 1]), "k_b": sb("k_b", [P, 1]), "v_b": sb("v_b", [P, LAT]),
            "o_w": sb("o_w", [P, D]), "o_b": sb("o_b", [P, DC]),
            "router_w": sb("router_w", [P, DC, E]), "router_b": sb("router_b", [P, E]),
            "w1": sb("w1", [P, E, DC, F]), "b1": sb("b1", [P, E, FC]),
            "w2": sb("w2", [P, E, FC, D]), "b2": sb("b2", [P, D]),
            "sel": sb("sel", [P, E, P]), "ident_b": sb("ident_b", [P, P], BF16),
        }
        x1 = nc.dram_tensor("x1", (B, S, D), F32, kind="Internal").ap()
        x2 = nc.dram_tensor("x2", (B, S, D), F32, kind="Internal").ap()
        scratch = [nc.dram_tensor(n, s, BF16, kind="Internal").ap() for n, s in
                   (("q_parts", (3, P, S)), ("k_parts", (3, P, S)), ("m_parts", (4, 3 * H // 4, S)))]

        loaded, q_full_loaded, made, zeroed, diag, gate_step = (
            sem("loaded"), sem("q_full_loaded"), sem("made"), sem("zeroed"), sem("diag"), sem("gate_step"))

        def load_and_make():
            with ExitStack() as inner:
                q_full = inner.enter_context(nc.sbuf_tensor("q_full", [P, DC, D], F32))
                ones = inner.enter_context(nc.sbuf_tensor("ones", [P, E, E], F32))
                block = inner.enter_context(nc.Block())

                plain = [
                    (w["k_w"][:, :, :], k_w.rearrange("(c p) n -> p c n", p=P)),
                    (w["v_w"][:, :, :], v_w.rearrange("(c p) n -> p c n", p=P)),
                    (w["k_b"][:, :], k_b.rearrange("(p one) -> p one", one=1)),
                    (w["v_b"][:, :], v_b.partition_broadcast(P)),
                    (w["o_w"][:, :], o_w[0:LAT, :]),
                    (w["o_b"][:, :], o_b),
                    (w["router_w"][:, :, :], router_w.rearrange("(c p) n -> p c n", p=P)),
                    (w["router_b"][:, :], router_b.partition_broadcast(P)),
                    (w["w1"][:, :, :, :], w1.rearrange("e (c p) f -> p e c f", p=P)),
                    (w["b1"][:, :, :], b1),
                    (w["w2"][:, :, :, :], w2.rearrange("e (c p) d -> p e c d", p=P)),
                ]
                QB = 16 * (len(plain) + H + 1)

                @block.sync
                def _(sp):
                    sp.dma_start(q_full[:, :, :], q_w.rearrange("(c p) n -> p c n", p=P)).then_inc(q_full_loaded, 16)
                    for h in range(H):
                        sp.dma_start(w["q_bs"][h * KPH:(h + 1) * KPH, :],
                                     q_b[h * HD:h * HD + KPH].rearrange("(p one) -> p one", one=1)).then_inc(loaded, 16)
                    for to, source in plain:
                        sp.dma_start(to, source).then_inc(loaded, 16)
                    sp.wait_ge(zeroed, 3)
                    sp.dma_start(w["b2"][0:E, :], b2).then_inc(loaded, 16)

                @block.gpsimd
                def _(pool):
                    pool.memset(w["b2"][:, :], 0.0).then_inc(zeroed, 1)
                    pool.memset(ident[:, :], 0.0).then_inc(zeroed, 1)
                    pool.memset(ones[:, :, :], 1.0).then_inc(zeroed, 1)
                    pool.wait_ge(zeroed, 3)
                    pool.affine_select(out=ident[:, :], in_=ident[:, :], compare_op=ALU.not_equal, fill=1.0,
                                       base=0, pattern=[[-1, P]], channel_multiplier=1).then_inc(diag, 1)
                    pool.affine_select(out=tri[:, :, :], in_=ones[:, :, :], compare_op=ALU.is_gt, fill=0.0,
                                       base=0, pattern=[[1, E], [-1, E]], channel_multiplier=0).then_inc(diag, 1)

                @block.vector
                def _(dve):
                    dve.wait_ge(diag, 2)
                    dve.tensor_copy(w["ident_b"][:, :], ident[:, :]).then_inc(made, 1)
                    for e in range(E):
                        dve.tensor_copy(w["sel"][:, e, :], ident[:, e:e + 1].to_broadcast([P, P])).then_inc(made, 1)
                    dve.wait_ge(q_full_loaded, 16)
                    for c in range(DC):
                        dve.tensor_copy(w["q_w"][:, c, :].rearrange("p (h k) -> p h k", k=KPH),
                                        q_full[:, c, :].rearrange("p (h x) -> p h x", x=HD)[:, :, 0:KPH]).then_inc(made, 1)
                    dve.wait_ge(loaded, QB)
                    dve.tensor_scalar(w["q_bs"][:, :], w["q_bs"][:, :], 1.0 / float(np.sqrt(KPH)), None,
                                      ALU.mult).then_inc(made, 1)
                    dve.wait_ge(made, 1 + E + DC + 1)

        dims = (B, S, D, H, HD, KPH, E, F)
        load_and_make()
        ffn_pass(nc, sem, "f1", 0, x, x1, bank, ident, tri, w, scratch, dims)

        with ExitStack() as inner:
            HK = AH * ADK
            KC = HK // P
            la = {"la_q": [P, DC, HK], "la_k": [P, DC, HK], "la_v": [P, DC, HK], "la_o": [P, KC, D],
                  "gate": [P, HK], "omg": [P, HK]}
            la = {k: inner.enter_context(nc.sbuf_tensor(k, s, F32)) for k, s in la.items()}
            la_loaded = sem("la_loaded")
            exp_ready = sem("exp_ready")
            with nc.Block() as block:
                @block.sync
                def _(sp):
                    for k, source in (("la_q", Wq), ("la_k", Wk), ("la_v", Wv), ("la_o", Wo)):
                        sp.dma_start(la[k][:, :, :], source.rearrange("(c p) n -> p c n", p=P)).then_inc(la_loaded, 16)
                    sp.dma_start(la["gate"][:, :], betas.rearrange("a h b v -> (a h b v)").partition_broadcast(P)) \
                      .then_inc(la_loaded, 16)

                @block.scalar
                def _(act):
                    act.wait_ge(la_loaded, 80)
                    act.activation(la["gate"][:, :], la["gate"][:, :], ACT.Exp, scale=-1.0).then_inc(exp_ready, 1)

                @block.vector
                def _(dve):
                    dve.wait_ge(exp_ready, 1)
                    dve.tensor_scalar(la["gate"][:, :], la["gate"][:, :], 1.0, None, ALU.add).then_inc(gate_step, 1)
                    dve.wait_ge(gate_step, 1)
                    dve.reciprocal(la["gate"][:, :], la["gate"][:, :]).then_inc(gate_step, 1)
                    dve.wait_ge(gate_step, 2)
                    dve.tensor_scalar(la["omg"][:, :], la["gate"][:, :], -1.0, 1.0, ALU.mult, ALU.add).then_inc(gate_step, 1)
                    dve.wait_ge(gate_step, 3)
            attention_pass(nc, sem, "la", x1, x2, bank, ident, w["ident_b"], la, B, S, D, AH, ADK, LSEG)

        ffn_pass(nc, sem, "f2", 1, x2, out, bank, ident, tri, w, scratch, dims)


_INS = ["L0_attn_x", "L0_attn_Wq", "L0_attn_Wk", "L0_attn_Wv", "L0_attn_betas", "L0_attn_Wo",
        "L0_ffn_q_w", "L0_ffn_q_b", "L0_ffn_k_w", "L0_ffn_k_b", "L0_ffn_v_w", "L0_ffn_v_b",
        "L0_ffn_o_w", "L0_ffn_o_b", "L0_ffn_router_w", "L0_ffn_router_b",
        "L0_ffn_w1", "L0_ffn_b1", "L0_ffn_w2", "L0_ffn_b2"]


def kernel(**inputs):
    import concourse.bacc as bacc
    from concourse.bass_utils import run_bass_kernel_spmd

    nc = bacc.Bacc("TRN2", target_bir_lowering=False, num_devices=1)
    arrays, args = {}, []
    for name in _INS:
        a = np.asarray(inputs[name])
        if name == "L0_ffn_o_b":
            a = a.reshape(-1, P).transpose(1, 0)
        if name == "L0_ffn_b1":
            a = a.reshape(a.shape[0], -1, P).transpose(2, 0, 1)
        a = np.ascontiguousarray(a)
        arrays[f"in_{name}"] = a
        args.append(nc.dram_tensor(f"in_{name}", a.shape, mybir.dt.from_np(a.dtype), kind="ExternalInput").ap())
    shape = inputs["L0_attn_x"].shape
    out = nc.dram_tensor("out", shape, F32, kind="ExternalOutput").ap()
    macaron(nc, *args, out)
    result = run_bass_kernel_spmd(nc, [arrays], core_ids=[0])
    return result.results[0]["out"]
```

```python
from contextlib import ExitStack

import numpy as np

import concourse.bass as bass
from concourse import mybir
from concourse.bass import ds

ALU = mybir.AluOpType
ACT = mybir.ActivationFunctionType
F32 = mybir.dt.float32
BF16 = mybir.dt.bfloat16
I32 = mybir.dt.int32
AX = mybir.AxisListType

P = 128
EPS = 1e-5


def wait(eng, sem, value):
    if not (isinstance(value, int) and value <= 0):
        eng.wait_ge(sem, value)


class Steps:

    def __init__(self, eng, sem, unit, per_unit):
        self.eng, self.sem, self.base, self.per_unit, self.n = eng, sem, unit * per_unit, per_unit, 0

    def own(self, instruction):
        instruction.then_inc(self.sem, 1)
        self.n += 1
        self.eng.wait_ge(self.sem, self.base + self.n)

    def end(self):
        assert self.n == self.per_unit, (self.n, self.per_unit)


LN_STEPS = 7


def ln_variance(dve, s, X, stats, mv, ve, T, var_ready, carrier):
    for t in range(T):
        last = dve.bn_stats(stats[:, t, :], X[:, t, :])
    s.own(last)
    dve.memset(carrier, 0.0)
    for t in range(T):
        last = dve.bn_aggr(mv[:, t, :], stats[:, t, :])
    s.own(last)
    dve.tensor_scalar(ve[:, :], mv[:, :, 1], EPS, None, ALU.add).then_inc(var_ready, 1)


def ln_normalise(dve, s, X, HS, mv, ve, sd, rs, T, sd_ready, hs_ready, unit):
    dve.wait_ge(sd_ready, unit + 1)
    s.own(dve.reciprocal(rs[:, :], sd[:, :]))
    s.own(dve.tensor_tensor(sd[:, :], rs[:, :], rs[:, :], ALU.mult))
    s.own(dve.tensor_tensor(sd[:, :], sd[:, :], ve[:, :], ALU.mult))
    s.own(dve.tensor_scalar(sd[:, :], sd[:, :], -0.5, 1.5, ALU.mult, ALU.add))
    s.own(dve.tensor_tensor(rs[:, :], rs[:, :], sd[:, :], ALU.mult))
    for t in range(T):
        last = dve.tensor_scalar(HS[:, t, :], X[:, t, :], mv[:, t, 0:1], rs[:, t:t + 1],
                                 ALU.subtract, ALU.mult)
    last.then_inc(hs_ready, 1)


def region_rows(tokens):
    return tokens + P


def attend_and_route(nc, new_sem, tag, nth, x_in, xr_out, xs, bank, ident, tri, w, scratch, routing, dims):
    B, S, D, H, HD, KPH, E, F = dims
    T, DC = S // P, D // P
    QUARTERS = 4
    HQ = H // QUARTERS
    PARTS = 3
    TERMS = [(0, 0), (1, 0), (2, 0), (0, 1), (1, 1), (0, 2)]
    K_MAX = 96
    K_EXP = K_MAX + PARTS
    PV_W = 32
    SC = H * T
    PER_Q = SC // QUARTERS
    GROUPS = SC // HQ
    SCORE_SCALE = 1.0 / float(np.sqrt(KPH))
    OUT_SCALE = 0.5 * 0.3
    START, END = nth * B, (nth + 1) * B
    A_FRONT, A_SCM, A_POST = LN_STEPS + 3, 3 * QUARTERS, T + 22
    PER_UNIT = SC + QUARTERS
    ROWS = 2 * T * 16
    HALF = 2 * len(TERMS) * 16
    q_scr, k_scr, m_scr = scratch
    ROW, CW, start_row = routing["ROW"], routing["CW"], routing["start_row"]

    def max_slot(q):
        return (q + 1) * PER_Q + min(HQ, SC - (q + 1) * PER_Q) + q

    def score_slot(i):
        return i + sum(1 for q in range(QUARTERS) if i >= (q + 1) * PER_Q + HQ)

    with ExitStack() as ctx:
        def sb(name, shape, dt=F32):
            return ctx.enter_context(nc.sbuf_tensor(f"{tag}_{name}", shape, dt))

        def sem(name):
            return new_sem(f"ffn_{name}")

        X, HS, XR = sb("x", [P, T, D]), sb("hs", [P, T, D]), sb("xr", [P, T, D])
        stats = sb("stats", [P, T, 6])
        mv = sb("mv", [P, T, 2])
        ve, sd, rs = sb("ve", [P, T]), sb("sd", [P, T]), sb("rs", [P, T])
        carrier = sb("carrier", [P, 1])
        hsT = sb("hsT", [P, DC, S])
        qf, kf = sb("qf", [P, S]), sb("kf", [P, S])
        qres, kres = sb("qres", [P, S]), sb("kres", [P, S])
        q3, k3 = sb("q3", [P, PARTS, S], BF16), sb("k3", [P, PARTS, S], BF16)
        QS = [sb(f"QS{i}", [K_EXP, H, S], BF16) for i in range(2)]
        KS = [sb(f"KS{i}", [K_EXP, H, S], BF16) for i in range(2)]
        V = [sb(f"V{i}", [P, T, H, PV_W]) for i in range(2)]
        M = sb("M", [P, T, H])
        mres = sb("mres", [P, T, HQ])
        m3 = sb("m3", [P, T, PARTS, HQ], BF16)
        mT = sb("mT", [PARTS * HQ, S], BF16)
        PT = sb("PT", [P, 8, S])
        PVS = sb("PVS", [P, QUARTERS, S])
        rec = sb("rec", [P, T, H])
        AO = sb("AO", [P, T, H * KPH])
        aoT = sb("aoT", [P, S])
        mlaT = sb("mlaT", [P, DC, S])
        NAT = sb("nat", [P, T, D])
        L = sb("L", [P, T, E])
        pr = sb("pr", [P, T, E])
        small = sb("small", [P, T])
        gt, eq = sb("gt", [P, T, E, E]), sb("eq", [P, T, E, E])
        rank = sb("rank", [P, T, E])
        comb = sb("comb", [P, T, E])
        chosen = sb("chosen", [P, T, E], BF16)
        hot, picked = sb("hot", [P, T, 2, E]), sb("picked", [P, T, 2, E])
        row, rows_f, weights = sb("row", [P, T, E]), sb("rows_f", [P, T, 2]), sb("weights", [P, T, 2])
        rows_i = sb("rows_i", [P, T, 2], I32)
        pad_f, pad_i = sb("pad_f", [P, E]), sb("pad_i", [P, E], I32)
        zero_rows = sb("zero_rows", [P, D])
        zero = sb("zero", [P, 1])
        pool_carrier = sb("pool_carrier", [P, 1])

        x_loaded, xr_ready, xr_stored = sem("x_loaded"), sem("xr_ready"), sem("xr_stored")
        var_ready, sd_ready, hs_ready = sem("var_ready"), sem("sd_ready"), sem("hs_ready")
        hsT_filled, hsT_ready = sem("hsT_filled"), sem("hsT_ready")
        q_filled, k_filled, v_filled = sem("q_filled"), sem("k_filled"), sem("v_filled")
        q_ready, k_ready, v_ready = sem("q_ready"), sem("k_ready"), sem("v_ready")
        q3_ready, k3_ready = sem("q3_ready"), sem("k3_ready")
        split_stored, half_loaded = sem("split_stored"), [sem(f"half_loaded{i}") for i in range(2)]
        scm_filled, scm_drained = sem("scm_filled"), sem("scm_drained")
        m3_ready, mT_filled = sem("m3_ready"), sem("mT_filled")
        m_stored, m_loaded = sem("m_stored"), [sem(f"m_loaded{q}") for q in range(QUARTERS)]
        sce_filled, probs_ready = sem("sce_filled"), sem("probs_ready")
        pv_used, pvs_ready = sem("pv_used"), sem("pvs_ready")
        pvT_filled, ao_ready = sem("pvT_filled"), sem("ao_ready")
        aoT_filled, aoT_ready = sem("aoT_filled"), sem("aoT_ready")
        mla_filled, mlaT_ready = sem("mla_filled"), sem("mlaT_ready")
        nat_filled, nat_ready = sem("nat_filled"), sem("nat_ready")
        router_filled, logits_ready, ex_ready = sem("router_filled"), sem("logits_ready"), sem("ex_ready")
        chosen_ready, prefix_filled, rows_ready, rows_stored = (
            sem("chosen_ready"), sem("prefix_filled"), sem("rows_ready"), sem("rows_stored"))
        pads_ready, pads_stored = sem("pads_ready"), sem("pads_stored")
        dve_front, dve_scm, dve_post, pool_front = sem("dve_front"), sem("dve_scm"), sem("dve_post"), sem("pool_front")
        dve_pads, carried, rows_out = sem("dve_pads"), sem("carried"), sem("rows_out")
        init = sem("init")
        N_INIT = 12
        INIT = N_INIT * (nth + 1)

        SCE, SIDE, PVB, SCM = bank[0:2], bank[2:4], bank[4:6], bank[6:8]

        def run_turns(eng, turn):
            turn(None, None, START, None)
            turn(None, START, START + 1, None)
            turn(START, START + 1, START + 2, None)
            full = B - 3
            with eng.Fori(0, full // 2) as k:
                for odd in range(2):
                    b = k * 2 + (START + 1 + odd)
                    turn(b, b + 1, b + 2, b - 1, (START + 1 + odd) % 2)
            for b in range(START + 1 + full // 2 * 2, END + 1):
                turn(b if b < END else None, b + 1 if b + 1 < END else None,
                     b + 2 if b + 2 < END else None, b - 1)

        def parity(unit, offset, par):
            if par is not None:
                return (par + offset) % 2
            return unit % 2 if unit is not None else None

        block = ctx.enter_context(nc.Block())

        @block.sync
        def _(sp):
            def load(a):
                sp.dma_start(X[:, :, :], x_in[a - START].rearrange("(t p) d -> p t d", p=P)).then_inc(x_loaded, 16)

            def stack_half(a, half, par, free):
                if free is not None:
                    wait(sp, sce_filled, free)
                if half == 0:
                    sp.wait_ge(split_stored, a * 32 + 32)
                heads = slice(half * H // 2, (half + 1) * H // 2)
                for n, (i, j) in enumerate(TERMS):
                    at = slice(n * KPH, (n + 1) * KPH)
                    for to, source in ((QS[par], q_scr[i]), (KS[par], k_scr[j])):
                        sp.dma_start(to[at, heads, :], source.rearrange("(h k) t -> k h t", k=KPH)[:, heads, :]) \
                          .then_inc(half_loaded[half], 16)

            def maxima(a, q, par):
                sp.wait_ge(scm_drained, a * PER_UNIT + max_slot(q) + 1)
                sp.dma_start(m_scr[q], mT[:, :]).then_inc(m_stored, 16)
                sp.wait_ge(m_stored, (a * QUARTERS + q) * 16 + 16)
                sp.dma_start(QS[par][K_MAX:K_EXP, q * HQ:(q + 1) * HQ, :],
                             m_scr[q].rearrange("(c h) t -> c h t", h=HQ)).then_inc(m_loaded[q], 16)

            def turn(e, s, f, p, par=None):
                par_s, par_f = parity(s, 1, par), parity(f, 0, par)
                if f is not None:
                    sp.wait_ge(xr_ready, f + 1)
                    sp.dma_start(xr_out[f - START].rearrange("(t p) d -> p t d", p=P), XR[:, :, :]).then_inc(xr_stored, 16)
                    wait(sp, half_loaded[1], f * HALF)
                    if not isinstance(f, int) or f + 1 < END:
                        load(f + 1)
                    sp.wait_ge(q3_ready, f + 1)
                    sp.dma_start(q_scr.rearrange("c r t -> r c t"), q3[:, :, :]).then_inc(split_stored, 16)
                    sp.wait_ge(k3_ready, f + 1)
                    sp.dma_start(k_scr.rearrange("c r t -> r c t"), k3[:, :, :]).then_inc(split_stored, 16)
                if s is not None:
                    maxima(s, 0, par_s)
                if f is not None:
                    sp.wait_ge(init, INIT)
                    stack_half(f, 0, par_f, e * SC + SC // 2 if e is not None else None)
                if s is not None:
                    for q in range(1, QUARTERS):
                        maxima(s, q, par_s)
                if f is not None:
                    stack_half(f, 1, par_f, (e + 1) * SC if e is not None else None)

            load(START)
            run_turns(sp, turn)
            sp.wait_ge(xr_stored, 16 * END)
            sp.wait_ge(m_stored, 16 * QUARTERS * END)
            sp.wait_ge(split_stored, 32 * END)
            sp.wait_ge(rows_stored, ROWS * END)
            sp.wait_ge(pads_stored, 16 * E * (nth + 1))

        @block.gpsimd
        def _(pool):
            for i in range(2):
                pool.memset(QS[i][0:K_MAX, :, :], 0.0).then_inc(init, 1)
                pool.memset(KS[i][0:K_MAX, :, :], 0.0).then_inc(init, 1)
                pool.memset(V[i][:, :, :, :], 0.0).then_inc(init, 1)
            pool.memset(zero[:, :], 0.0).then_inc(init, 1)
            pool.memset(zero_rows[:, :], 0.0).then_inc(init, 1)
            for i in range(2):
                pool.wait_ge(init, INIT - 4 + 2 * i)
                pool.memset(KS[i][K_MAX:K_EXP, :, :], 1.0).then_inc(init, 1)
                pool.wait_ge(init, INIT - 3 + 2 * i)
                pool.memset(V[i][:, :, :, KPH:KPH + 1], 1.0).then_inc(init, 1)
            if nth == 0:
                pool.memset(pool_carrier[:, :], 0.0).then_inc(carried, 1)
                pool.memset(NAT[:, 0, 0:1], 0.0).then_inc(rows_out, 1)
            nothing = zero[:, :].to_broadcast([P, S])

            def split_k(a):
                s = Steps(pool, pool_front, a, 3)
                pool.wait_ge(k_ready, a + 1)
                wait(pool, split_stored, a * 32)
                s.own(pool.tensor_tensor(k3[:, 0, :], kf[:, :], nothing, ALU.add))
                s.own(pool.tensor_tensor(kres[:, :], kf[:, :], k3[:, 0, :], ALU.subtract))
                s.own(pool.tensor_tensor(k3[:, 1, :], kres[:, :], nothing, ALU.add))
                pool.tensor_tensor(k3[:, 2, :], kres[:, :], k3[:, 1, :], ALU.subtract).then_inc(k3_ready, 1)
                s.end()

            def send_rows(a):
                pool.wait_ge(nat_ready, (a + 1) * 2)
                pool.wait_ge(rows_ready, a + 1)
                pool.wait_ge(rows_out, a + 1)
                pool.tensor_tensor(pool_carrier[:, :], zero[:, :], zero[:, :], ALU.add).then_inc(carried, 1)
                for t in range(T):
                    for n in range(2):
                        pool.indirect_dma_start(
                            out=xs, out_offset=bass.IndirectOffsetOnAxis(ap=rows_i[:, t, n:n + 1], axis=0),
                            in_=NAT[:, t, :], in_offset=None).then_inc(rows_stored, 16)
                pool.wait_ge(carried, a + 2)
                pool.wait_ge(rows_stored, (a + 1) * ROWS)
                pool.tensor_tensor(pool_carrier[:, :], zero[:, :], zero[:, :], ALU.add).then_inc(rows_out, 1)

            def turn(e, s, f, p, par=None):
                if f is not None:
                    split_k(f)
                if p is not None:
                    send_rows(p)

            pool.wait_ge(init, INIT)
            run_turns(pool, turn)
            pool.wait_ge(pads_ready, nth + 1)
            for e in range(E):
                pool.indirect_dma_start(
                    out=xs, out_offset=bass.IndirectOffsetOnAxis(ap=pad_i[:, e:e + 1], axis=0),
                    in_=zero_rows[:, :], in_offset=None).then_inc(pads_stored, 16)

        @block.scalar
        def _(act):
            def root(a):
                act.wait_ge(var_ready, a + 1)
                act.activation(sd[:, :], ve[:, :], ACT.Sqrt).then_inc(sd_ready, 1)

            def evacuate_hsT(a):
                for c in range(DC):
                    act.wait_ge(hsT_filled, a * DC + c + 1)
                    act.activation(hsT[:, c, :], SIDE[c], ACT.Copy).then_inc(hsT_ready, 1)

            def evacuate_qk(a):
                wait(act, q3_ready, a)
                act.wait_ge(q_filled, a + 1)
                act.activation(qf[:, :], SIDE[0][:, :], ACT.Identity, bias=w["q_bs"][:, 0:1],
                               scale=SCORE_SCALE).then_inc(q_ready, 1)
                wait(act, k3_ready, a)
                act.wait_ge(k_filled, a + 1)
                act.activation(kf[:, :], SIDE[1][:, :], ACT.Identity, bias=w["k_b"][:, 0:1]).then_inc(k_ready, 1)

            def evacuate_aoT(a):
                act.wait_ge(aoT_filled, a + 1)
                act.activation(aoT[:, :], SIDE[0][:, :], ACT.Copy).then_inc(aoT_ready, 1)

            def evacuate_mla(a):
                for c in range(DC):
                    act.wait_ge(mla_filled, a * DC + c + 1)
                    act.activation(mlaT[:, c, :], SIDE[1 - c][:, :], ACT.Identity,
                                   bias=w["o_b"][:, c:c + 1]).then_inc(mlaT_ready, 1)

            def router_exp(a):
                act.wait_ge(logits_ready, a + 1)
                act.activation(L[:, :, :], L[:, :, :], ACT.Exp).then_inc(ex_ready, 1)

            FRONT = {0: root, 2: evacuate_hsT, 3: evacuate_qk}
            POST = {7: evacuate_aoT, 8: evacuate_mla, 11: router_exp}

            def turn(e, s, f, p, par=None):
                for g in range(GROUPS):
                    if e is not None:
                        for i in range(g * HQ, (g + 1) * HQ):
                            act.wait_ge(sce_filled, e * SC + i + 1)
                            wait(act, pv_used, e * SC + i - 7)
                            act.activation(PT[:, i % 8, :], SCE[i % 2][:, :], ACT.Exp).then_inc(probs_ready, 1)
                    if f is not None and g in FRONT:
                        FRONT[g](f)
                    if p is not None and g in POST:
                        POST[g](p)

            act.wait_ge(init, INIT)
            run_turns(act, turn)

        @block.vector
        def _(dve):
            def evacuate_v(a, par):
                wait(dve, pv_used, (a - 1) * SC)
                dve.wait_ge(v_filled, a + 1)
                for t in range(T):
                    last = dve.tensor_tensor(V[par][:, t, :, 0:KPH],
                                             SIDE[1][:, t * P:(t + 1) * P].rearrange("p (h k) -> p h k", k=KPH),
                                             w["v_b"][:, :].rearrange("p (h k) -> p h k", k=KPH), ALU.add)
                last.then_inc(v_ready, 1)

            def variance(a, s):
                dve.wait_ge(x_loaded, a * 16 + 16)
                ln_variance(dve, s, X, stats, mv, ve, T, var_ready, carrier[:, :])

            def normalise(a, s):
                ln_normalise(dve, s, X, HS, mv, ve, sd, rs, T, sd_ready, hs_ready, a)
                wait(dve, xr_stored, a * 16)
                dve.wait_ge(hs_ready, a + 1)
                dve.scalar_tensor_tensor(XR[:, :, :], HS[:, :, :], 0.5, X[:, :, :],
                                         ALU.mult, ALU.add).then_inc(xr_ready, 1)

            def split_q(a, s):
                dve.wait_ge(q_ready, a + 1)
                wait(dve, split_stored, a * 32)
                s.own(dve.tensor_copy(q3[:, 0, :], qf[:, :]))
                s.own(dve.tensor_tensor(qres[:, :], qf[:, :], q3[:, 0, :], ALU.subtract))
                s.own(dve.tensor_copy(q3[:, 1, :], qres[:, :]))
                dve.tensor_tensor(q3[:, 2, :], qres[:, :], q3[:, 1, :], ALU.subtract).then_inc(q3_ready, 1)

            def maximum(a, i):
                n = score_slot(i)
                dve.wait_ge(scm_filled, a * SC + i + 1)
                h, t = i // T, i % T
                dve.tensor_reduce(M[:, t, h:h + 1], SCM[n % 2][:, :], AX.X, ALU.max).then_inc(scm_drained, 1)

            def split_maxima(a, q, s):
                mq = M[:, :, q * HQ:(q + 1) * HQ]
                dve.wait_ge(scm_drained, a * PER_UNIT + score_slot((q + 1) * PER_Q - 1) + 1)
                wait(dve, mT_filled, a * QUARTERS + q)
                s.own(dve.tensor_scalar(m3[:, :, 0, :], mq, -1.0, None, ALU.mult))
                s.own(dve.scalar_tensor_tensor(mres[:, :, :], mq, -1.0, m3[:, :, 0, :], ALU.mult, ALU.subtract))
                s.own(dve.tensor_copy(m3[:, :, 1, :], mres[:, :, :]))
                dve.tensor_tensor(m3[:, :, 2, :], mres[:, :, :], m3[:, :, 1, :], ALU.subtract).then_inc(m3_ready, 1)

            def evacuate_mT(a, q):
                dve.wait_ge(mT_filled, a * QUARTERS + q + 1)
                wait(dve, m_stored, (a * QUARTERS + q) * 16)
                dve.tensor_copy(mT[:, :], SCM[max_slot(q) % 2].bitcast(BF16)[0:PARTS * HQ, 0:S]).then_inc(scm_drained, 1)

            def pv_out(a, q):
                dve.wait_ge(pv_used, a * SC + (q + 1) * PER_Q)
                dve.tensor_copy(PVS[:, q, :], PVB[q % 2][:, :]).then_inc(pvs_ready, 1)

            def divide(ts):
                def piece(a, s):
                    for t in ts:
                        dve.wait_ge(pvT_filled, a * T + t + 1)
                        out = SIDE[t % 2][:, :].rearrange("p (h c) -> p h c", c=PV_W)
                        s.own(dve.reciprocal(rec[:, t, :], out[:, :, KPH]))
                        dve.tensor_tensor(AO[:, t, :].rearrange("p (h k) -> p h k", k=KPH), out[:, :, 0:KPH],
                                          rec[:, t, :].unsqueeze(2).to_broadcast([P, H, KPH]),
                                          ALU.mult).then_inc(ao_ready, 1)
                return piece

            def natural(a, s):
                dve.wait_ge(rows_out, a + 1)
                for n in range(2):
                    dve.wait_ge(nat_filled, a * 2 + n + 1)
                    dve.tensor_tensor(NAT[:, 2 * n:2 * n + 2, :], SIDE[1 - n][:, :].rearrange("p (t d) -> p t d", d=D),
                                      w["o_b_row"][:, :].unsqueeze(1).to_broadcast([P, 2, D]),
                                      ALU.add).then_inc(nat_ready, 1)

            per_token = small[:, :].unsqueeze(2).to_broadcast([P, T, E])

            def logits(a, s):
                dve.wait_ge(router_filled, a + 1)
                s.own(dve.tensor_tensor(L[:, :, :], SIDE[1][:, 0:T * E].rearrange("p (t e) -> p t e", e=E),
                                        w["router_b"][:, :].unsqueeze(1).to_broadcast([P, T, E]), ALU.add))
                s.own(dve.tensor_reduce(small[:, :], L[:, :, :], AX.X, ALU.max))
                dve.tensor_tensor(L[:, :, :], L[:, :, :], per_token, ALU.subtract).then_inc(logits_ready, 1)

            def choose(a, s):
                dve.wait_ge(ex_ready, a + 1)
                s.own(dve.tensor_reduce(small[:, :], L[:, :, :], AX.X, ALU.add))
                s.own(dve.reciprocal(small[:, :], small[:, :]))
                s.own(dve.tensor_tensor(pr[:, :, :], L[:, :, :], per_token, ALU.mult))
                other = pr[:, :, :].unsqueeze(2).to_broadcast([P, T, E, E])
                this = pr[:, :, :].unsqueeze(3).to_broadcast([P, T, E, E])
                dve.tensor_tensor(gt[:, :, :, :], other, this, ALU.is_gt)
                s.own(dve.tensor_tensor(eq[:, :, :, :], other, this, ALU.is_equal))
                s.own(dve.tensor_tensor(eq[:, :, :, :], eq[:, :, :, :],
                                        tri[:, :, :].unsqueeze(1).to_broadcast([P, T, E, E]), ALU.mult))
                s.own(dve.tensor_tensor(gt[:, :, :, :], gt[:, :, :, :], eq[:, :, :, :], ALU.add))
                s.own(dve.tensor_reduce(rank[:, :, :], gt[:, :, :, :], AX.X, ALU.add))
                dve.tensor_scalar(chosen[:, :, :], rank[:, :, :], 1.5, None, ALU.is_lt).then_inc(chosen_ready, 1)
                for n in range(2):
                    dve.tensor_scalar(hot[:, :, n, :], rank[:, :, :], float(n), None, ALU.is_equal)
                s.own(dve.scalar_tensor_tensor(comb[:, :, :], rank[:, :, :], 1.5, pr[:, :, :], ALU.is_lt, ALU.mult))
                s.own(dve.tensor_reduce(small[:, :], comb[:, :, :], AX.X, ALU.add))
                s.own(dve.tensor_scalar(small[:, :], small[:, :], 1e-8, None, ALU.add))
                s.own(dve.reciprocal(small[:, :], small[:, :]))
                s.own(dve.tensor_tensor(comb[:, :, :], comb[:, :, :], per_token, ALU.mult))
                s.own(dve.tensor_tensor(picked[:, :, :, :], hot[:, :, :, :],
                                        comb[:, :, :].unsqueeze(2).to_broadcast([P, T, 2, E]), ALU.mult))
                s.own(dve.tensor_reduce(weights[:, :, :], picked[:, :, :, :], AX.X, ALU.add))
                s.own(dve.tensor_scalar(CW[:, ds((a - START) * T, T), :], weights[:, :, :], OUT_SCALE, None, ALU.mult))

            def place(a, s):
                dve.wait_ge(prefix_filled, a + 1)
                prefix = SIDE[0][:, 0:T * E].rearrange("p (t e) -> p t e", e=E)
                s.own(dve.tensor_tensor(row[:, :, :], prefix,
                                        start_row[:, :].unsqueeze(1).to_broadcast([P, T, E]), ALU.add))
                s.own(dve.tensor_tensor(start_row[:, :], start_row[:, :], SIDE[0][:, T * E:(T + 1) * E], ALU.add))
                s.own(dve.tensor_tensor(picked[:, :, :, :], hot[:, :, :, :],
                                        row[:, :, :].unsqueeze(2).to_broadcast([P, T, 2, E]), ALU.mult))
                s.own(dve.tensor_reduce(rows_f[:, :, :], picked[:, :, :, :], AX.X, ALU.add))
                s.own(dve.tensor_scalar(ROW[:, ds((a - START) * T, T), :], rows_f[:, :, :], 0.0, None, ALU.add))
                dve.tensor_copy(rows_i[:, :, :], rows_f[:, :, :]).then_inc(rows_ready, 1)

            FRONT = {0: variance, 1: normalise, 4: split_q}
            POST = {5: divide((0, 1)), 6: divide((2, 3)), 9: natural, 10: logits, 11: choose, 12: place}

            def turn(e, s, f, p, par=None):
                s_scm = Steps(dve, dve_scm, s, A_SCM) if s is not None else None
                s_front = Steps(dve, dve_front, f, A_FRONT) if f is not None else None
                s_post = Steps(dve, dve_post, p, A_POST) if p is not None else None
                if s is not None:
                    evacuate_v(s, parity(s, 1, par))
                for g in range(GROUPS):
                    if s is not None:
                        for i in range(g * HQ, (g + 1) * HQ):
                            maximum(s, i)
                        if g % HQ == 0 and g >= 1:
                            evacuate_mT(s, g // HQ - 1)
                        if g % HQ == HQ - 1:
                            split_maxima(s, g // HQ, s_scm)
                    if e is not None and g % HQ == HQ - 1 and g >= HQ:
                        pv_out(e, g // HQ - 1)
                    if f is not None and g in FRONT:
                        FRONT[g](f, s_front)
                    if p is not None and g in POST:
                        POST[g](p, s_post)
                if s is not None:
                    evacuate_mT(s, QUARTERS - 1)
                if e is not None:
                    pv_out(e, QUARTERS - 1)
                for steps in (s_scm, s_front, s_post):
                    if steps is not None:
                        steps.end()

            dve.wait_ge(init, INIT)
            s = Steps(dve, dve_pads, nth, 2)
            s.own(dve.tensor_copy(start_row[:, :], w["region"][:, :]))
            run_turns(dve, turn)
            s.own(dve.tensor_tensor(pad_f[:, :], start_row[:, :], w["partition"][:, 0:1].to_broadcast([P, E]), ALU.add))
            dve.tensor_copy(pad_i[:, :], pad_f[:, :]).then_inc(pads_ready, 1)
            s.end()

        @block.tensor
        def _(pe):
            def turn_hs(a, par):
                pe.wait_ge(hs_ready, a + 1)
                wait(pe, v_ready, a)
                for c in range(DC):
                    for t in range(T):
                        last = pe.transpose(SIDE[c][:, t * P:(t + 1) * P], HS[:, t, c * P:(c + 1) * P], ident[:, :])
                    last.then_inc(hsT_filled, 1)

            def project_qk(a, par):
                pe.wait_ge(hsT_ready, (a + 1) * DC)
                for filled, to, weight in ((q_filled, SIDE[0], w["q_w"]), (k_filled, SIDE[1], w["k_w"])):
                    for c in range(DC):
                        last = pe.matmul(to[:, :], weight[:, c, :], hsT[:, c, :], start=(c == 0), stop=(c == DC - 1))
                    last.then_inc(filled, 1)

            def release_front(a, par):
                pe.wait_ge(q_ready, a + 1)
                pe.wait_ge(k_ready, a + 1)

            def project_v(a, par):
                for t in range(T):
                    for c in range(DC):
                        last = pe.matmul(SIDE[1][:, t * P:(t + 1) * P], hsT[:, c, t * P:(t + 1) * P],
                                         w["v_w"][:, c, :], start=(c == 0), stop=(c == DC - 1))
                last.then_inc(v_filled, 1)

            def turn_pv(ts):
                def piece(a, par):
                    pe.wait_ge(pvs_ready, (a + 1) * QUARTERS)
                    for t in ts:
                        if t >= 2:
                            pe.wait_ge(ao_ready, a * T + t - 1)
                        for q in range(QUARTERS):
                            last = pe.transpose(SIDE[t % 2][:, q * P:(q + 1) * P], PVS[:, q, t * P:(t + 1) * P],
                                                ident[:, :])
                        last.then_inc(pvT_filled, 1)
                return piece

            def turn_ao(a, par):
                pe.wait_ge(ao_ready, (a + 1) * T)
                for t in range(T):
                    last = pe.transpose(SIDE[0][:, t * P:(t + 1) * P], AO[:, t, :], ident[:, :])
                last.then_inc(aoT_filled, 1)

            def project_out(a, par):
                pe.wait_ge(aoT_ready, a + 1)
                for c in range(DC):
                    pe.matmul(SIDE[1 - c][:, :], w["o_w"][:, c * P:(c + 1) * P], aoT[:, :],
                              start=True, stop=True).then_inc(mla_filled, 1)

            def natural(a, par):
                for t in range(T):
                    if t % 2 == 0:
                        pe.wait_ge(mlaT_ready, a * DC + t // 2 + 1)
                    last = pe.matmul(SIDE[1 - t // 2][:, (t % 2) * D:(t % 2 + 1) * D], aoT[:, t * P:(t + 1) * P],
                                     w["o_w"][:, :], start=True, stop=True)
                    if t % 2:
                        last.then_inc(nat_filled, 1)

            def router(a, par):
                pe.wait_ge(nat_ready, a * 2 + 1)
                for t in range(T):
                    for c in range(DC):
                        last = pe.matmul(SIDE[1][:, t * E:(t + 1) * E], mlaT[:, c, t * P:(t + 1) * P],
                                         w["router_w"][:, c, :], start=(c == 0), stop=(c == DC - 1))
                last.then_inc(router_filled, 1)

            def prefix(a, par):
                pe.wait_ge(nat_ready, a * 2 + 2)
                pe.wait_ge(chosen_ready, a + 1)
                for t in range(T + 1):
                    to = SIDE[0][:, t * E:(t + 1) * E]
                    for earlier in range(t):
                        last = pe.matmul(to, w["ones_b"][:, :], chosen[:, earlier, :], start=(earlier == 0), stop=(t == T and earlier == T - 1))
                    if t < T:
                        last = pe.matmul(to, w["before_b"][:, :], chosen[:, t, :], start=(t == 0), stop=True)
                last.then_inc(prefix_filled, 1)

            def release_post(a, par):
                pe.wait_ge(logits_ready, a + 1)
                pe.wait_ge(rows_ready, a + 1)

            FRONT = {2: turn_hs, 3: project_qk, 4: release_front, 14: project_v}
            POST = {5: turn_pv((0, 1)), 6: turn_pv((2, 3)), 7: turn_ao, 8: project_out, 9: natural,
                    10: router, 12: prefix, 13: release_post}

            def score_for_max(a, i, par):
                n = score_slot(i)
                if i % (SC // 2) == 0:
                    pe.wait_ge(half_loaded[i // (SC // 2)], (a + 1) * HALF)
                wait(pe, scm_drained, a * PER_UNIT + n - 1)
                h, t = i // T, i % T
                pe.matmul(SCM[n % 2][:, :], QS[par][0:K_MAX, h, t * P:(t + 1) * P], KS[par][0:K_MAX, h, :],
                          start=True, stop=True).then_inc(scm_filled, 1)

            def turn_maxima(a, q):
                n = max_slot(q)
                pe.wait_ge(scm_drained, a * PER_UNIT + n - 1)
                pe.wait_ge(m3_ready, a * QUARTERS + q + 1)
                rows = SCM[n % 2].bitcast(BF16)
                for t in range(T):
                    last = pe.transpose(rows[0:PARTS * HQ, t * P:(t + 1) * P],
                                        m3[:, t, :, :].rearrange("p c h -> p (c h)"), w["ident_b"][:, :])
                last.then_inc(mT_filled, 1)

            def score(a, i, par):
                q, j = divmod(i, PER_Q)
                t, h = j // HQ, q * HQ + j % HQ
                if j == 0:
                    pe.wait_ge(m_loaded[q], a * 16 + 16)
                wait(pe, probs_ready, a * SC + i - 1)
                pe.matmul(SCE[i % 2][:, :], KS[par][0:K_EXP, h, t * P:(t + 1) * P], QS[par][0:K_EXP, h, :],
                          start=True, stop=True).then_inc(sce_filled, 1)

            def weigh(a, i, par):
                q, j = divmod(i, PER_Q)
                t, hq = j // HQ, j % HQ
                if j == 0:
                    wait(pe, pvs_ready, a * QUARTERS + q - 1)
                pe.wait_ge(probs_ready, a * SC + i + 1)
                pe.matmul(PVB[q % 2][hq * PV_W:(hq + 1) * PV_W, :], V[par][:, t, q * HQ + hq, :],
                          PT[:, i % 8, :], start=(t == 0), stop=(t == T - 1)).then_inc(pv_used, 1)

            def turn(e, s, f, p, par=None):
                par_e, par_s = parity(e, 0, par), parity(s, 1, par)
                par_p = parity(p, 1, par)
                if e is not None:
                    pe.wait_ge(v_ready, e + 1)
                for g in range(GROUPS):
                    for i in range(g * HQ, (g + 1) * HQ):
                        if e is not None:
                            score(e, i, par_e)
                        if s is not None:
                            score_for_max(s, i, par_s)
                    if s is not None and g % HQ == 0 and g >= 1:
                        turn_maxima(s, g // HQ - 1)
                    if e is not None and g >= 1:
                        for i in range((g - 1) * HQ, g * HQ):
                            weigh(e, i, par_e)
                    if f is not None and g in FRONT:
                        FRONT[g](f, None)
                    if p is not None and g in POST:
                        POST[g](p, par_p)
                if s is not None:
                    turn_maxima(s, QUARTERS - 1)
                if e is not None:
                    for i in range((GROUPS - 1) * HQ, GROUPS * HQ):
                        weigh(e, i, par_e)

            pe.wait_ge(init, INIT)
            run_turns(pe, turn)


def tile_tables(nc, new_sem, tag, nth, w, tri, routing, tokens, E, NT):
    REG = region_rows(tokens)
    start_row, tables, ROW, IDX = (routing[n] for n in ("start_row", "tables", "ROW", "IDX"))
    RUNGS = tokens // P + 1
    PAIRS = 2 * tokens // P

    with ExitStack() as ctx:
        def sb(name, shape, dt=F32):
            return ctx.enter_context(nc.sbuf_tensor(f"{tag}_{name}", shape, dt))

        count, tiles, ends = sb("count", [P, E]), sb("tiles", [P, E]), sb("ends", [P, E])
        above = sb("above", [P, E, RUNGS])
        low, lower = sb("low", [P, E, E]), sb("total", [P, 1])
        jj = sb("jj", [P, NT])
        unused, less = sb("unused", [P, PAIRS, E - 1]), sb("less", [P, PAIRS])
        past, work = sb("past", [P, NT, E]), sb("work", [P, NT, E])
        expert, first, at = sb("expert", [P, NT]), sb("first", [P, NT]), sb("at", [P, NT])
        step = new_sem("tables_step")
        block = ctx.enter_context(nc.Block())

        @block.vector
        def _(dve):
            s = Steps(dve, step, nth, 21)
            own = s.own
            j = w["tile"][:, :]
            own(dve.tensor_tensor(count[:, :], start_row[:, :], w["region"][:, :], ALU.subtract))
            own(dve.tensor_tensor(above[:, :, :], count[:, :].unsqueeze(2).to_broadcast([P, E, RUNGS]),
                                  w["rung"][:, :].unsqueeze(1).to_broadcast([P, E, RUNGS]), ALU.is_gt))
            own(dve.tensor_reduce(tiles[:, :], above[:, :, :], AX.X, ALU.add))
            own(dve.tensor_tensor(low[:, :, :], tri[:, :, :], tiles[:, :].unsqueeze(1).to_broadcast([P, E, E]), ALU.mult))
            own(dve.tensor_reduce(ends[:, :], low[:, :, :], AX.X, ALU.add))
            own(dve.tensor_tensor(ends[:, :], ends[:, :], tiles[:, :], ALU.add))
            own(dve.tensor_scalar(lower[:, :], ends[:, E - 1:E], -1.0, None, ALU.add))
            own(dve.tensor_tensor(jj[:, :], j, lower[:, 0:1].to_broadcast([P, NT]), ALU.min))
            own(dve.tensor_tensor(past[:, :, :], jj[:, :].unsqueeze(2).to_broadcast([P, NT, E]),
                                  ends[:, :].unsqueeze(1).to_broadcast([P, NT, E]), ALU.is_ge))
            own(dve.tensor_reduce(expert[:, :], past[:, :, :], AX.X, ALU.add))
            own(dve.tensor_tensor(work[:, :, :], past[:, :, :],
                                  tiles[:, :].unsqueeze(1).to_broadcast([P, NT, E]), ALU.mult))
            own(dve.tensor_reduce(first[:, :], work[:, :, :], AX.X, ALU.add))
            own(dve.tensor_tensor(first[:, :], jj[:, :], first[:, :], ALU.subtract))
            own(dve.tensor_scalar(at[:, :], expert[:, :], float(REG), None, ALU.mult))
            own(dve.scalar_tensor_tensor(at[:, :], first[:, :], float(P), at[:, :], ALU.mult, ALU.add))
            dve.tensor_copy(tables[:, 0, :], expert[:, :])
            own(dve.tensor_copy(tables[:, 1, :], at[:, :]))
            own(dve.tensor_scalar(tiles[:, :], tiles[:, :], -float(P), float(REG), ALU.mult, ALU.add))
            own(dve.tensor_tensor(unused[:, :, :], ROW[:, :, :].rearrange("p t n -> p (t n)").unsqueeze(2).to_broadcast([P, PAIRS, E - 1]),
                                  w["region"][:, 1:E].unsqueeze(1).to_broadcast([P, PAIRS, E - 1]), ALU.is_ge))
            own(dve.tensor_tensor(unused[:, :, :], unused[:, :, :],
                                  tiles[:, 0:E - 1].unsqueeze(1).to_broadcast([P, PAIRS, E - 1]), ALU.mult))
            own(dve.tensor_reduce(less[:, :], unused[:, :, :], AX.X, ALU.add))
            own(dve.tensor_tensor(IDX[:, :, :].rearrange("p t n -> p (t n)"), ROW[:, :, :].rearrange("p t n -> p (t n)"),
                                  less[:, :], ALU.subtract))
            s.end()


def experts(nc, new_sem, tag, nth, xs, ys, bank, ident, w, routing, dims, NT):
    B, S, D, H, HD, KPH, E, F = dims
    DC, FC = D // P, F // P
    tables = routing["tables"]
    BASE = nth * NT
    STAGES = 4

    with ExitStack() as ctx:
        def sb(name, shape, dt=F32):
            return ctx.enter_context(nc.sbuf_tensor(f"{tag}_{name}", shape, dt))

        def sem(name):
            return new_sem(f"moe_{name}")

        XN, XT = sb("xn", [P, 2, D]), sb("xT", [P, 2, DC, P])
        Hb, G, GT = sb("hb", [P, 2, F]), sb("g", [P, 2, F]), sb("gT", [P, 2, FC, P])
        Y = sb("y", [P, 2, D])

        x_loaded, xT_filled, xT_ready = [sem("x_loaded0"), sem("x_loaded1")], sem("xT_filled"), sem("xT_ready")
        h_filled, h_ready, g_ready = sem("h_filled"), sem("h_ready"), sem("g_ready")
        gT_filled, gT_ready, o_filled, y_ready = sem("gT_filled"), sem("gT_ready"), sem("o_filled"), sem("y_ready")
        y_stored = [sem("y_stored0"), sem("y_stored1")]
        BEFORE = [nth * ((NT + 1) // 2), nth * (NT // 2)]

        XB, HB, GB, OB = bank[0:2], bank[2:4], bank[4:6], bank[6:8]

        def run_slots(eng, slot):
            peeled = STAGES + 1
            for s in range(peeled):
                slot(s, 0)
            n = (NT - peeled) // 2
            with eng.Fori(0, n) as k:
                for odd in range(2):
                    slot(peeled + odd, k)
            for s in range(peeled + 2 * n, NT + STAGES - 1):
                slot(s, 0)

        def live(s, k, stage):
            return 0 <= s - stage < NT or not isinstance(k, int)

        block = ctx.enter_context(nc.Block())

        @block.sync
        def _(sp):
            def load(s, k):
                buf, j = s % 2, k * 2 + s
                at = sp.value_load(tables[0:1, 1, ds(j, 1)], min_val=0, max_val=xs.shape[0] - P)
                wait(sp, xT_filled, j + (BASE - 1))
                sp.dma_start(XN[:, buf, :], xs[ds(at, P), :]).then_inc(x_loaded[buf], 16)

            def slot(s, k):
                if live(s, k, 0):
                    load(s, k)

            run_slots(sp, slot)
            for buf in range(2):
                sp.wait_ge(y_stored[buf], 16 * (BEFORE[buf] + (NT + 1 - buf) // 2))

        @block.scalar
        def _(act):
            def slot(s, k):
                if live(s, k, 1):
                    buf, j = (s - 1) % 2, k * 2 + (s - 1)
                    act.wait_ge(h_ready, j + (BASE + 1))
                    wait(act, gT_filled, j + (BASE - 1))
                    act.activation(G[:, buf, :], Hb[:, buf, :], ACT.Gelu).then_inc(g_ready, 1)
                if live(s, k, 2):
                    buf, j = (s - 2) % 2, k * 2 + (s - 2)
                    act.wait_ge(gT_filled, j + (BASE + 1))
                    wait(act, o_filled, j + (BASE - 1))
                    act.activation(GT[:, buf, :, :].rearrange("p f t -> p (f t)"), GB[buf][:, :],
                                   ACT.Copy).then_inc(gT_ready, 1)
                if live(s, k, 3):
                    buf, j = (s - 3) % 2, k * 2 + (s - 3)
                    act.wait_ge(y_ready, j + (BASE + 1))
                    act.dma_start(ys[ds(j * P, P), :], Y[:, buf, :]).then_inc(y_stored[buf], 16)

            run_slots(act, slot)

        @block.vector
        def _(dve):
            def slot(s, k):
                if live(s, k, 0):
                    buf, j = s % 2, k * 2 + s
                    dve.wait_ge(xT_filled, j + (BASE + 1))
                    wait(dve, h_filled, j + (BASE - 1))
                    dve.tensor_copy(XT[:, buf, :, :].rearrange("p c t -> p (c t)"),
                                    XB[buf][:, 0:D]).then_inc(xT_ready, 1)
                if live(s, k, 1):
                    buf, j = (s - 1) % 2, k * 2 + (s - 1)
                    e = dve.value_load(tables[0:1, 0, ds(j, 1)], min_val=0, max_val=E - 1)
                    wait(dve, g_ready, j + (BASE - 1))
                    dve.wait_ge(h_filled, j + (BASE + 1))
                    dve.tensor_tensor(Hb[:, buf, :], HB[buf][:, :], w["b1"][:, ds(e * F, F)], ALU.add).then_inc(h_ready, 1)
                if live(s, k, 3):
                    buf, j = (s - 3) % 2, k * 2 + (s - 3)
                    e = dve.value_load(tables[0:1, 0, ds(j, 1)], min_val=0, max_val=E - 1)
                    dve.wait_ge(o_filled, j + (BASE + 1))
                    wait(dve, y_stored[buf], stored(s - 3, k, buf))
                    dve.tensor_tensor(Y[:, buf, :], OB[buf][:, 0:D], w["b2"][:, ds(e * D, D)], ALU.add).then_inc(y_ready, 1)

            def stored(s, k, buf):
                return (k + ((s - buf) // 2 + BEFORE[buf])) * 16

            run_slots(dve, slot)

        @block.tensor
        def _(pe):
            def slot(s, k):
                if live(s, k, 0):
                    buf, j = s % 2, k * 2 + s
                    pe.wait_ge(x_loaded[buf], (k + ((s - buf) // 2 + BEFORE[buf] + 1)) * 16)
                    wait(pe, xT_ready, j + (BASE - 1))
                    for c in range(DC):
                        last = pe.transpose(XB[buf][:, c * P:(c + 1) * P], XN[:, buf, c * P:(c + 1) * P], ident[:, :])
                    last.then_inc(xT_filled, 1)
                if live(s, k, 1):
                    buf, j = (s - 1) % 2, k * 2 + (s - 1)
                    e = pe.value_load(tables[0:1, 0, ds(j, 1)], min_val=0, max_val=E - 1)
                    wait(pe, h_ready, j + (BASE - 1))
                    pe.wait_ge(xT_ready, j + (BASE + 1))
                    for c in range(DC):
                        last = pe.matmul(HB[buf][:, :], XT[:, buf, c, :], w["w1"][:, ds(e * (DC * F) + c * F, F)],
                                         start=(c == 0), stop=(c == DC - 1))
                    last.then_inc(h_filled, 1)
                if live(s, k, 2):
                    buf, j = (s - 2) % 2, k * 2 + (s - 2)
                    pe.wait_ge(g_ready, j + (BASE + 1))
                    wait(pe, gT_ready, j + (BASE - 1))
                    for f in range(FC):
                        last = pe.transpose(GB[buf][:, f * P:(f + 1) * P], G[:, buf, f * P:(f + 1) * P], ident[:, :])
                    last.then_inc(gT_filled, 1)
                if live(s, k, 3):
                    buf, j = (s - 3) % 2, k * 2 + (s - 3)
                    e = pe.value_load(tables[0:1, 0, ds(j, 1)], min_val=0, max_val=E - 1)
                    wait(pe, y_ready, j + (BASE - 1))
                    pe.wait_ge(gT_ready, j + (BASE + 1))
                    for f in range(FC):
                        last = pe.matmul(OB[buf][:, 0:D], GT[:, buf, f, :], w["w2"][:, ds(e * (FC * D) + f * D, D)],
                                         start=(f == 0), stop=(f == FC - 1))
                    last.then_inc(o_filled, 1)

            run_slots(pe, slot)


def combine(nc, new_sem, tag, nth, xr, ys, x_out, routing, dims):
    B, S, D = dims[0:3]
    T = S // P
    BASE = nth * B
    GATHERED = 2 * T * 16
    IDX, CW = routing["IDX"], routing["CW"]

    with ExitStack() as ctx:
        def sb(name, shape, dt=F32):
            return ctx.enter_context(nc.sbuf_tensor(f"{tag}_{name}", shape, dt))

        def sem(name):
            return new_sem(f"combine_{name}")

        XR = [sb(f"xr{i}", [P, T, D]) for i in range(2)]
        R = [sb(f"rows{i}", [P, T, 2, D]) for i in range(2)]
        Y = [sb(f"y{i}", [P, T, D]) for i in range(2)]
        idx = [sb(f"idx{i}", [P, T, 2], I32) for i in range(2)]
        cw = [sb(f"cw{i}", [P, T, 2]) for i in range(2)]
        zero = sb("zero", [P, 1])
        carrier = sb("carrier", [P, 1])
        Y_carrier = sb("dve_carrier", [P, 1])

        xr_loaded, gathered = [sem("xr_loaded0"), sem("xr_loaded1")], [sem("gathered0"), sem("gathered1")]
        idx_ready, y_ready, y_stored, half_ready = (
            sem("idx_ready"), sem("y_ready"), [sem("y_stored0"), sem("y_stored1")], sem("half_ready"))
        zeroed, carried = sem("zeroed"), sem("carried")
        block = ctx.enter_context(nc.Block())

        @block.sync
        def _(sp):
            def load(k, i):
                b = k * 2 + i
                wait(sp, y_ready, b + (BASE - 1))
                sp.dma_start(XR[i][:, :, :], xr[b].rearrange("(t p) d -> p t d", p=P)).then_inc(xr_loaded[i], 16)

            def store(k, i):
                b = k * 2 + i
                sp.wait_ge(y_ready, b + (BASE + 1))
                sp.dma_start(x_out[b].rearrange("(t p) d -> p t d", p=P), Y[i][:, :, :]).then_inc(y_stored[i], 16)

            load(0, 0)
            load(0, 1)
            with sp.Fori(0, B // 2 - 1) as k:
                for i in range(2):
                    store(k, i)
                    load(k + 1, i)
            for i in range(2):
                store(B // 2 - 1, i)
            for i in range(2):
                sp.wait_ge(y_stored[i], 16 * ((BASE + B) // 2 + 1))

        @block.gpsimd
        def _(pool):
            pool.memset(zero[:, :], 0.0).then_inc(zeroed, 1)
            if nth == 0:
                pool.memset(carrier[:, :], 0.0).then_inc(carried, 1)
                for i in range(2):
                    pool.memset(Y[i][:, 0, 0:1], 0.0).then_inc(y_stored[i], 16)
            pool.wait_ge(zeroed, nth + 1)
            with pool.Fori(0, B // 2) as k:
                for i in range(2):
                    pool.wait_ge(idx_ready, k * 2 + (i + BASE + 1))
                    pool.wait_ge(carried, k * 2 + (i + BASE + 1))
                    pool.tensor_tensor(carrier[:, :], zero[:, :], zero[:, :], ALU.add).then_inc(carried, 1)
                    for t in range(T):
                        for n in range(2):
                            pool.indirect_dma_start(
                                out=R[i][:, t, n, :], out_offset=None, in_=ys,
                                in_offset=bass.IndirectOffsetOnAxis(ap=idx[i][:, t, n:n + 1], axis=0),
                            ).then_inc(gathered[i], 16)

        @block.vector
        def _(dve):
            def prepare(k, i):
                at = ds((k * 2 + i) * T, T)
                dve.tensor_copy(cw[i][:, :, :], CW[:, at, :])
                dve.tensor_copy(idx[i][:, :, :], IDX[:, at, :]).then_inc(idx_ready, 1)

            def add(k, i):
                b = k * 2 + i
                dve.wait_ge(xr_loaded[i], (k + (BASE // 2 + 1)) * 16)
                dve.wait_ge(gathered[i], (k + (BASE // 2 + 1)) * GATHERED)
                dve.wait_ge(idx_ready, b + (BASE + 1))
                dve.wait_ge(y_stored[i], (k + (BASE // 2 + 1)) * 16)
                for n in range(2):
                    for t in range(T):
                        last = dve.scalar_tensor_tensor(Y[i][:, t, :], R[i][:, t, n, :], cw[i][:, t, n:n + 1],
                                                        Y[i][:, t, :] if n else XR[i][:, t, :], ALU.mult, ALU.add)
                    last.then_inc(half_ready if n == 0 else y_ready, 1)
                    if n == 0:
                        dve.wait_ge(half_ready, b + (BASE + 1))

            prepare(0, 0)
            prepare(0, 1)
            with dve.Fori(0, B // 2 - 1) as k:
                for i in range(2):
                    add(k, i)
                    dve.wait_ge(y_ready, k * 2 + (i + BASE + 1))
                    dve.memset(Y_carrier[:, :], 0.0)
                    prepare(k + 1, i)
            for i in range(2):
                add(B // 2 - 1, i)


def attention_pass(nc, new_sem, tag, x_in, x_out, bank, ident, ident_b, w, B, S, D, H, DK, LSEG):
    T, DC, NSEG, PAIRS = S // P, D // P, S // LSEG, H // 2
    HK = H * DK
    KC = HK // P
    VW = DK + 1
    SCALE = 1.0 / float(np.sqrt(DK))
    QK = 2 * PAIRS
    FRONT, PER_TILE = LN_STEPS, 9

    with ExitStack() as ctx:
        def sb(name, shape, dt=F32):
            return ctx.enter_context(nc.sbuf_tensor(f"{tag}_{name}", shape, dt))

        def sem(name):
            return new_sem(f"{tag}_{name}")

        X, HS, Y = sb("x", [P, T, D]), sb("hs", [P, T, D]), sb("y", [P, T, D])
        stats, mv = sb("stats", [P, T, 6]), sb("mv", [P, T, 2])
        ve, sd, rs = sb("ve", [P, T]), sb("sd", [P, T]), sb("rs", [P, T])
        carrier = sb("carrier", [P, 1])
        hsT = sb("hsT", [P, DC, S])
        qk = sb("qk", [P, QK, S])
        low = sb("low", [P, 2, S])
        ex = sb("ex", [P, 2, S])
        sqk = sb("sqk", [P, QK, S])
        sk = sb("sk", [P, T, HK])
        V = sb("V", [P, T, H, VW])
        MEM = sb("MEM", [P, NSEG, PAIRS, VW])
        SS = sb("SS", [P, 2, H, LSEG])
        mx, rr = sb("mx", [P, H]), sb("rr", [P, H])
        PB = sb("PB", [P, H, P])
        PBT = sb("PBT", [P, H, P])
        rz = sb("rz", [P, 2, PAIRS])
        AM = sb("AM", [P, HK])
        AL = sb("AL", [P, HK])
        AT = sb("AT", [P, HK])
        attT = sb("attT", [P, KC, P])

        x_loaded, y_ready, y_stored = sem("x_loaded"), sem("y_ready"), sem("y_stored")
        var_ready, sd_ready, hs_ready = sem("var_ready"), sem("sd_ready"), sem("hs_ready")
        hsT_filled, hsT_ready = sem("hsT_filled"), sem("hsT_ready")
        qk_filled, qk_ready, low_ready, ex_ready, sqk_ready = (
            sem("qk_filled"), sem("qk_ready"), sem("low_ready"), sem("ex_ready"), sem("sqk_ready"))
        v_filled, v_ready, sk_filled, sk_ready = sem("v_filled"), sem("v_ready"), sem("sk_filled"), sem("sk_ready")
        u_filled, mem_ready = sem("u_filled"), sem("mem_ready")
        s_filled, s_ready, e_ready, pb_ready = sem("s_filled"), sem("s_ready"), sem("e_ready"), sem("pb_ready")
        pbT_filled, pbT_ready = sem("pbT_filled"), sem("pbT_ready")
        l_filled, am_filled, at_ready = sem("l_filled"), sem("am_filled"), sem("at_ready")
        attT_filled, attT_ready, o_filled = sem("attT_filled"), sem("attT_ready"), sem("o_filled")
        dve_front, dve_tile = sem("dve_front"), sem("dve_tile")
        init = sem("init")
        INIT = 4

        RING = bank[2:6]
        block = ctx.enter_context(nc.Block())

        @block.sync
        def _(sp):
            with sp.Fori(0, B) as a:
                sp.dma_start(X[:, :, :], x_in[a].rearrange("(t p) d -> p t d", p=P)).then_inc(x_loaded, 16)
                wait(sp, y_ready, a * T + T)
                sp.dma_start(x_out[a].rearrange("(t p) d -> p t d", p=P), Y[:, :, :]).then_inc(y_stored, 16)
            sp.wait_ge(y_stored, 16 * (B + 1))

        @block.gpsimd
        def _(pool):
            pool.memset(PB[:, :, :], 0.0).then_inc(init, 1)
            pool.memset(Y[:, 0, 0:1], 0.0).then_inc(y_stored, 16)
            pool.memset(V[:, :, :, DK:VW], 1.0).then_inc(init, 1)
            pool.memset(MEM[:, 0, :, 0:DK], 0.0).then_inc(init, 1)
            pool.memset(MEM[:, 0, :, DK:VW], 1.0 / DK).then_inc(init, 1)

        @block.scalar
        def _(act):
            act.wait_ge(init, INIT)
            with act.Fori(0, B) as a:
                act.wait_ge(var_ready, a + 1)
                act.activation(sd[:, :], ve[:, :], ACT.Sqrt).then_inc(sd_ready, 1)
                for c in range(DC):
                    act.wait_ge(hsT_filled, a * DC + c + 1)
                    act.activation(hsT[:, c, :], bank[c], ACT.Copy).then_inc(hsT_ready, 1)
                for i in range(QK + 1):
                    if i < QK:
                        act.wait_ge(qk_filled, a * QK + i + 1)
                        act.activation(qk[:, i, :], RING[i % 4], ACT.Copy).then_inc(qk_ready, 1)
                    if i >= 1:
                        act.wait_ge(low_ready, a * QK + i)
                        if i >= 3:
                            act.wait_ge(sqk_ready, a * QK + i - 2)
                        act.activation(ex[:, (i - 1) % 2, :], low[:, (i - 1) % 2, :], ACT.Exp).then_inc(ex_ready, 1)
                for t in range(T):
                    act.wait_ge(v_filled, a * T + t + 1)
                    act.activation(V[:, t, :, 0:DK], RING[t].rearrange("p (h v) -> p h v", v=DK),
                                   ACT.Copy).then_inc(v_ready, 1)
                for t in range(T):
                    act.wait_ge(sk_filled, a * T + t + 1)
                    act.activation(sk[:, t, :], RING[t], ACT.Copy).then_inc(sk_ready, 1)
                for t in range(T):
                    act.wait_ge(s_ready, a * T + t + 1)
                    act.activation(SS[:, t % 2, :, :], SS[:, t % 2, :, :], ACT.Exp, scale=SCALE).then_inc(e_ready, 1)
                    act.wait_ge(pbT_filled, a * T + t + 1)
                    for n in range(2):
                        act.activation(PBT[:, n * PAIRS:(n + 1) * PAIRS, :].rearrange("p h i -> p (h i)"),
                                       bank[2 + n], ACT.Copy).then_inc(pbT_ready, 1)
                    act.wait_ge(attT_filled, a * T + t + 1)
                    act.activation(attT[:, :, :].rearrange("p c i -> p (c i)"), bank[5], ACT.Copy).then_inc(attT_ready, 1)

        @block.vector
        def _(dve):
            dve.wait_ge(init, INIT)
            with dve.Fori(0, B) as a:
                s = Steps(dve, dve_front, a, FRONT)
                dve.wait_ge(x_loaded, a * 16 + 16)
                ln_variance(dve, s, X, stats, mv, ve, T, var_ready, carrier[:, :])
                ln_normalise(dve, s, X, HS, mv, ve, sd, rs, T, sd_ready, hs_ready, a)
                s.end()
                for i in range(QK + 1):
                    if i < QK:
                        dve.wait_ge(qk_ready, a * QK + i + 1)
                        if i >= 2:
                            dve.wait_ge(ex_ready, a * QK + i - 1)
                        dve.tensor_scalar(low[:, i % 2, :], qk[:, i, :], 0.0, None, ALU.min).then_inc(low_ready, 1)
                    if i >= 1:
                        dve.wait_ge(ex_ready, a * QK + i)
                        dve.scalar_tensor_tensor(sqk[:, i - 1, :], qk[:, i - 1, :], 0.0, ex[:, (i - 1) % 2, :],
                                                 ALU.max, ALU.add).then_inc(sqk_ready, 1)
                for n in range(NSEG - 1):
                    dve.wait_ge(u_filled, a * (NSEG - 1) + n + 1)
                    if n >= 1:
                        dve.wait_ge(mem_ready, a * (NSEG - 1) + n)
                    dve.tensor_tensor(MEM[:, n + 1, :, :], MEM[:, n, :, :],
                                      bank[2 + n % 2][:, 0:PAIRS * VW].rearrange("p (h v) -> p h v", v=VW),
                                      ALU.add).then_inc(mem_ready, 1)
                s = Steps(dve, dve_tile, a, PER_TILE * T)
                for t in range(T):
                    dve.wait_ge(s_filled, a * T + t + 1)
                    if t >= 1:
                        dve.wait_ge(pbT_filled, a * T + t)
                    for n in range(2):
                        sc = bank[6 + n][:, 0:PAIRS * LSEG].rearrange("p (h j) -> p h j", j=LSEG)
                        last = dve.tensor_reduce(mx[:, n * PAIRS:(n + 1) * PAIRS], sc, AX.X, ALU.max)
                    s.own(last)
                    for n in range(2):
                        sc = bank[6 + n][:, 0:PAIRS * LSEG].rearrange("p (h j) -> p h j", j=LSEG)
                        last = dve.tensor_tensor(SS[:, t % 2, n * PAIRS:(n + 1) * PAIRS, :], sc,
                                                 mx[:, n * PAIRS:(n + 1) * PAIRS].unsqueeze(2).to_broadcast([P, PAIRS, LSEG]),
                                                 ALU.subtract)
                    last.then_inc(s_ready, 1)
                    dve.wait_ge(e_ready, a * T + t + 1)
                    s.own(dve.tensor_reduce(rr[:, :], SS[:, t % 2, :, :], AX.X, ALU.add))
                    s.own(dve.reciprocal(rr[:, :], rr[:, :]))
                    for n in range(2):
                        half = slice(n * LSEG, (n + 1) * LSEG)
                        last = dve.tensor_tensor(PB[half, :, half], SS[half, t % 2, :, :],
                                                 rr[half, :].unsqueeze(2).to_broadcast([LSEG, H, LSEG]), ALU.mult)
                    last.then_inc(pb_ready, 1)
                    dve.wait_ge(am_filled, a * T + t + 1)
                    by_head = AM[:, :].rearrange("p (c two v) -> p two c v", two=2, v=DK)
                    for n in range(2):
                        am = bank[n][:, 0:PAIRS * VW].rearrange("p (c v) -> p c v", v=VW)
                        last = dve.reciprocal(rz[:, n, :], am[:, :, DK])
                    s.own(last)
                    for n in range(2):
                        am = bank[n][:, 0:PAIRS * VW].rearrange("p (c v) -> p c v", v=VW)
                        last = dve.tensor_tensor(by_head[:, n, :, :], am[:, :, 0:DK],
                                                 rz[:, n, :].unsqueeze(2).to_broadcast([P, PAIRS, DK]), ALU.mult)
                    s.own(last)
                    s.own(dve.tensor_tensor(AM[:, :], AM[:, :], w["gate"][:, :], ALU.mult))
                    dve.wait_ge(l_filled, a * T + t + 1)
                    s.own(dve.tensor_tensor(AL[:, :], bank[4], w["omg"][:, :], ALU.mult))
                    if t >= 1:
                        dve.wait_ge(attT_filled, a * T + t)
                    dve.tensor_tensor(AT[:, :], AM[:, :], AL[:, :], ALU.add).then_inc(at_ready, 1)
                    if t == 0:
                        dve.wait_ge(y_stored, a * 16 + 16)
                    dve.wait_ge(o_filled, a * T + t + 1)
                    s.own(dve.tensor_copy(Y[:, t, :], bank[5][:, 0:D]))
                    s.own(dve.memset(rz[:, :, 0:1], 0.0))
                    dve.tensor_tensor(Y[:, t, :], Y[:, t, :], X[:, t, :], ALU.add).then_inc(y_ready, 1)
                s.end()

        @block.tensor
        def _(pe):
            def carry(free):
                pe.matmul(free[:, 510:512], ident_b[:, :], ident_b[:, 0:2], start=True, stop=True)

            pe.wait_ge(init, INIT)
            with pe.Fori(0, B) as a:
                pe.wait_ge(hs_ready, a + 1)
                for c in range(DC):
                    for t in range(T):
                        last = pe.transpose(bank[c][:, t * P:(t + 1) * P], HS[:, t, c * P:(c + 1) * P], ident[:, :])
                    last.then_inc(hsT_filled, 1)
                pe.wait_ge(hsT_ready, (a + 1) * DC)
                for i in range(QK):
                    weight = w["la_q"] if i < PAIRS else w["la_k"]
                    pair = i % PAIRS
                    if i >= 4:
                        pe.wait_ge(qk_ready, a * QK + i - 3)
                    for c in range(DC):
                        last = pe.matmul(RING[i % 4], weight[:, c, pair * P:(pair + 1) * P], hsT[:, c, :],
                                         start=(c == 0), stop=(c == DC - 1))
                    last.then_inc(qk_filled, 1)
                for t in range(T):
                    pe.wait_ge(qk_ready, a * QK + QK - 4 + t + 1)
                    for c in range(DC):
                        last = pe.matmul(RING[t], hsT[:, c, t * P:(t + 1) * P], w["la_v"][:, c, :],
                                         start=(c == 0), stop=(c == DC - 1))
                    last.then_inc(v_filled, 1)
                pe.wait_ge(sqk_ready, (a + 1) * QK)
                for t in range(T):
                    pe.wait_ge(v_ready, a * T + t + 1)
                    for pair in range(PAIRS):
                        last = pe.transpose(RING[t][:, pair * P:(pair + 1) * P],
                                            sqk[:, PAIRS + pair, t * P:(t + 1) * P], ident[:, :])
                    last.then_inc(sk_filled, 1)
                pe.wait_ge(sk_ready, (a + 1) * T)
                carry(bank[2])
                for n in range(NSEG - 1):
                    t, rows = n // 2, slice((n % 2) * LSEG, (n % 2 + 1) * LSEG)
                    if n >= 2:
                        pe.wait_ge(mem_ready, a * (NSEG - 1) + n - 1)
                        carry(bank[2 + n % 2])
                    for h in range(H):
                        pair, one = h // 2, h % 2
                        last = pe.matmul(bank[2 + n % 2][one * DK:(one + 1) * DK, pair * VW:(pair + 1) * VW],
                                         sk[rows, t, h * DK:(h + 1) * DK], V[rows, t, h, :], start=True, stop=True)
                    last.then_inc(u_filled, 1)
                pe.wait_ge(mem_ready, (a + 1) * (NSEG - 1))
                carry(bank[6])
                for t in range(T):
                    if t >= 1:
                        pe.wait_ge(s_ready, a * T + t)
                        carry(bank[6])
                    for h in range(H):
                        pair, one = h // 2, h % 2
                        part = slice(one * DK, (one + 1) * DK)
                        for n in range(2):
                            seg = slice((2 * t + n) * LSEG, (2 * t + n + 1) * LSEG)
                            last = pe.matmul(bank[6 + one][n * LSEG:(n + 1) * LSEG, pair * LSEG:(pair + 1) * LSEG],
                                             qk[part, pair, seg], qk[part, PAIRS + pair, seg], start=True, stop=True)
                    last.then_inc(s_filled, 1)
                    for h in range(H):
                        pair, one = h // 2, h % 2
                        part = slice(one * DK, (one + 1) * DK)
                        for n in range(2):
                            seg = slice((2 * t + n) * LSEG, (2 * t + n + 1) * LSEG)
                            last = pe.matmul(bank[one][n * LSEG:(n + 1) * LSEG, pair * VW:(pair + 1) * VW],
                                             sqk[part, pair, seg], MEM[part, 2 * t + n, pair, :], start=True, stop=True)
                    last.then_inc(am_filled, 1)
                    pe.wait_ge(pb_ready, a * T + t + 1)
                    for h in range(H):
                        last = pe.transpose(bank[2 + h // PAIRS][:, (h % PAIRS) * P:(h % PAIRS + 1) * P],
                                            PB[:, h, :], ident[:, :])
                    last.then_inc(pbT_filled, 1)
                    pe.wait_ge(pbT_ready, (a * T + t + 1) * 2)
                    for h in range(H):
                        last = pe.matmul(bank[4][:, h * DK:(h + 1) * DK], PBT[:, (h % 2) * PAIRS + h // 2, :],
                                         V[:, t, h, 0:DK], start=True, stop=True)
                    last.then_inc(l_filled, 1)
                    pe.wait_ge(at_ready, a * T + t + 1)
                    for c in range(KC):
                        last = pe.transpose(bank[5][:, c * P:(c + 1) * P], AT[:, c * P:(c + 1) * P], ident[:, :])
                    last.then_inc(attT_filled, 1)
                    pe.wait_ge(attT_ready, a * T + t + 1)
                    for c in range(KC):
                        last = pe.matmul(bank[5][:, 0:D], attT[:, c, :], w["la_o"][:, c, :],
                                         start=(c == 0), stop=(c == KC - 1))
                    last.then_inc(o_filled, 1)
                    pe.wait_ge(y_ready, a * T + t + 1)


def macaron(nc, x, Wq, Wk, Wv, betas, Wo, q_w, q_b, k_w, k_b, v_w, v_b, o_w, o_b,
            router_w, router_b, w1, b1, w2, b2, out):
    B, S, D = x.shape
    E, _, F = w1.shape
    H = 16
    LAT = k_w.shape[1]
    KPH, HD = LAT // H, D // H
    AH, ADK = betas.shape[1], betas.shape[3]
    LSEG = 64
    DC, FC = D // P, F // P
    TOKENS = B * S
    REG = region_rows(TOKENS)
    NT = 2 * TOKENS // P + E - 1
    assert LAT == P and AH * ADK == Wq.shape[1]

    with ExitStack() as ctx:
        def sb(name, shape, dt=F32):
            return ctx.enter_context(nc.sbuf_tensor(name, shape, dt))

        semaphores = {}

        def sem(name):
            if name not in semaphores:
                semaphores[name] = ctx.enter_context(nc.semaphore(name))
            return semaphores[name]

        bank = [ctx.enter_context(nc.psum_tensor(f"bank{i}", [P, 512], F32))[:, :] for i in range(8)]
        ident = sb("ident", [P, P])
        tri = sb("tri", [P, E, E])
        w = {
            "q_w": sb("q_w", [P, DC, LAT]), "k_w": sb("k_w", [P, DC, LAT]), "v_w": sb("v_w", [P, DC, LAT]),
            "q_bs": sb("q_bs", [P, 1]), "k_b": sb("k_b", [P, 1]), "v_b": sb("v_b", [P, LAT]),
            "o_w": sb("o_w", [P, D]), "o_b": sb("o_b", [P, DC]),
            "router_w": sb("router_w", [P, DC, E]), "router_b": sb("router_b", [P, E]),
            "w1": sb("w1", [P, E * DC * F]), "o_b_row": sb("o_b_row", [P, D]),
            "ident_b": sb("ident_b", [P, P], BF16), "ones_b": sb("ones_b", [P, P], BF16),
            "before_b": sb("before_b", [P, P], BF16),
            "region": sb("region", [P, E]), "partition": sb("partition", [P, 1]),
            "rung": sb("rung", [P, B * S // P + 1]), "tile": sb("tile", [P, NT]),
        }
        x1 = nc.dram_tensor("x1", (B, S, D), F32, kind="Internal").ap()
        x2 = nc.dram_tensor("x2", (B, S, D), F32, kind="Internal").ap()
        xr = nc.dram_tensor("xr", (B, S, D), F32, kind="Internal").ap()
        xs = nc.dram_tensor("routed_rows", (E * REG, D), F32, kind="Internal").ap()
        ys = nc.dram_tensor("expert_rows", (NT * P, D), F32, kind="Internal").ap()
        routing = {"ROW": sb("ROW", [P, TOKENS // P, 2]), "IDX": sb("IDX", [P, TOKENS // P, 2], I32), "CW": sb("CW", [P, TOKENS // P, 2]),
                   "start_row": sb("start_row", [P, E]), "tables": sb("tables", [P, 2, NT], I32)}
        scratch = [nc.dram_tensor(n, s, BF16, kind="Internal").ap() for n, s in
                   (("q_parts", (3, P, S)), ("k_parts", (3, P, S)), ("m_parts", (4, 3 * H // 4, S)))]

        loaded, q_full_loaded, made, zeroed, diag, gate_step = (
            sem("loaded"), sem("q_full_loaded"), sem("made"), sem("zeroed"), sem("diag"), sem("gate_step"))

        w1_loaded, w2_loaded = sem("w1_loaded"), sem("w2_loaded")

        def load_and_make():
            with ExitStack() as inner:
                q_full = inner.enter_context(nc.sbuf_tensor("q_full", [P, DC, D], F32))
                ones = inner.enter_context(nc.sbuf_tensor("ones", [P, E, E], F32))
                RUNGS = TOKENS // P + 1
                counts = inner.enter_context(nc.sbuf_tensor("counts", [P, 1 + E + RUNGS + NT], I32))
                block = inner.enter_context(nc.Block())

                plain = [
                    (w["k_w"][:, :, :], k_w.rearrange("(c p) n -> p c n", p=P)),
                    (w["v_w"][:, :, :], v_w.rearrange("(c p) n -> p c n", p=P)),
                    (w["k_b"][:, :], k_b.rearrange("(p one) -> p one", one=1)),
                    (w["v_b"][:, :], v_b.partition_broadcast(P)),
                    (w["o_w"][:, :], o_w[0:LAT, :]),
                    (w["o_b"][:, 0:1], o_b[0:P].rearrange("(p one) -> p one", one=1)),
                    (w["o_b"][:, 1:2], o_b[P:2 * P].rearrange("(p one) -> p one", one=1)),
                    (w["router_w"][:, :, :], router_w.rearrange("(c p) n -> p c n", p=P)),
                    (w["router_b"][:, :], router_b.partition_broadcast(P)),
                    (w["o_b_row"][:, :], o_b.partition_broadcast(P)),
                ]
                QB = 16 * (len(plain) + H)

                @block.sync
                def _(sp):
                    sp.dma_start(q_full[:, :, :], q_w.rearrange("(c p) n -> p c n", p=P)).then_inc(q_full_loaded, 16)
                    for h in range(H):
                        sp.dma_start(w["q_bs"][h * KPH:(h + 1) * KPH, :],
                                     q_b[h * HD:h * HD + KPH].rearrange("(p one) -> p one", one=1)).then_inc(loaded, 16)
                    for to, source in plain:
                        sp.dma_start(to, source).then_inc(loaded, 16)
                    sp.dma_start(w["w1"][:, :].rearrange("p (e c f) -> p e c f", e=E, c=DC),
                                 w1.rearrange("e (c p) f -> p e c f", p=P)).then_inc(w1_loaded, 16)

                @block.gpsimd
                def _(pool):
                    pool.memset(w["ones_b"][:, :], 1.0).then_inc(zeroed, 1)
                    pool.memset(ident[:, :], 0.0).then_inc(zeroed, 1)
                    pool.memset(ones[:, :, :], 1.0).then_inc(zeroed, 1)
                    pool.wait_ge(zeroed, 3)
                    pool.affine_select(out=ident[:, :], in_=ident[:, :], compare_op=ALU.not_equal, fill=1.0,
                                       base=0, pattern=[[-1, P]], channel_multiplier=1).then_inc(diag, 1)
                    pool.affine_select(out=tri[:, :, :], in_=ones[:, :, :], compare_op=ALU.is_gt, fill=0.0,
                                       base=0, pattern=[[1, E], [-1, E]], channel_multiplier=0).then_inc(diag, 1)
                    pool.affine_select(out=w["before_b"][:, :], in_=w["ones_b"][:, :], compare_op=ALU.is_gt, fill=0.0,
                                       base=0, pattern=[[1, P]], channel_multiplier=-1).then_inc(diag, 1)
                    pool.iota(counts[:, 0:1], pattern=[[0, 1]], base=0, channel_multiplier=1).then_inc(diag, 1)
                    pool.iota(counts[:, 1:1 + E], pattern=[[REG, E]], base=0, channel_multiplier=0).then_inc(diag, 1)
                    pool.iota(counts[:, 1 + E:1 + E + RUNGS], pattern=[[P, RUNGS]], base=0,
                              channel_multiplier=0).then_inc(diag, 1)
                    pool.iota(counts[:, 1 + E + RUNGS:], pattern=[[1, NT]], base=0, channel_multiplier=0).then_inc(diag, 1)

                @block.vector
                def _(dve):
                    dve.wait_ge(diag, 7)
                    dve.tensor_copy(w["ident_b"][:, :], ident[:, :]).then_inc(made, 1)
                    dve.tensor_copy(w["partition"][:, :], counts[:, 0:1]).then_inc(made, 1)
                    dve.tensor_copy(w["region"][:, :], counts[:, 1:1 + E]).then_inc(made, 1)
                    dve.tensor_copy(w["rung"][:, :], counts[:, 1 + E:1 + E + RUNGS]).then_inc(made, 1)
                    dve.tensor_copy(w["tile"][:, :], counts[:, 1 + E + RUNGS:]).then_inc(made, 1)
                    dve.wait_ge(q_full_loaded, 16)
                    for c in range(DC):
                        dve.tensor_copy(w["q_w"][:, c, :].rearrange("p (h k) -> p h k", k=KPH),
                                        q_full[:, c, :].rearrange("p (h x) -> p h x", x=HD)[:, :, 0:KPH]).then_inc(made, 1)
                    dve.wait_ge(loaded, QB)
                    dve.tensor_scalar(w["q_bs"][:, :], w["q_bs"][:, :], 1.0 / float(np.sqrt(KPH)), None,
                                      ALU.mult).then_inc(made, 1)
                    dve.wait_ge(made, 5 + DC + 1)

        dims = (B, S, D, H, HD, KPH, E, F)

        def ffn(tag, nth, x_in, x_out):
            attend_and_route(nc, sem, tag, nth, x_in, xr, xs, bank, ident, tri, w, scratch, routing, dims)
            tile_tables(nc, sem, tag + "t", nth, w, tri, routing, TOKENS, E, NT)
            with ExitStack() as inner:
                w["w2"] = inner.enter_context(nc.sbuf_tensor(f"{tag}_w2", [P, E * FC * D], F32))
                w["b1"] = inner.enter_context(nc.sbuf_tensor(f"{tag}_b1", [P, E * F], F32))
                w["b2"] = inner.enter_context(nc.sbuf_tensor(f"{tag}_b2", [P, E * D], F32))
                with nc.Block() as block:
                    @block.sync
                    def _(sp):
                        sp.dma_start(w["w2"][:, :].rearrange("p (e c d) -> p e c d", e=E, c=FC),
                                     w2.rearrange("e (c p) d -> p e c d", p=P)).then_inc(w2_loaded, 16)
                        sp.dma_start(w["b1"][:, :], b1.rearrange("e f -> (e f)").partition_broadcast(P)).then_inc(w2_loaded, 16)
                        sp.dma_start(w["b2"][:, :], b2.rearrange("e d -> (e d)").partition_broadcast(P)).then_inc(w2_loaded, 16)
                        sp.wait_ge(w1_loaded, 16)
                        sp.wait_ge(w2_loaded, 48 * (nth + 1))
                experts(nc, sem, tag + "m", nth, xs, ys, bank, ident, w, routing, dims, NT)
            combine(nc, sem, tag + "c", nth, xr, ys, x_out, routing, dims)

        load_and_make()
        ffn("f1", 0, x, x1)

        with ExitStack() as inner:
            HK = AH * ADK
            KC = HK // P
            la = {"la_q": [P, DC, HK], "la_k": [P, DC, HK], "la_v": [P, DC, HK], "la_o": [P, KC, D],
                  "gate": [P, HK], "omg": [P, HK]}
            la = {k: inner.enter_context(nc.sbuf_tensor(k, s, F32)) for k, s in la.items()}
            la_loaded = sem("la_loaded")
            exp_ready = sem("exp_ready")
            with nc.Block() as block:
                @block.sync
                def _(sp):
                    for k, source in (("la_q", Wq), ("la_k", Wk), ("la_v", Wv), ("la_o", Wo)):
                        sp.dma_start(la[k][:, :, :], source.rearrange("(c p) n -> p c n", p=P)).then_inc(la_loaded, 16)
                    sp.dma_start(la["gate"][:, :], betas.rearrange("a h b v -> (a h b v)").partition_broadcast(P)) \
                      .then_inc(la_loaded, 16)

                @block.scalar
                def _(act):
                    act.wait_ge(la_loaded, 80)
                    act.activation(la["gate"][:, :], la["gate"][:, :], ACT.Exp, scale=-1.0).then_inc(exp_ready, 1)

                @block.vector
                def _(dve):
                    dve.wait_ge(exp_ready, 1)
                    dve.tensor_scalar(la["gate"][:, :], la["gate"][:, :], 1.0, None, ALU.add).then_inc(gate_step, 1)
                    dve.wait_ge(gate_step, 1)
                    dve.reciprocal(la["gate"][:, :], la["gate"][:, :]).then_inc(gate_step, 1)
                    dve.wait_ge(gate_step, 2)
                    dve.tensor_scalar(la["omg"][:, :], la["gate"][:, :], -1.0, 1.0, ALU.mult, ALU.add).then_inc(gate_step, 1)
                    dve.wait_ge(gate_step, 3)
            attention_pass(nc, sem, "la", x1, x2, bank, ident, w["ident_b"], la, B, S, D, AH, ADK, LSEG)

        ffn("f2", 1, x2, out)


_INS = ["L0_attn_x", "L0_attn_Wq", "L0_attn_Wk", "L0_attn_Wv", "L0_attn_betas", "L0_attn_Wo",
        "L0_ffn_q_w", "L0_ffn_q_b", "L0_ffn_k_w", "L0_ffn_k_b", "L0_ffn_v_w", "L0_ffn_v_b",
        "L0_ffn_o_w", "L0_ffn_o_b", "L0_ffn_router_w", "L0_ffn_router_b",
        "L0_ffn_w1", "L0_ffn_b1", "L0_ffn_w2", "L0_ffn_b2"]


def kernel(**inputs):
    import concourse.bacc as bacc
    from concourse.bass_utils import run_bass_kernel_spmd

    nc = bacc.Bacc("TRN2", target_bir_lowering=False, num_devices=1)
    arrays, args = {}, []
    for name in _INS:
        a = np.asarray(inputs[name])
        a = np.ascontiguousarray(a)
        arrays[f"in_{name}"] = a
        args.append(nc.dram_tensor(f"in_{name}", a.shape, mybir.dt.from_np(a.dtype), kind="ExternalInput").ap())
    shape = inputs["L0_attn_x"].shape
    out = nc.dram_tensor("out", shape, F32, kind="ExternalOutput").ap()
    macaron(nc, *args, out)
    result = run_bass_kernel_spmd(nc, [arrays], core_ids=[0])
    return result.results[0]["out"]
```

```python
from contextlib import ExitStack

import numpy as np

import concourse.bass as bass
from concourse import mybir
from concourse.bass import ds

ALU = mybir.AluOpType
ACT = mybir.ActivationFunctionType
F32 = mybir.dt.float32
BF16 = mybir.dt.bfloat16
I32 = mybir.dt.int32
AX = mybir.AxisListType

P = 128
EPS = 1e-5


def wait(eng, sem, value):
    if not (isinstance(value, int) and value <= 0):
        eng.wait_ge(sem, value)


class Steps:

    def __init__(self, eng, sem, unit, per_unit):
        self.eng, self.sem, self.base, self.per_unit, self.n = eng, sem, unit * per_unit, per_unit, 0

    def own(self, instruction):
        instruction.then_inc(self.sem, 1)
        self.n += 1
        self.eng.wait_ge(self.sem, self.base + self.n)

    def end(self):
        assert self.n == self.per_unit, (self.n, self.per_unit)


LN_STEPS = 7


def ln_variance(dve, s, X, stats, mv, ve, T, var_ready, carrier):
    for t in range(T):
        last = dve.bn_stats(stats[:, t, :], X[:, t, :])
    s.own(last)
    dve.memset(carrier, 0.0)
    for t in range(T):
        last = dve.bn_aggr(mv[:, t, :], stats[:, t, :])
    s.own(last)
    dve.tensor_scalar(ve[:, :], mv[:, :, 1], EPS, None, ALU.add).then_inc(var_ready, 1)


def ln_normalise(dve, s, X, HS, mv, ve, sd, rs, T, sd_ready, hs_ready, unit):
    dve.wait_ge(sd_ready, unit + 1)
    s.own(dve.reciprocal(rs[:, :], sd[:, :]))
    s.own(dve.tensor_tensor(sd[:, :], rs[:, :], rs[:, :], ALU.mult))
    s.own(dve.tensor_tensor(sd[:, :], sd[:, :], ve[:, :], ALU.mult))
    s.own(dve.tensor_scalar(sd[:, :], sd[:, :], -0.5, 1.5, ALU.mult, ALU.add))
    s.own(dve.tensor_tensor(rs[:, :], rs[:, :], sd[:, :], ALU.mult))
    for t in range(T):
        last = dve.tensor_scalar(HS[:, t, :], X[:, t, :], mv[:, t, 0:1], rs[:, t:t + 1],
                                 ALU.subtract, ALU.mult)
    last.then_inc(hs_ready, 1)


def region_rows(tokens):
    return tokens + P


def attend_and_route(nc, new_sem, tag, nth, x_in, xr_out, xs, bank, ident, tri, w, scratch, routing, dims,
                     load_w1):
    B, S, D, H, HD, KPH, E, F = dims
    T, DC = S // P, D // P
    QUARTERS = 4
    HQ = H // QUARTERS
    PARTS = 3
    TERMS = [(0, 0), (1, 0), (2, 0), (0, 1), (1, 1), (0, 2)]
    K_MAX = 96
    K_EXP = K_MAX + PARTS
    PV_W = 32
    SC = H * T
    PER_Q = SC // QUARTERS
    GROUPS = SC // HQ
    SCORE_SCALE = 1.0 / float(np.sqrt(KPH))
    OUT_SCALE = 0.5 * 0.3
    START, END = nth * B, (nth + 1) * B
    A_FRONT, A_SCM, A_POST = LN_STEPS + 3, 3 * QUARTERS, T + 22
    PER_UNIT = SC + QUARTERS
    ROWS = 2 * T * 16
    HALF = 2 * len(TERMS) * 16
    q_scr, k_scr, m_scr = scratch
    ROW, CW, start_row = routing["ROW"], routing["CW"], routing["start_row"]

    def max_slot(q):
        return (q + 1) * PER_Q + min(HQ, SC - (q + 1) * PER_Q) + q

    def score_slot(i):
        return i + sum(1 for q in range(QUARTERS) if i >= (q + 1) * PER_Q + HQ)

    with ExitStack() as ctx:
        def sb(name, shape, dt=F32):
            return ctx.enter_context(nc.sbuf_tensor(f"{tag}_{name}", shape, dt))

        def sem(name):
            return new_sem(f"ffn_{name}")

        X, HS, XR = sb("x", [P, T, D]), sb("hs", [P, T, D]), sb("xr", [P, T, D])
        stats = sb("stats", [P, T, 6])
        mv = sb("mv", [P, T, 2])
        ve, sd, rs = sb("ve", [P, T]), sb("sd", [P, T]), sb("rs", [P, T])
        carrier = sb("carrier", [P, 1])
        hsT = sb("hsT", [P, DC, S])
        qf, kf = sb("qf", [P, S]), sb("kf", [P, S])
        qres, kres = sb("qres", [P, S]), sb("kres", [P, S])
        q3, k3 = sb("q3", [P, PARTS, S], BF16), sb("k3", [P, PARTS, S], BF16)
        QS = [sb(f"QS{i}", [K_EXP, H, S], BF16) for i in range(2)]
        KS = [sb(f"KS{i}", [K_EXP, H, S], BF16) for i in range(2)]
        V = [sb(f"V{i}", [P, T, H, PV_W]) for i in range(2)]
        M = sb("M", [P, T, H])
        mres = sb("mres", [P, T, HQ])
        m3 = sb("m3", [P, T, PARTS, HQ], BF16)
        mT = sb("mT", [PARTS * HQ, S], BF16)
        PT = sb("PT", [P, 8, S])
        PVS = sb("PVS", [P, QUARTERS, S])
        rec = sb("rec", [P, T, H])
        AO = sb("AO", [P, T, H * KPH])
        aoT = sb("aoT", [P, S])
        mlaT = sb("mlaT", [P, DC, S])
        NAT = sb("nat", [P, T, D])
        L = sb("L", [P, T, E])
        pr = sb("pr", [P, T, E])
        small = sb("small", [P, T])
        gt, eq = (qres[:, i * T * E * E:(i + 1) * T * E * E].rearrange("p (t e j) -> p t e j", t=T, e=E) for i in range(2))
        rank = sb("rank", [P, T, E])
        comb = sb("comb", [P, T, E])
        chosen = sb("chosen", [P, T, E], BF16)
        hot, picked = sb("hot", [P, T, 2, E]), sb("picked", [P, T, 2, E])
        row, rows_f, weights = sb("row", [P, T, E]), sb("rows_f", [P, T, 2]), sb("weights", [P, T, 2])
        rows_i = sb("rows_i", [P, T, 2], I32)
        pad_f, pad_i = sb("pad_f", [P, E]), sb("pad_i", [P, E], I32)
        zero_rows = sb("zero_rows", [P, D])
        zero, half = sb("zero", [P, 1]), sb("half", [P, T])
        pool_carrier = sb("pool_carrier", [P, 1])

        x_loaded, xr_ready, xr_stored = sem("x_loaded"), sem("xr_ready"), sem("xr_stored")
        var_ready, sd_ready, hs_ready = sem("var_ready"), sem("sd_ready"), sem("hs_ready")
        hsT_filled, hsT_ready = sem("hsT_filled"), sem("hsT_ready")
        q_filled, k_filled, v_filled = sem("q_filled"), sem("k_filled"), sem("v_filled")
        q_ready, k_ready, v_ready = sem("q_ready"), sem("k_ready"), sem("v_ready")
        q3_ready, k3_ready = sem("q3_ready"), sem("k3_ready")
        split_stored, half_loaded = sem("split_stored"), [sem(f"half_loaded{i}") for i in range(2)]
        scm_filled, scm_drained = sem("scm_filled"), sem("scm_drained")
        m3_ready, mT_filled = sem("m3_ready"), sem("mT_filled")
        m_stored, m_loaded = sem("m_stored"), [sem(f"m_loaded{q}") for q in range(QUARTERS)]
        sce_filled, probs_ready = sem("sce_filled"), sem("probs_ready")
        pv_used, pvs_ready = sem("pv_used"), sem("pvs_ready")
        pvT_filled, ao_ready = sem("pvT_filled"), sem("ao_ready")
        aoT_filled, aoT_ready = sem("aoT_filled"), sem("aoT_ready")
        mla_filled, mlaT_ready = sem("mla_filled"), sem("mlaT_ready")
        nat_filled, nat_ready = sem("nat_filled"), sem("nat_ready")
        router_filled, logits_ready, ex_ready = sem("router_filled"), sem("logits_ready"), sem("ex_ready")
        chosen_ready, prefix_filled, rows_ready, rows_stored = (
            sem("chosen_ready"), sem("prefix_filled"), sem("rows_ready"), sem("rows_stored"))
        pads_ready, pads_stored = sem("pads_ready"), sem("pads_stored")
        dve_front, dve_scm, dve_post, pool_front = sem("dve_front"), sem("dve_scm"), sem("dve_post"), sem("pool_front")
        xr_half = sem("xr_half")
        dve_pads, carried, rows_out = sem("dve_pads"), sem("carried"), sem("rows_out")
        init = sem("init")
        N_INIT = 9
        INIT = N_INIT * (nth + 1)

        SCE, SIDE, PVB, SCM = bank[0:2], bank[2:4], bank[4], bank[5:8]

        def run_turns(eng, turn):
            turn(None, None, START, None)
            turn(None, START, START + 1, None)
            turn(START, START + 1, START + 2, None)
            full = B - 3
            with eng.Fori(0, full // 2) as k:
                for odd in range(2):
                    b = k * 2 + (START + 1 + odd)
                    turn(b, b + 1, b + 2, b - 1, (START + 1 + odd) % 2)
            for b in range(START + 1 + full // 2 * 2, END + 1):
                turn(b if b < END else None, b + 1 if b + 1 < END else None,
                     b + 2 if b + 2 < END else None, b - 1)

        def parity(unit, offset, par):
            if par is not None:
                return (par + offset) % 2
            return unit % 2 if unit is not None else None

        block = ctx.enter_context(nc.Block())

        @block.sync
        def _(sp):
            def load(a):
                sp.dma_start(X[:, :, :], x_in[a - START].rearrange("(t p) d -> p t d", p=P)).then_inc(x_loaded, 16)

            def stack_half(a, half, par, free):
                if free is not None:
                    wait(sp, sce_filled, free)
                if half == 0:
                    sp.wait_ge(split_stored, a * 32 + 32)
                heads = slice(half * H // 2, (half + 1) * H // 2)
                for n, (i, j) in enumerate(TERMS):
                    at = slice(n * KPH, (n + 1) * KPH)
                    for to, source in ((QS[par], q_scr[i]), (KS[par], k_scr[j])):
                        sp.dma_start(to[at, heads, :], source.rearrange("(h k) t -> k h t", k=KPH)[:, heads, :]) \
                          .then_inc(half_loaded[half], 16)

            def maxima(a, q, par):
                sp.wait_ge(scm_drained, a * PER_UNIT + max_slot(q) + 1)
                sp.dma_start(m_scr[q], mT[:, :]).then_inc(m_stored, 16)
                sp.wait_ge(m_stored, (a * QUARTERS + q) * 16 + 16)
                sp.dma_start(QS[par][K_MAX:K_EXP, q * HQ:(q + 1) * HQ, :],
                             m_scr[q].rearrange("(c h) t -> c h t", h=HQ)).then_inc(m_loaded[q], 16)

            def turn(e, s, f, p, par=None):
                par_s, par_f = parity(s, 1, par), parity(f, 0, par)
                if e is None and s is not None:
                    load_w1(sp)
                if f is not None:
                    sp.wait_ge(xr_ready, f + 1)
                    sp.dma_start(xr_out[f - START].rearrange("(t p) d -> p t d", p=P), XR[:, :, :]).then_inc(xr_stored, 16)
                    wait(sp, half_loaded[1], f * HALF)
                    if not isinstance(f, int) or f + 1 < END:
                        load(f + 1)
                    sp.wait_ge(q3_ready, f + 1)
                    sp.dma_start(q_scr.rearrange("c r t -> r c t"), q3[:, :, :]).then_inc(split_stored, 16)
                    sp.wait_ge(k3_ready, f + 1)
                    sp.dma_start(k_scr.rearrange("c r t -> r c t"), k3[:, :, :]).then_inc(split_stored, 16)
                if s is not None:
                    maxima(s, 0, par_s)
                if f is not None:
                    if e is None:
                        sp.wait_ge(init, INIT if s is not None else INIT - 3)
                    stack_half(f, 0, par_f, e * SC + SC // 2 if e is not None else None)
                if s is not None:
                    for q in range(1, QUARTERS):
                        maxima(s, q, par_s)
                if f is not None:
                    stack_half(f, 1, par_f, (e + 1) * SC if e is not None else None)

            load(START)
            run_turns(sp, turn)
            sp.wait_ge(xr_stored, 16 * END)
            sp.wait_ge(m_stored, 16 * QUARTERS * END)
            sp.wait_ge(split_stored, 32 * END)
            sp.wait_ge(rows_stored, ROWS * END)
            sp.wait_ge(pads_stored, 16 * E * (nth + 1))

        @block.gpsimd
        def _(pool):
            pool.memset(half[:, :], 0.5).then_inc(init, 1)
            pool.memset(zero[:, :], 0.0).then_inc(init, 1)
            pool.memset(zero_rows[:, :], 0.0).then_inc(init, 1)

            def prepare_stacks(i, done):
                pool.memset(QS[i][0:K_MAX, :, :], 0.0).then_inc(init, 1)
                pool.memset(KS[i][0:K_MAX, :, :], 0.0).then_inc(init, 1)
                pool.wait_ge(init, INIT - N_INIT + done + 2)
                pool.memset(KS[i][K_MAX:K_EXP, :, :], 1.0).then_inc(init, 1)
                pool.wait_ge(init, INIT - N_INIT + done + 3)

            prepare_stacks(0, 3)
            if nth == 0:
                pool.memset(pool_carrier[:, :], 0.0).then_inc(carried, 1)
                pool.memset(NAT[:, 0, 0:1], 0.0).then_inc(rows_out, 1)
            nothing = zero[:, :].to_broadcast([P, S])

            def residual(a):
                pool.wait_ge(hs_ready, a + 1)
                wait(pool, xr_stored, a * 16)
                pool.tensor_tensor(XR[:, :, :], HS[:, :, :], half[:, :].unsqueeze(2).to_broadcast([P, T, D]),
                                   ALU.mult).then_inc(xr_half, 1)
                pool.wait_ge(xr_half, a + 1)
                pool.tensor_tensor(XR[:, :, :], XR[:, :, :], X[:, :, :], ALU.add).then_inc(xr_ready, 1)

            def split_k(a):
                s = Steps(pool, pool_front, a, 3)
                pool.wait_ge(k_ready, a + 1)
                wait(pool, split_stored, a * 32)
                s.own(pool.tensor_tensor(k3[:, 0, :], kf[:, :], nothing, ALU.add))
                s.own(pool.tensor_tensor(kres[:, :], kf[:, :], k3[:, 0, :], ALU.subtract))
                s.own(pool.tensor_tensor(k3[:, 1, :], kres[:, :], nothing, ALU.add))
                pool.tensor_tensor(k3[:, 2, :], kres[:, :], k3[:, 1, :], ALU.subtract).then_inc(k3_ready, 1)
                s.end()

            def send_rows(a):
                pool.wait_ge(nat_ready, (a + 1) * 2)
                pool.wait_ge(rows_ready, a + 1)
                pool.wait_ge(rows_out, a + 1)
                pool.tensor_tensor(pool_carrier[:, :], zero[:, :], zero[:, :], ALU.add).then_inc(carried, 1)
                for t in range(T):
                    for n in range(2):
                        pool.indirect_dma_start(
                            out=xs, out_offset=bass.IndirectOffsetOnAxis(ap=rows_i[:, t, n:n + 1], axis=0),
                            in_=NAT[:, t, :], in_offset=None).then_inc(rows_stored, 16)
                pool.wait_ge(carried, a + 2)
                pool.wait_ge(rows_stored, (a + 1) * ROWS)
                pool.tensor_tensor(pool_carrier[:, :], zero[:, :], zero[:, :], ALU.add).then_inc(rows_out, 1)

            def turn(e, s, f, p, par=None):
                if f is not None:
                    residual(f)
                    split_k(f)
                if p is not None:
                    send_rows(p)
                if s is None and p is None:
                    prepare_stacks(1, 6)

            run_turns(pool, turn)
            pool.wait_ge(pads_ready, nth + 1)
            for e in range(E):
                pool.indirect_dma_start(
                    out=xs, out_offset=bass.IndirectOffsetOnAxis(ap=pad_i[:, e:e + 1], axis=0),
                    in_=zero_rows[:, :], in_offset=None).then_inc(pads_stored, 16)

        @block.scalar
        def _(act):
            def root(a):
                act.wait_ge(var_ready, a + 1)
                act.activation(sd[:, :], ve[:, :], ACT.Sqrt).then_inc(sd_ready, 1)

            def evacuate_hsT(a):
                for c in range(DC):
                    act.wait_ge(hsT_filled, a * DC + c + 1)
                    act.activation(hsT[:, c, :], SIDE[c], ACT.Copy).then_inc(hsT_ready, 1)

            def evacuate_qk(a):
                wait(act, q3_ready, a)
                act.wait_ge(q_filled, a + 1)
                act.activation(qf[:, :], SIDE[0][:, :], ACT.Identity, bias=w["q_bs"][:, 0:1],
                               scale=SCORE_SCALE).then_inc(q_ready, 1)
                wait(act, k3_ready, a)
                act.wait_ge(k_filled, a + 1)
                act.activation(kf[:, :], SIDE[1][:, :], ACT.Identity, bias=w["k_b"][:, 0:1]).then_inc(k_ready, 1)

            def evacuate_aoT(a):
                act.wait_ge(aoT_filled, a + 1)
                act.activation(aoT[:, :], SIDE[0][:, :], ACT.Copy).then_inc(aoT_ready, 1)

            def evacuate_mla(a):
                for c in range(DC):
                    act.wait_ge(mla_filled, a * DC + c + 1)
                    act.activation(mlaT[:, c, :], SIDE[1 - c][:, :], ACT.Identity,
                                   bias=w["o_b"][:, c:c + 1]).then_inc(mlaT_ready, 1)

            def router_exp(a):
                act.wait_ge(logits_ready, a + 1)
                act.activation(L[:, :, :], L[:, :, :], ACT.Exp).then_inc(ex_ready, 1)

            def pv_out(a, q):
                if q == 0:
                    wait(act, pvT_filled, a * T)
                act.wait_ge(pv_used, a * SC + (q + 1) * PER_Q)
                act.activation(PVS[:, q, :], PVB[:, :], ACT.Copy).then_inc(pvs_ready, 1)

            FRONT = {0: root, 4: evacuate_hsT, 5: evacuate_qk}
            POST = {3: evacuate_aoT, 7: evacuate_mla, 9: router_exp}

            def turn(e, s, f, p, par=None):
                for g in range(GROUPS):
                    if e is not None:
                        for i in range(g * HQ, (g + 1) * HQ):
                            act.wait_ge(sce_filled, e * SC + i + 1)
                            wait(act, pv_used, e * SC + i - 7)
                            act.activation(PT[:, i % 8, :], SCE[i % 2][:, :], ACT.Exp).then_inc(probs_ready, 1)
                    if f is not None and g in FRONT:
                        FRONT[g](f)
                    if p is not None and g in POST:
                        POST[g](p)
                    if e is not None and g % HQ == 0 and g >= HQ:
                        pv_out(e, g // HQ - 1)
                if e is not None:
                    pv_out(e, QUARTERS - 1)

            run_turns(act, turn)

        @block.vector
        def _(dve):
            def evacuate_v(a, par, n):
                if n == 0:
                    wait(dve, pv_used, (a - 1) * SC)
                    dve.wait_ge(v_filled, a + 1)
                for t in (2 * n, 2 * n + 1):
                    last = dve.tensor_tensor(V[par][:, t, :, 0:KPH],
                                             SIDE[1][:, t * P:(t + 1) * P].rearrange("p (h k) -> p h k", k=KPH),
                                             w["v_b"][:, :].rearrange("p (h k) -> p h k", k=KPH), ALU.add)
                if n == 1:
                    last.then_inc(v_ready, 1)

            def variance(a, s, n):
                if n == 0:
                    dve.wait_ge(x_loaded, a * 16 + 16)
                    ln_variance(dve, s, X, stats, mv, ve, T, var_ready, carrier[:, :])

            def normalise(a, s, n):
                if n == 0:
                    ln_normalise(dve, s, X, HS, mv, ve, sd, rs, T, sd_ready, hs_ready, a)

            def split_q(a, s, n):
                if n == 0:
                    dve.wait_ge(q_ready, a + 1)
                    wait(dve, split_stored, a * 32)
                    s.own(dve.tensor_copy(q3[:, 0, :], qf[:, :]))
                if n == 1:
                    s.own(dve.tensor_tensor(qres[:, :], qf[:, :], q3[:, 0, :], ALU.subtract))
                if n == 2:
                    s.own(dve.tensor_copy(q3[:, 1, :], qres[:, :]))
                if n == 3:
                    dve.tensor_tensor(q3[:, 2, :], qres[:, :], q3[:, 1, :], ALU.subtract).then_inc(q3_ready, 1)

            def maximum(a, i):
                n = score_slot(i)
                dve.wait_ge(scm_filled, a * SC + i + 1)
                h, t = i // T, i % T
                dve.tensor_reduce(M[:, t, h:h + 1], SCM[n % 3][:, :], AX.X, ALU.max).then_inc(scm_drained, 1)

            def split_maxima(a, q, s):
                mq = M[:, :, q * HQ:(q + 1) * HQ]
                dve.wait_ge(scm_drained, a * PER_UNIT + score_slot((q + 1) * PER_Q - 1) + 1)
                wait(dve, mT_filled, a * QUARTERS + q)
                s.own(dve.tensor_scalar(m3[:, :, 0, :], mq, -1.0, None, ALU.mult))
                s.own(dve.scalar_tensor_tensor(mres[:, :, :], mq, -1.0, m3[:, :, 0, :], ALU.mult, ALU.subtract))
                s.own(dve.tensor_copy(m3[:, :, 1, :], mres[:, :, :]))
                dve.tensor_tensor(m3[:, :, 2, :], mres[:, :, :], m3[:, :, 1, :], ALU.subtract).then_inc(m3_ready, 1)

            def evacuate_mT(a, q):
                dve.wait_ge(mT_filled, a * QUARTERS + q + 1)
                wait(dve, m_stored, (a * QUARTERS + q) * 16)
                dve.tensor_copy(mT[:, :], SCM[max_slot(q) % 3].bitcast(BF16)[0:PARTS * HQ, 0:S]).then_inc(scm_drained, 1)

            def divide(ts):
                def piece(a, s, n):
                    for t in ts[n - 2:n - 1] if n >= 2 else ():
                        dve.wait_ge(pvT_filled, a * T + t + 1)
                        out = SIDE[t % 2][:, :].rearrange("p (h c) -> p h c", c=PV_W)
                        s.own(dve.reciprocal(rec[:, t, :], out[:, :, KPH]))
                        dve.tensor_tensor(AO[:, t, :].rearrange("p (h k) -> p h k", k=KPH), out[:, :, 0:KPH],
                                          rec[:, t, :].unsqueeze(2).to_broadcast([P, H, KPH]),
                                          ALU.mult).then_inc(ao_ready, 1)
                return piece

            def natural(a, s, step):
                if step == 2:
                    dve.wait_ge(rows_out, a + 1)
                for n in (step - 2,) if step >= 2 else ():
                    dve.wait_ge(nat_filled, a * 2 + n + 1)
                    dve.tensor_tensor(NAT[:, 2 * n:2 * n + 2, :], SIDE[1 - n][:, :].rearrange("p (t d) -> p t d", d=D),
                                      w["o_b_row"][:, :].unsqueeze(1).to_broadcast([P, 2, D]),
                                      ALU.add).then_inc(nat_ready, 1)

            per_token = small[:, :].unsqueeze(2).to_broadcast([P, T, E])

            def logits(a, s, n):
                if n < HQ - 1:
                    return
                dve.wait_ge(router_filled, a + 1)
                s.own(dve.tensor_tensor(L[:, :, :], SIDE[1][:, 0:T * E].rearrange("p (t e) -> p t e", e=E),
                                        w["router_b"][:, :].unsqueeze(1).to_broadcast([P, T, E]), ALU.add))
                s.own(dve.tensor_reduce(small[:, :], L[:, :, :], AX.X, ALU.max))
                dve.tensor_tensor(L[:, :, :], L[:, :, :], per_token, ALU.subtract).then_inc(logits_ready, 1)

            def rank_experts(a, s, n):
                if n == 0:
                    return
                if n == 1:
                    dve.wait_ge(ex_ready, a + 1)
                    s.own(dve.tensor_reduce(small[:, :], L[:, :, :], AX.X, ALU.add))
                    s.own(dve.reciprocal(small[:, :], small[:, :]))
                    s.own(dve.tensor_tensor(pr[:, :, :], L[:, :, :], per_token, ALU.mult))
                    return
                other = pr[:, :, :].unsqueeze(2).to_broadcast([P, T, E, E])
                this = pr[:, :, :].unsqueeze(3).to_broadcast([P, T, E, E])
                if n == 2:
                    dve.tensor_tensor(gt[:, :, :, :], other, this, ALU.is_gt)
                    s.own(dve.tensor_tensor(eq[:, :, :, :], other, this, ALU.is_equal))
                    s.own(dve.tensor_tensor(eq[:, :, :, :], eq[:, :, :, :],
                                            tri[:, :, :].unsqueeze(1).to_broadcast([P, T, E, E]), ALU.mult))
                    return
                s.own(dve.tensor_tensor(gt[:, :, :, :], gt[:, :, :, :], eq[:, :, :, :], ALU.add))
                s.own(dve.tensor_reduce(rank[:, :, :], gt[:, :, :, :], AX.X, ALU.add))
                dve.tensor_scalar(chosen[:, :, :], rank[:, :, :], 1.5, None, ALU.is_lt).then_inc(chosen_ready, 1)
                for n in range(2):
                    dve.tensor_scalar(hot[:, :, n, :], rank[:, :, :], float(n), None, ALU.is_equal)

            def weigh_experts(a, s, n):
                if n == 0:
                    s.own(dve.scalar_tensor_tensor(comb[:, :, :], rank[:, :, :], 1.5, pr[:, :, :], ALU.is_lt, ALU.mult))
                    s.own(dve.tensor_reduce(small[:, :], comb[:, :, :], AX.X, ALU.add))
                if n == 1:
                    s.own(dve.tensor_scalar(small[:, :], small[:, :], 1e-8, None, ALU.add))
                    s.own(dve.reciprocal(small[:, :], small[:, :]))
                if n == 2:
                    s.own(dve.tensor_tensor(comb[:, :, :], comb[:, :, :], per_token, ALU.mult))
                if n < HQ - 1:
                    return
                s.own(dve.tensor_tensor(picked[:, :, :, :], hot[:, :, :, :],
                                        comb[:, :, :].unsqueeze(2).to_broadcast([P, T, 2, E]), ALU.mult))
                s.own(dve.tensor_reduce(weights[:, :, :], picked[:, :, :, :], AX.X, ALU.add))
                s.own(dve.tensor_scalar(CW[:, ds((a - START) * T, T), :], weights[:, :, :], OUT_SCALE, None, ALU.mult))

            def place(a, s, n):
                if n == 0:
                    dve.wait_ge(prefix_filled, a + 1)
                    prefix = SIDE[0][:, 0:T * E].rearrange("p (t e) -> p t e", e=E)
                    s.own(dve.tensor_tensor(row[:, :, :], prefix,
                                            start_row[:, :].unsqueeze(1).to_broadcast([P, T, E]), ALU.add))
                    s.own(dve.tensor_tensor(start_row[:, :], start_row[:, :], SIDE[0][:, T * E:(T + 1) * E], ALU.add))
                if n != 2:
                    return
                s.own(dve.tensor_tensor(picked[:, :, :, :], hot[:, :, :, :],
                                        row[:, :, :].unsqueeze(2).to_broadcast([P, T, 2, E]), ALU.mult))
                s.own(dve.tensor_reduce(rows_f[:, :, :], picked[:, :, :, :], AX.X, ALU.add))
                s.own(dve.tensor_scalar(ROW[:, ds((a - START) * T, T), :], rows_f[:, :, :], 0.0, None, ALU.add))
                dve.tensor_copy(rows_i[:, :, :], rows_f[:, :, :]).then_inc(rows_ready, 1)

            FRONT = {0: variance, 1: normalise, 6: split_q}
            POST = {1: divide((0, 1)), 2: divide((2, 3)), 8: natural, 9: logits, 10: rank_experts,
                    11: weigh_experts, 13: place}

            def turn(e, s, f, p, par=None):
                s_scm = Steps(dve, dve_scm, s, A_SCM) if s is not None else None
                s_front = Steps(dve, dve_front, f, A_FRONT) if f is not None else None
                s_post = Steps(dve, dve_post, p, A_POST) if p is not None else None
                for g in range(GROUPS):
                    for i in range(g * HQ, (g + 1) * HQ):
                        if s is not None:
                            maximum(s, i)
                        if s is not None and i < 2:
                            evacuate_v(s, parity(s, 1, par), i)
                        if f is not None and g in FRONT:
                            FRONT[g](f, s_front, i % HQ)
                        if p is not None and g in POST:
                            POST[g](p, s_post, i % HQ)
                    if s is not None:
                        if g % HQ == 0 and g >= 1:
                            evacuate_mT(s, g // HQ - 1)
                        if g % HQ == HQ - 1:
                            split_maxima(s, g // HQ, s_scm)
                if s is not None:
                    evacuate_mT(s, QUARTERS - 1)
                for steps in (s_scm, s_front, s_post):
                    if steps is not None:
                        steps.end()

            s = Steps(dve, dve_pads, nth, 4)
            for i in range(2):
                last = dve.memset(V[i][:, :, :, :], 0.0)
            s.own(last)
            for i in range(2):
                last = dve.memset(V[i][:, :, :, KPH:KPH + 1], 1.0)
            s.own(last)
            s.own(dve.tensor_copy(start_row[:, :], w["region"][:, :]))
            run_turns(dve, turn)
            s.own(dve.tensor_tensor(pad_f[:, :], start_row[:, :], w["partition"][:, 0:1].to_broadcast([P, E]), ALU.add))
            dve.tensor_copy(pad_i[:, :], pad_f[:, :]).then_inc(pads_ready, 1)
            s.end()

        @block.tensor
        def _(pe):
            def turn_hs(a, n):
                c, first = n // 2, n % 2 * 2
                if n == 0:
                    pe.wait_ge(hs_ready, a + 1)
                    wait(pe, v_ready, a)
                for t in (first, first + 1):
                    last = pe.transpose(SIDE[c][:, t * P:(t + 1) * P], HS[:, t, c * P:(c + 1) * P], ident[:, :])
                if first:
                    last.then_inc(hsT_filled, 1)

            def project_qk(a, n):
                if n == 0:
                    pe.wait_ge(hsT_ready, (a + 1) * DC)
                filled, weight = ((q_filled, w["q_w"]), (k_filled, w["k_w"]))[n // 2]
                c = n % 2
                last = pe.matmul(SIDE[n // 2][:, :], weight[:, c, :], hsT[:, c, :], start=(c == 0), stop=(c == DC - 1))
                if c == DC - 1:
                    last.then_inc(filled, 1)

            def release_front(a, n):
                if n == 0:
                    pe.wait_ge(q_ready, a + 1)
                    pe.wait_ge(k_ready, a + 1)

            def project_v(a, t):
                for c in range(DC):
                    last = pe.matmul(SIDE[1][:, t * P:(t + 1) * P], hsT[:, c, t * P:(t + 1) * P],
                                     w["v_w"][:, c, :], start=(c == 0), stop=(c == DC - 1))
                if t == T - 1:
                    last.then_inc(v_filled, 1)

            def turn_pv(ts):
                def piece(a, n):
                    t, first = ts[n // 2], n % 2 * 2
                    if n == 0:
                        pe.wait_ge(pvs_ready, (a + 1) * QUARTERS)
                    if t == 1 and first == 0:
                        pe.wait_ge(v_ready, min(a + 3, END) if isinstance(a, int) else a + 3)
                    if t >= 2 and first == 0:
                        pe.wait_ge(ao_ready, a * T + t - 1)
                    for q in (first, first + 1):
                        last = pe.transpose(SIDE[t % 2][:, q * P:(q + 1) * P], PVS[:, q, t * P:(t + 1) * P],
                                            ident[:, :])
                    if first:
                        last.then_inc(pvT_filled, 1)
                return piece

            def turn_ao(a, t):
                if t == 0:
                    pe.wait_ge(ao_ready, (a + 1) * T)
                last = pe.transpose(SIDE[0][:, t * P:(t + 1) * P], AO[:, t, :], ident[:, :])
                if t == T - 1:
                    last.then_inc(aoT_filled, 1)

            def release_ao(a, n):
                if n == 0:
                    pe.wait_ge(aoT_ready, a + 1)

            def project_out(a, c):
                if c == 0:
                    pe.wait_ge(aoT_ready, a + 1)
                if c < DC:
                    pe.matmul(SIDE[1 - c][:, :], w["o_w"][:, c * P:(c + 1) * P], aoT[:, :],
                              start=True, stop=True).then_inc(mla_filled, 1)

            def natural(a, t):
                if t % 2 == 0:
                    pe.wait_ge(mlaT_ready, a * DC + t // 2 + 1)
                last = pe.matmul(SIDE[1 - t // 2][:, (t % 2) * D:(t % 2 + 1) * D], aoT[:, t * P:(t + 1) * P],
                                 w["o_w"][:, :], start=True, stop=True)
                if t % 2:
                    last.then_inc(nat_filled, 1)

            def router(a, t):
                if t == 0:
                    pe.wait_ge(nat_ready, a * 2 + 1)
                for c in range(DC):
                    last = pe.matmul(SIDE[1][:, t * E:(t + 1) * E], mlaT[:, c, t * P:(t + 1) * P],
                                     w["router_w"][:, c, :], start=(c == 0), stop=(c == DC - 1))
                if t == T - 1:
                    last.then_inc(router_filled, 1)

            def prefix(a, n):
                if n == 0:
                    pe.wait_ge(nat_ready, a * 2 + 2)
                    pe.wait_ge(chosen_ready, a + 1)
                for t in (0, 1) if n == 0 else (n + 1,):
                    to = SIDE[0][:, t * E:(t + 1) * E]
                    for earlier in range(t):
                        last = pe.matmul(to, w["ones_b"][:, :], chosen[:, earlier, :], start=(earlier == 0),
                                         stop=(t == T and earlier == T - 1))
                    if t < T:
                        last = pe.matmul(to, w["before_b"][:, :], chosen[:, t, :], start=(t == 0), stop=True)
                if n == HQ - 1:
                    last.then_inc(prefix_filled, 1)

            def release_post(a, n):
                if n == 0:
                    pe.wait_ge(logits_ready, a + 1)
                    pe.wait_ge(rows_ready, a + 1)

            FRONT = {4: turn_hs, 5: project_qk, 6: release_front, 15: project_v}
            POST = {1: turn_pv((0, 1)), 2: turn_pv((2, 3)), 3: turn_ao, 4: release_ao, 7: project_out,
                    8: natural, 9: router, 12: prefix, 14: release_post}

            def score_for_max(a, i, par):
                n = score_slot(i)
                if i % (SC // 2) == 0:
                    pe.wait_ge(half_loaded[i // (SC // 2)], (a + 1) * HALF)
                wait(pe, scm_drained, a * PER_UNIT + (n - 2 if n >= 3 else 0))
                h, t = i // T, i % T
                pe.matmul(SCM[n % 3][:, :], QS[par][0:K_MAX, h, t * P:(t + 1) * P], KS[par][0:K_MAX, h, :],
                          start=True, stop=True).then_inc(scm_filled, 1)

            def turn_maxima(a, q):
                n = max_slot(q)
                pe.wait_ge(scm_drained, a * PER_UNIT + n - 2)
                pe.wait_ge(m3_ready, a * QUARTERS + q + 1)
                rows = SCM[n % 3].bitcast(BF16)
                for t in range(T):
                    last = pe.transpose(rows[0:PARTS * HQ, t * P:(t + 1) * P],
                                        m3[:, t, :, :].rearrange("p c h -> p (c h)"), w["ident_b"][:, :])
                last.then_inc(mT_filled, 1)

            def score(a, i, par):
                q, j = divmod(i, PER_Q)
                t, h = j // HQ, q * HQ + j % HQ
                if j == 0:
                    pe.wait_ge(m_loaded[q], a * 16 + 16)
                wait(pe, probs_ready, a * SC + i - 1)
                pe.matmul(SCE[i % 2][:, :], KS[par][0:K_EXP, h, t * P:(t + 1) * P], QS[par][0:K_EXP, h, :],
                          start=True, stop=True).then_inc(sce_filled, 1)

            def weigh(a, i, par):
                q, j = divmod(i, PER_Q)
                t, hq = j // HQ, j % HQ
                if j == 0:
                    wait(pe, pvs_ready, a * QUARTERS + q)
                pe.wait_ge(probs_ready, a * SC + i + 1)
                pe.matmul(PVB[hq * PV_W:(hq + 1) * PV_W, :], V[par][:, t, q * HQ + hq, :],
                          PT[:, i % 8, :], start=(t == 0), stop=(t == T - 1)).then_inc(pv_used, 1)

            def turn(e, s, f, p, par=None):
                par_e, par_s = parity(e, 0, par), parity(s, 1, par)
                if e is not None:
                    pe.wait_ge(v_ready, e + 1)
                for g in range(GROUPS):
                    for i in range(g * HQ, (g + 1) * HQ):
                        if e is not None:
                            score(e, i, par_e)
                        if s is not None:
                            score_for_max(s, i, par_s)
                        if p is not None and g in POST:
                            POST[g](p, i % HQ)
                        if f is not None and g in FRONT:
                            FRONT[g](f, i % HQ)
                    if s is not None and g % HQ == 0 and g >= 1:
                        turn_maxima(s, g // HQ - 1)
                    if e is not None and g >= 1:
                        for i in range((g - 1) * HQ, g * HQ):
                            weigh(e, i, par_e)
                if e is not None:
                    for i in range((GROUPS - 1) * HQ, GROUPS * HQ):
                        weigh(e, i, par_e)
                if s is not None:
                    turn_maxima(s, QUARTERS - 1)

            run_turns(pe, turn)


def tile_tables(nc, new_sem, tag, nth, w, tri, routing, tokens, E, NT, load):
    REG = region_rows(tokens)
    start_row, tables, ROW, IDX = (routing[n] for n in ("start_row", "tables", "ROW", "IDX"))
    RUNGS = tokens // P + 1
    PAIRS = 2 * tokens // P

    with ExitStack() as ctx:
        def sb(name, shape, dt=F32):
            return ctx.enter_context(nc.sbuf_tensor(f"{tag}_{name}", shape, dt))

        count, tiles, ends = sb("count", [P, E]), sb("tiles", [P, E]), sb("ends", [P, E])
        above = sb("above", [P, E, RUNGS])
        low, lower = sb("low", [P, E, E]), sb("total", [P, 1])
        jj = sb("jj", [P, NT])
        unused, less = sb("unused", [P, PAIRS, E - 1]), sb("less", [P, PAIRS])
        past, work = sb("past", [P, NT, E]), sb("work", [P, NT, E])
        expert, first, at = sb("expert", [P, NT]), sb("first", [P, NT]), sb("at", [P, NT])
        step = new_sem("tables_step")
        block = ctx.enter_context(nc.Block())

        @block.sync
        def _(sp):
            load(sp)

        @block.vector
        def _(dve):
            s = Steps(dve, step, nth, 21)
            own = s.own
            j = w["tile"][:, :]
            own(dve.tensor_tensor(count[:, :], start_row[:, :], w["region"][:, :], ALU.subtract))
            own(dve.tensor_tensor(above[:, :, :], count[:, :].unsqueeze(2).to_broadcast([P, E, RUNGS]),
                                  w["rung"][:, :].unsqueeze(1).to_broadcast([P, E, RUNGS]), ALU.is_gt))
            own(dve.tensor_reduce(tiles[:, :], above[:, :, :], AX.X, ALU.add))
            own(dve.tensor_tensor(low[:, :, :], tri[:, :, :], tiles[:, :].unsqueeze(1).to_broadcast([P, E, E]), ALU.mult))
            own(dve.tensor_reduce(ends[:, :], low[:, :, :], AX.X, ALU.add))
            own(dve.tensor_tensor(ends[:, :], ends[:, :], tiles[:, :], ALU.add))
            own(dve.tensor_scalar(lower[:, :], ends[:, E - 1:E], -1.0, None, ALU.add))
            own(dve.tensor_tensor(jj[:, :], j, lower[:, 0:1].to_broadcast([P, NT]), ALU.min))
            own(dve.tensor_tensor(past[:, :, :], jj[:, :].unsqueeze(2).to_broadcast([P, NT, E]),
                                  ends[:, :].unsqueeze(1).to_broadcast([P, NT, E]), ALU.is_ge))
            own(dve.tensor_reduce(expert[:, :], past[:, :, :], AX.X, ALU.add))
            own(dve.tensor_tensor(work[:, :, :], past[:, :, :],
                                  tiles[:, :].unsqueeze(1).to_broadcast([P, NT, E]), ALU.mult))
            own(dve.tensor_reduce(first[:, :], work[:, :, :], AX.X, ALU.add))
            own(dve.tensor_tensor(first[:, :], jj[:, :], first[:, :], ALU.subtract))
            own(dve.tensor_scalar(at[:, :], expert[:, :], float(REG), None, ALU.mult))
            own(dve.scalar_tensor_tensor(at[:, :], first[:, :], float(P), at[:, :], ALU.mult, ALU.add))
            dve.tensor_copy(tables[:, 0, :], expert[:, :])
            own(dve.tensor_copy(tables[:, 1, :], at[:, :]))
            own(dve.tensor_scalar(tiles[:, :], tiles[:, :], -float(P), float(REG), ALU.mult, ALU.add))
            own(dve.tensor_tensor(unused[:, :, :], ROW[:, :, :].rearrange("p t n -> p (t n)").unsqueeze(2).to_broadcast([P, PAIRS, E - 1]),
                                  w["region"][:, 1:E].unsqueeze(1).to_broadcast([P, PAIRS, E - 1]), ALU.is_ge))
            own(dve.tensor_tensor(unused[:, :, :], unused[:, :, :],
                                  tiles[:, 0:E - 1].unsqueeze(1).to_broadcast([P, PAIRS, E - 1]), ALU.mult))
            own(dve.tensor_reduce(less[:, :], unused[:, :, :], AX.X, ALU.add))
            own(dve.tensor_tensor(IDX[:, :, :].rearrange("p t n -> p (t n)"), ROW[:, :, :].rearrange("p t n -> p (t n)"),
                                  less[:, :], ALU.subtract))
            s.end()


def experts(nc, new_sem, tag, nth, xs, ys, bank, ident, w, loaded, load_rest, routing, dims, NT):
    B, S, D, H, HD, KPH, E, F = dims
    DC, FC = D // P, F // P
    tables = routing["tables"]
    w1_loaded, w2_loaded, b_loaded = loaded
    BASE = nth * NT
    STAGES = 4

    with ExitStack() as ctx:
        def sb(name, shape, dt=F32):
            return ctx.enter_context(nc.sbuf_tensor(f"{tag}_{name}", shape, dt))

        def sem(name):
            return new_sem(f"moe_{name}")

        XN, XT = sb("xn", [P, 2, D]), sb("xT", [P, 2, DC, P])
        Hb, G, GT = sb("hb", [P, 2, F]), sb("g", [P, 2, F]), sb("gT", [P, 2, FC, P])
        Y = sb("y", [P, 2, D])

        x_loaded, xT_filled, xT_ready = [sem("x_loaded0"), sem("x_loaded1")], sem("xT_filled"), sem("xT_ready")
        h_filled, h_ready, g_ready = sem("h_filled"), sem("h_ready"), sem("g_ready")
        gT_filled, gT_ready, o_filled, y_ready = sem("gT_filled"), sem("gT_ready"), sem("o_filled"), sem("y_ready")
        y_stored = [sem("y_stored0"), sem("y_stored1")]
        BEFORE = [nth * ((NT + 1) // 2), nth * (NT // 2)]

        XB, HB, GB, OB = bank[0:2], bank[2:4], bank[4:6], bank[6:8]

        def run_slots(eng, slot):
            peeled = STAGES + 1
            for s in range(peeled):
                slot(s, 0)
            n = (NT - peeled) // 2
            with eng.Fori(0, n) as k:
                for odd in range(2):
                    slot(peeled + odd, k)
            for s in range(peeled + 2 * n, NT + STAGES - 1):
                slot(s, 0)

        def live(s, k, stage):
            return 0 <= s - stage < NT or not isinstance(k, int)

        block = ctx.enter_context(nc.Block())

        @block.sync
        def _(sp):
            def load(s, k):
                buf, j = s % 2, k * 2 + s
                at = sp.value_load(tables[0:1, 1, ds(j, 1)], min_val=0, max_val=xs.shape[0] - P)
                wait(sp, xT_filled, j + (BASE - 1))
                sp.dma_start(XN[:, buf, :], xs[ds(at, P), :]).then_inc(x_loaded[buf], 16)

            def slot(s, k):
                if live(s, k, 0):
                    load(s, k)
                if s == 1:
                    load_rest(sp)

            run_slots(sp, slot)
            for buf in range(2):
                sp.wait_ge(y_stored[buf], 16 * (BEFORE[buf] + (NT + 1 - buf) // 2))

        @block.scalar
        def _(act):
            def slot(s, k):
                if live(s, k, 1):
                    buf, j = (s - 1) % 2, k * 2 + (s - 1)
                    act.wait_ge(h_ready, j + (BASE + 1))
                    wait(act, gT_filled, j + (BASE - 1))
                    act.activation(G[:, buf, :], Hb[:, buf, :], ACT.Gelu).then_inc(g_ready, 1)
                if live(s, k, 2):
                    buf, j = (s - 2) % 2, k * 2 + (s - 2)
                    act.wait_ge(gT_filled, j + (BASE + 1))
                    wait(act, o_filled, j + (BASE - 1))
                    act.activation(GT[:, buf, :, :].rearrange("p f t -> p (f t)"), GB[buf][:, :],
                                   ACT.Copy).then_inc(gT_ready, 1)
                if live(s, k, 3):
                    buf, j = (s - 3) % 2, k * 2 + (s - 3)
                    act.wait_ge(y_ready, j + (BASE + 1))
                    act.dma_start(ys[ds(j * P, P), :], Y[:, buf, :]).then_inc(y_stored[buf], 16)

            run_slots(act, slot)

        @block.vector
        def _(dve):
            def slot(s, k):
                if live(s, k, 0):
                    buf, j = s % 2, k * 2 + s
                    dve.wait_ge(xT_filled, j + (BASE + 1))
                    wait(dve, h_filled, j + (BASE - 1))
                    dve.tensor_copy(XT[:, buf, :, :].rearrange("p c t -> p (c t)"),
                                    XB[buf][:, 0:D]).then_inc(xT_ready, 1)
                if live(s, k, 1):
                    buf, j = (s - 1) % 2, k * 2 + (s - 1)
                    e = dve.value_load(tables[0:1, 0, ds(j, 1)], min_val=0, max_val=E - 1)
                    if s == 1:
                        dve.wait_ge(b_loaded, 16 * (nth + 1))
                    wait(dve, g_ready, j + (BASE - 1))
                    dve.wait_ge(h_filled, j + (BASE + 1))
                    dve.tensor_tensor(Hb[:, buf, :], HB[buf][:, :], w["b1"][:, ds(e * F, F)], ALU.add).then_inc(h_ready, 1)
                if live(s, k, 3):
                    buf, j = (s - 3) % 2, k * 2 + (s - 3)
                    e = dve.value_load(tables[0:1, 0, ds(j, 1)], min_val=0, max_val=E - 1)
                    if s == 3:
                        dve.wait_ge(w2_loaded, 48 * (nth + 1))
                    dve.wait_ge(o_filled, j + (BASE + 1))
                    wait(dve, y_stored[buf], stored(s - 3, k, buf))
                    dve.tensor_tensor(Y[:, buf, :], OB[buf][:, 0:D], w["b2"][:, ds(e * D, D)], ALU.add).then_inc(y_ready, 1)

            def stored(s, k, buf):
                return (k + ((s - buf) // 2 + BEFORE[buf])) * 16

            run_slots(dve, slot)

        @block.tensor
        def _(pe):
            def slot(s, k):
                if live(s, k, 0):
                    buf, j = s % 2, k * 2 + s
                    pe.wait_ge(x_loaded[buf], (k + ((s - buf) // 2 + BEFORE[buf] + 1)) * 16)
                    wait(pe, xT_ready, j + (BASE - 1))
                    for c in range(DC):
                        last = pe.transpose(XB[buf][:, c * P:(c + 1) * P], XN[:, buf, c * P:(c + 1) * P], ident[:, :])
                    last.then_inc(xT_filled, 1)
                if live(s, k, 1):
                    buf, j = (s - 1) % 2, k * 2 + (s - 1)
                    e = pe.value_load(tables[0:1, 0, ds(j, 1)], min_val=0, max_val=E - 1)
                    if s == 1:
                        pe.wait_ge(w1_loaded, 16 * (nth + 1))
                    wait(pe, h_ready, j + (BASE - 1))
                    pe.wait_ge(xT_ready, j + (BASE + 1))
                    for c in range(DC):
                        last = pe.matmul(HB[buf][:, :], XT[:, buf, c, :], w["w1"][:, ds(e * (DC * F) + c * F, F)],
                                         start=(c == 0), stop=(c == DC - 1))
                    last.then_inc(h_filled, 1)
                if live(s, k, 2):
                    buf, j = (s - 2) % 2, k * 2 + (s - 2)
                    pe.wait_ge(g_ready, j + (BASE + 1))
                    wait(pe, gT_ready, j + (BASE - 1))
                    for f in range(FC):
                        last = pe.transpose(GB[buf][:, f * P:(f + 1) * P], G[:, buf, f * P:(f + 1) * P], ident[:, :])
                    last.then_inc(gT_filled, 1)
                if live(s, k, 3):
                    buf, j = (s - 3) % 2, k * 2 + (s - 3)
                    e = pe.value_load(tables[0:1, 0, ds(j, 1)], min_val=0, max_val=E - 1)
                    if s == 3:
                        pe.wait_ge(w2_loaded, 48 * (nth + 1))
                    wait(pe, y_ready, j + (BASE - 1))
                    pe.wait_ge(gT_ready, j + (BASE + 1))
                    for f in range(FC):
                        last = pe.matmul(OB[buf][:, 0:D], GT[:, buf, f, :], w["w2"][:, ds(e * (FC * D) + f * D, D)],
                                         start=(f == 0), stop=(f == FC - 1))
                    last.then_inc(o_filled, 1)

            run_slots(pe, slot)


def combine(nc, new_sem, tag, nth, xr, ys, x_out, routing, dims):
    B, S, D = dims[0:3]
    T = S // P
    BASE = nth * B
    GATHERED = 2 * T * 16
    IDX, CW = routing["IDX"], routing["CW"]

    with ExitStack() as ctx:
        def sb(name, shape, dt=F32):
            return ctx.enter_context(nc.sbuf_tensor(f"{tag}_{name}", shape, dt))

        def sem(name):
            return new_sem(f"combine_{name}")

        XR = [sb(f"xr{i}", [P, T, D]) for i in range(2)]
        R = [sb(f"rows{i}", [P, T, 2, D]) for i in range(2)]
        Y = [sb(f"y{i}", [P, T, D]) for i in range(2)]
        idx = [sb(f"idx{i}", [P, T, 2], I32) for i in range(2)]
        cw = [sb(f"cw{i}", [P, T, 2]) for i in range(2)]
        zero = sb("zero", [P, 1])
        carrier = sb("carrier", [P, 1])
        Y_carrier = sb("dve_carrier", [P, 1])

        xr_loaded, gathered = [sem("xr_loaded0"), sem("xr_loaded1")], [sem("gathered0"), sem("gathered1")]
        idx_ready, y_ready, y_stored, half_ready = (
            sem("idx_ready"), sem("y_ready"), [sem("y_stored0"), sem("y_stored1")], sem("half_ready"))
        zeroed, carried = sem("zeroed"), sem("carried")
        block = ctx.enter_context(nc.Block())

        @block.sync
        def _(sp):
            def load_xr(k, i):
                b = k * 2 + i
                wait(sp, y_ready, b + (BASE - 1))
                sp.dma_start(XR[i][:, :, :], xr[b].rearrange("(t p) d -> p t d", p=P)).then_inc(xr_loaded[i], 16)

            def store(k, i):
                b = k * 2 + i
                sp.wait_ge(y_ready, b + (BASE + 1))
                sp.dma_start(x_out[b].rearrange("(t p) d -> p t d", p=P), Y[i][:, :, :]).then_inc(y_stored[i], 16)

            load_xr(0, 0)
            load_xr(0, 1)
            with sp.Fori(0, B // 2 - 1) as k:
                for i in range(2):
                    store(k, i)
                    load_xr(k + 1, i)
            for i in range(2):
                store(B // 2 - 1, i)
            for i in range(2):
                sp.wait_ge(y_stored[i], 16 * ((BASE + B) // 2 + 1))

        @block.gpsimd
        def _(pool):
            pool.memset(zero[:, :], 0.0).then_inc(zeroed, 1)
            if nth == 0:
                pool.memset(carrier[:, :], 0.0).then_inc(carried, 1)
                for i in range(2):
                    pool.memset(Y[i][:, 0, 0:1], 0.0).then_inc(y_stored[i], 16)
            pool.wait_ge(zeroed, nth + 1)
            with pool.Fori(0, B // 2) as k:
                for i in range(2):
                    pool.wait_ge(idx_ready, k * 2 + (i + BASE + 1))
                    pool.wait_ge(carried, k * 2 + (i + BASE + 1))
                    pool.tensor_tensor(carrier[:, :], zero[:, :], zero[:, :], ALU.add).then_inc(carried, 1)
                    for t in range(T):
                        for n in range(2):
                            pool.indirect_dma_start(
                                out=R[i][:, t, n, :], out_offset=None, in_=ys,
                                in_offset=bass.IndirectOffsetOnAxis(ap=idx[i][:, t, n:n + 1], axis=0),
                            ).then_inc(gathered[i], 16)

        @block.vector
        def _(dve):
            def prepare(k, i):
                at = ds((k * 2 + i) * T, T)
                dve.tensor_copy(cw[i][:, :, :], CW[:, at, :])
                dve.tensor_copy(idx[i][:, :, :], IDX[:, at, :]).then_inc(idx_ready, 1)

            def add(k, i):
                b = k * 2 + i
                dve.wait_ge(xr_loaded[i], (k + (BASE // 2 + 1)) * 16)
                dve.wait_ge(gathered[i], (k + (BASE // 2 + 1)) * GATHERED)
                dve.wait_ge(idx_ready, b + (BASE + 1))
                dve.wait_ge(y_stored[i], (k + (BASE // 2 + 1)) * 16)
                for n in range(2):
                    for t in range(T):
                        last = dve.scalar_tensor_tensor(Y[i][:, t, :], R[i][:, t, n, :], cw[i][:, t, n:n + 1],
                                                        Y[i][:, t, :] if n else XR[i][:, t, :], ALU.mult, ALU.add)
                    last.then_inc(half_ready if n == 0 else y_ready, 1)
                    if n == 0:
                        dve.wait_ge(half_ready, b + (BASE + 1))

            prepare(0, 0)
            prepare(0, 1)
            with dve.Fori(0, B // 2 - 1) as k:
                for i in range(2):
                    add(k, i)
                    dve.wait_ge(y_ready, k * 2 + (i + BASE + 1))
                    dve.memset(Y_carrier[:, :], 0.0)
                    prepare(k + 1, i)
            for i in range(2):
                add(B // 2 - 1, i)


def attention_pass(nc, new_sem, tag, xr, ys, x_mid, x_out, bank, ident, ident_b, w, load, routing,
                   B, S, D, H, DK, LSEG):
    T, DC, NSEG, PAIRS = S // P, D // P, S // LSEG, H // 2
    HK = H * DK
    KC = HK // P
    VW = DK + 1
    SCALE = 1.0 / float(np.sqrt(DK))
    QK = 2 * PAIRS
    SLOTS = T + 2
    U = NSEG - 1
    FRONT, PER_TILE = LN_STEPS + 1, 6
    GATHERED = 2 * T * 16
    IDX, CW = routing["IDX"], routing["CW"]
    PLACES = [[("hsT", 0), ("hsT", 1)], [("qk", 0), ("qk", 1)], [("qk", 2), ("qk", 3)], [("qk", 4), ("qk", 5)],
              [("qk", 6), ("qk", 7)], [("v", 0), ("v", 1)], [("v", 2), ("v", 3)], [("sk", 0), ("sk", 1)],
              [("sk", 2), ("sk", 3)], [("mem", 0), ("mem", 1), ("mem", 2)], [("mem", 3), ("mem", 4)],
              [("mem", 5), ("mem", 6)]]
    ORDER = [item for place in PLACES for item in place]
    COUNT = {"hsT": DC, "qk": QK, "v": T, "sk": T, "mem": U}
    assert len(PLACES) == 2 * SLOTS and len(ORDER) == sum(COUNT.values())

    with ExitStack() as ctx:
        def sb(name, shape, dt=F32):
            return ctx.enter_context(nc.sbuf_tensor(f"{tag}_{name}", shape, dt))

        def sem(name):
            return new_sem(f"{tag}_{name}")

        R = sb("rows", [P, T, 2, D])
        idx, cw = sb("idx", [P, T, 2], I32), sb("cw", [P, T, 2])
        zero, pool_carrier = sb("zero", [P, 1]), sb("pool_carrier", [P, 1])
        X, XR, HS, Y = sb("x", [P, T, D]), sb("xr", [P, T, D]), sb("hs", [P, T, D]), sb("y", [P, T, D])
        stats, mv = sb("stats", [P, T, 6]), sb("mv", [P, T, 2])
        ve, sd, rs = sb("ve", [P, T]), sb("sd", [P, T]), sb("rs", [P, T])
        carrier = sb("carrier", [P, 1])
        hsT = sb("hsT", [P, DC, S])
        qk = [sb(f"qk{i}", [P, QK, S]) for i in range(2)]
        sqk = [sb(f"sqk{i}", [P, QK, S]) for i in range(2)]
        low = sb("low", [P, 2, S])
        ex = sb("ex", [P, 2, S])
        sk = sb("sk", [P, T, HK])
        V = [sb(f"V{i}", [P, T, H, VW]) for i in range(2)]
        MEM = [sb(f"MEM{i}", [P, NSEG, PAIRS, VW]) for i in range(2)]
        SS = sb("SS", [P, 2, H, LSEG])
        mx, rr = sb("mx", [P, H]), sb("rr", [P, H])
        PB = [sb(f"PB{i}", [P, H, P]) for i in range(2)]
        PBT = sb("PBT", [P, H, P])
        rz = sb("rz", [P, 2, PAIRS])
        AM = sb("AM", [P, 2, HK])
        AL = sb("AL", [P, HK])
        AT = sb("AT", [P, HK])
        attT = sb("attT", [P, KC, P])

        x_loaded, xr_loaded, y_ready, y_stored = sem("x_loaded"), sem("xr_loaded"), sem("y_ready"), sem("y_stored")
        var_ready, sd_ready, hs_ready = sem("var_ready"), sem("sd_ready"), sem("hs_ready")
        idx_ready, gathered, carried = sem("idx_ready"), sem("gathered"), sem("carried")
        mid_ready, mid_stored = sem("mid_ready"), sem("mid_stored")
        la_loaded, gate_exp, gate_step = sem("loaded"), sem("gate_exp"), sem("gate_step")
        low_ready, ex_ready, sqk_ready = sem("low_ready"), sem("ex_ready"), sem("sqk_ready")
        filled = {kind: sem(f"{kind}_filled") for kind in COUNT}
        drained = {kind: sem(f"{kind}_ready") for kind in COUNT}
        s_filled, s_ready, e_ready, pb_ready = sem("s_filled"), sem("s_ready"), sem("e_ready"), sem("pb_ready")
        pbT_filled, pbT_ready = sem("pbT_filled"), sem("pbT_ready")
        l_filled, am_filled, am_read, at_ready = sem("l_filled"), sem("am_filled"), sem("am_read"), sem("at_ready")
        attT_filled, attT_ready, o_filled = sem("attT_filled"), sem("attT_ready"), sem("o_filled")
        dve_front, dve_tile = sem("dve_front"), sem("dve_tile")
        init = sem("init")
        INIT = 10

        SC, AMB, LB, OB, RING = bank[0:2], bank[2:4], bank[4], bank[5], bank[6:8]

        def ring(kind, i):
            return ORDER.index((kind, i)) % 2

        def run_turns(eng, turn):
            turn(None, 0, 1)
            turn(0, 1, 0)
            with eng.Fori(0, (B - 4) // 2) as k:
                for odd in range(2):
                    b = k * 2 + (1 + odd)
                    turn(b, b + 1, (1 + odd) % 2)
            for b in range(1 + (B - 4) // 2 * 2, B):
                turn(b, b + 1 if b + 1 < B else None, b % 2)

        def has_beyond(n):
            return n is not None and (not isinstance(n, int) or n + 1 < B)

        block = ctx.enter_context(nc.Block())

        @block.sync
        def _(sp):
            def load_x(a):
                sp.dma_start(X[:, :, :], xr[a].rearrange("(t p) d -> p t d", p=P)).then_inc(x_loaded, 16)

            def turn(b, n, par):
                if b is not None:
                    wait(sp, y_ready, b * T)
                    sp.dma_start(XR[:, :, :], x_mid[b].rearrange("(t p) d -> p t d", p=P)).then_inc(xr_loaded, 16)
                if n is not None:
                    sp.wait_ge(mid_ready, n + 1)
                    sp.dma_start(x_mid[n].rearrange("(t p) d -> p t d", p=P), X[:, :, :]).then_inc(mid_stored, 16)
                    sp.wait_ge(mid_stored, n * 16 + 16)
                if has_beyond(n):
                    wait(sp, hs_ready, n + 1)
                    load_x(n + 1)
                if b is not None:
                    wait(sp, y_ready, b * T + T)
                    sp.dma_start(x_out[b].rearrange("(t p) d -> p t d", p=P), Y[:, :, :]).then_inc(y_stored, 16)

            load_x(0)
            load(sp, la_loaded)
            run_turns(sp, turn)
            sp.wait_ge(y_stored, 16 * B)

        @block.gpsimd
        def _(pool):
            for i in range(2):
                pool.memset(V[i][:, :, :, DK:VW], 1.0).then_inc(init, 1)
                pool.memset(MEM[i][:, 0, :, 0:DK], 0.0).then_inc(init, 1)
                pool.memset(MEM[i][:, 0, :, DK:VW], 1.0 / DK).then_inc(init, 1)
            for i in range(2):
                pool.memset(PB[i][:, :, :], 0.0).then_inc(init, 1)
            pool.memset(zero[:, :], 0.0).then_inc(init, 1)
            pool.memset(pool_carrier[:, :], 0.0).then_inc(init, 1)

            def gather(a):
                pool.wait_ge(idx_ready, a + 1)
                wait(pool, carried, a)
                pool.tensor_tensor(pool_carrier[:, :], zero[:, :], zero[:, :], ALU.add).then_inc(carried, 1)
                for t in range(T):
                    for n in range(2):
                        pool.indirect_dma_start(
                            out=R[:, t, n, :], out_offset=None, in_=ys,
                            in_offset=bass.IndirectOffsetOnAxis(ap=idx[:, t, n:n + 1], axis=0),
                        ).then_inc(gathered, 16)

            def turn(b, n, par):
                if has_beyond(n):
                    gather(n + 1)

            pool.wait_ge(init, INIT)
            gather(0)
            run_turns(pool, turn)

        @block.scalar
        def _(act):
            def root(a):
                act.wait_ge(var_ready, a + 1)
                act.activation(sd[:, :], ve[:, :], ACT.Sqrt).then_inc(sd_ready, 1)

            def evacuate(kind, i, n, par):
                if kind == "mem":
                    return
                act.wait_ge(filled[kind], n * COUNT[kind] + i + 1)
                source = RING[ring(kind, i)]
                if kind == "hsT":
                    act.activation(hsT[:, i, :], source, ACT.Copy).then_inc(drained[kind], 1)
                if kind == "qk":
                    act.activation(qk[par][:, i, :], source, ACT.Copy).then_inc(drained[kind], 1)
                if kind == "v":
                    act.activation(V[par][:, i, :, 0:DK], source.rearrange("p (h v) -> p h v", v=DK),
                                   ACT.Copy).then_inc(drained[kind], 1)
                if kind == "sk":
                    if i == 0:
                        wait(act, filled["mem"], n * U)
                    act.activation(sk[:, i, :], source, ACT.Copy).then_inc(drained[kind], 1)

            def exponential(i, n):
                act.wait_ge(low_ready, n * QK + i + 1)
                wait(act, sqk_ready, n * QK + i - 1)
                act.activation(ex[:, i % 2, :], low[:, i % 2, :], ACT.Exp).then_inc(ex_ready, 1)

            def prepare(place, n, par):
                for kind, i in PLACES[place][1 if place % 2 == 0 else 0:]:
                    evacuate(kind, i, n, par)
                for kind, i in PLACES[place - 1] if place else []:
                    if kind == "qk":
                        exponential(i, n)

            def turn(b, n, par):
                for slot in range(SLOTS):
                    if b is not None and slot < T:
                        act.wait_ge(s_ready, b * T + slot + 1)
                        act.activation(SS[:, slot % 2, :, :], SS[:, slot % 2, :, :], ACT.Exp,
                                       scale=SCALE).then_inc(e_ready, 1)
                    if n is not None:
                        evacuate(*PLACES[2 * slot][0], n, 1 - par)
                    if b is not None and slot >= 2:
                        g = b * T + (slot - 2)
                        act.wait_ge(attT_filled, g + 1)
                        wait(act, o_filled, g)
                        act.activation(attT[:, :, :].rearrange("p c i -> p (c i)"), OB, ACT.Copy).then_inc(attT_ready, 1)
                    if n is not None:
                        prepare(2 * slot, n, 1 - par)
                    if b is not None and 1 <= slot <= T:
                        g = b * T + (slot - 1)
                        for half in range(2):
                            act.wait_ge(pbT_filled, g * 2 + half + 1)
                            if half == 0:
                                wait(act, l_filled, g)
                            act.activation(PBT[:, half * PAIRS:(half + 1) * PAIRS, :].rearrange("p h i -> p (h i)"),
                                           (LB, OB)[half], ACT.Copy).then_inc(pbT_ready, 1)
                    if n is not None:
                        prepare(2 * slot + 1, n, 1 - par)
                    if has_beyond(n) and slot == T:
                        root(n + 1)

            act.wait_ge(init, INIT)
            act.wait_ge(la_loaded, 80)
            act.activation(w["gate"][:, :], w["gate"][:, :], ACT.Exp, scale=-1.0).then_inc(gate_exp, 1)
            root(0)
            run_turns(act, turn)

        @block.vector
        def _(dve):
            def call_for_rows(a):
                at = ds(a * T, T)
                dve.tensor_copy(cw[:, :, :], CW[:, at, :])
                dve.tensor_copy(idx[:, :, :], IDX[:, at, :]).then_inc(idx_ready, 1)

            def combine_rows(a, s):
                dve.wait_ge(x_loaded, a * 16 + 16)
                dve.wait_ge(gathered, (a + 1) * GATHERED)
                dve.wait_ge(idx_ready, a + 1)
                for n in range(2):
                    for t in range(T):
                        last = dve.scalar_tensor_tensor(X[:, t, :], R[:, t, n, :], cw[:, t, n:n + 1], X[:, t, :],
                                                        ALU.mult, ALU.add)
                    if n == 0:
                        s.own(last)
                last.then_inc(mid_ready, 1)
                dve.wait_ge(mid_ready, a + 1)
                if not isinstance(a, int) or a + 1 < B:
                    call_for_rows(a + 1)

            def variance(a, s):
                ln_variance(dve, s, X, stats, mv, ve, T, var_ready, carrier[:, :])

            def normalise(a, s):
                wait(dve, filled["hsT"], a * DC)
                ln_normalise(dve, s, X, HS, mv, ve, sd, rs, T, sd_ready, hs_ready, a)
                s.end()

            def subtract_maximum(t, g, s):
                dve.wait_ge(s_filled, g + 1)
                for n in range(2):
                    sc = SC[n][:, 0:PAIRS * LSEG].rearrange("p (h j) -> p h j", j=LSEG)
                    last = dve.tensor_reduce(mx[:, n * PAIRS:(n + 1) * PAIRS], sc, AX.X, ALU.max)
                s.own(last)
                for n in range(2):
                    sc = SC[n][:, 0:PAIRS * LSEG].rearrange("p (h j) -> p h j", j=LSEG)
                    last = dve.tensor_tensor(SS[:, t % 2, n * PAIRS:(n + 1) * PAIRS, :], sc,
                                             mx[:, n * PAIRS:(n + 1) * PAIRS].unsqueeze(2).to_broadcast([P, PAIRS, LSEG]),
                                             ALU.subtract)
                last.then_inc(s_ready, 1)

            def put_out(t, b, g):
                if t == 0:
                    wait(dve, y_stored, b * 16)
                    dve.wait_ge(xr_loaded, b * 16 + 16)
                dve.wait_ge(o_filled, g + 1)
                dve.tensor_tensor(Y[:, t, :], OB[:, 0:D], XR[:, t, :], ALU.add).then_inc(y_ready, 1)

            def probabilities(t, g, s):
                dve.wait_ge(e_ready, g + 1)
                s.own(dve.tensor_reduce(rr[:, :], SS[:, t % 2, :, :], AX.X, ALU.add))
                s.own(dve.reciprocal(rr[:, :], rr[:, :]))
                wait(dve, pbT_filled, (g - 1) * 2)
                for n in range(2):
                    half = slice(n * LSEG, (n + 1) * LSEG)
                    last = dve.tensor_tensor(PB[t % 2][half, :, half], SS[half, t % 2, :, :],
                                             rr[half, :].unsqueeze(2).to_broadcast([LSEG, H, LSEG]), ALU.mult)
                last.then_inc(pb_ready, 1)

            def from_memory(t, g, s):
                dve.wait_ge(am_filled, g + 1)
                by_head = AM[:, t % 2, :].rearrange("p (c two v) -> p two c v", two=2, v=DK)
                for n in range(2):
                    am = AMB[n][:, 0:PAIRS * VW].rearrange("p (c v) -> p c v", v=VW)
                    last = dve.reciprocal(rz[:, n, :], am[:, :, DK])
                s.own(last)
                for n in range(2):
                    am = AMB[n][:, 0:PAIRS * VW].rearrange("p (c v) -> p c v", v=VW)
                    last = dve.tensor_tensor(by_head[:, n, :, :], am[:, :, 0:DK],
                                             rz[:, n, :].unsqueeze(2).to_broadcast([P, PAIRS, DK]), ALU.mult)
                last.then_inc(am_read, 1)
                dve.wait_ge(am_read, g + 1)
                s.own(dve.tensor_tensor(AM[:, t % 2, :], AM[:, t % 2, :], w["gate"][:, :], ALU.mult))

            def add_up(t, g, s):
                dve.wait_ge(l_filled, g + 1)
                s.own(dve.tensor_tensor(AL[:, :], LB, w["omg"][:, :], ALU.mult))
                wait(dve, attT_filled, g)
                dve.tensor_tensor(AT[:, :], AM[:, t % 2, :], AL[:, :], ALU.add).then_inc(at_ready, 1)

            def prepare(place, n, par):
                for kind, i in PLACES[place - 1] if place else []:
                    if kind == "qk":
                        dve.wait_ge(ex_ready, n * QK + i + 1)
                        dve.scalar_tensor_tensor(sqk[par][:, i, :], qk[par][:, i, :], 0.0, ex[:, i % 2, :],
                                                 ALU.max, ALU.add).then_inc(sqk_ready, 1)
                for kind, i in PLACES[place]:
                    if kind == "qk":
                        dve.wait_ge(drained["qk"], n * QK + i + 1)
                        wait(dve, ex_ready, n * QK + i - 1)
                        dve.tensor_scalar(low[:, i % 2, :], qk[par][:, i, :], 0.0, None, ALU.min).then_inc(low_ready, 1)
                    if kind == "mem":
                        dve.wait_ge(filled["mem"], n * U + i + 1)
                        if i >= 1:
                            dve.wait_ge(drained["mem"], n * U + i)
                        dve.tensor_tensor(MEM[par][:, i + 1, :, :], MEM[par][:, i, :, :],
                                          RING[ring("mem", i)][:, 0:PAIRS * VW].rearrange("p (h v) -> p h v", v=VW),
                                          ALU.add).then_inc(drained["mem"], 1)

            def turn(b, n, par):
                s = Steps(dve, dve_tile, b, PER_TILE * T) if b is not None else None
                beyond = Steps(dve, dve_front, n + 1, FRONT) if has_beyond(n) else None
                for slot in range(SLOTS):
                    tile = b is not None and slot < T
                    if tile:
                        subtract_maximum(slot, b * T + slot, s)
                    if tile:
                        from_memory(slot, b * T + slot, s)
                        probabilities(slot, b * T + slot, s)
                    if n is not None:
                        prepare(2 * slot, n, 1 - par)
                    if b is not None and slot >= 2:
                        put_out(slot - 2, b, b * T + (slot - 2))
                    if n is not None:
                        prepare(2 * slot + 1, n, 1 - par)
                    if b is not None and 1 <= slot <= T:
                        add_up(slot - 1, b * T + (slot - 1), s)
                    if has_beyond(n) and slot >= T - 1:
                        (combine_rows, variance, normalise)[slot - (T - 1)](n + 1, beyond)
                for steps in (s, beyond):
                    if steps is not None:
                        steps.end()

            dve.wait_ge(init, INIT)
            call_for_rows(0)
            dve.wait_ge(gate_exp, 1)
            dve.tensor_scalar(w["gate"][:, :], w["gate"][:, :], 1.0, None, ALU.add).then_inc(gate_step, 1)
            dve.wait_ge(gate_step, 1)
            dve.reciprocal(w["gate"][:, :], w["gate"][:, :]).then_inc(gate_step, 1)
            dve.wait_ge(gate_step, 2)
            dve.tensor_scalar(w["omg"][:, :], w["gate"][:, :], -1.0, 1.0, ALU.mult, ALU.add).then_inc(gate_step, 1)
            dve.wait_ge(gate_step, 3)
            s = Steps(dve, dve_front, 0, FRONT)
            for stage in (combine_rows, variance, normalise):
                stage(0, s)
            run_turns(dve, turn)

        @block.tensor
        def _(pe):
            def carry(free):
                pe.matmul(free[:, 510:512], ident_b[:, :], ident_b[:, 0:2], start=True, stop=True)

            def turn_out(g):
                pe.wait_ge(at_ready, g + 1)
                for c in range(KC):
                    last = pe.transpose(OB[:, c * P:(c + 1) * P], AT[:, c * P:(c + 1) * P], ident[:, :])
                last.then_inc(attT_filled, 1)

            def project_out(g):
                pe.wait_ge(attT_ready, g + 1)
                for c in range(KC):
                    last = pe.matmul(OB[:, 0:D], attT[:, c, :], w["la_o"][:, c, :],
                                     start=(c == 0), stop=(c == KC - 1))
                last.then_inc(o_filled, 1)

            def score(t, g, par):
                if not isinstance(g, int) or g >= 1:
                    pe.wait_ge(s_ready, g)
                carry(SC[0])
                for h in range(H):
                    pair, one = h // 2, h % 2
                    part = slice(one * DK, (one + 1) * DK)
                    for n in range(2):
                        seg = slice((2 * t + n) * LSEG, (2 * t + n + 1) * LSEG)
                        last = pe.matmul(SC[one][n * LSEG:(n + 1) * LSEG, pair * LSEG:(pair + 1) * LSEG],
                                         qk[par][part, pair, seg], qk[par][part, PAIRS + pair, seg], start=True, stop=True)
                last.then_inc(s_filled, 1)

            def recall(t, g, par):
                wait(pe, am_read, g)
                carry(AMB[0])
                for h in range(H):
                    pair, one = h // 2, h % 2
                    part = slice(one * DK, (one + 1) * DK)
                    for n in range(2):
                        seg = slice((2 * t + n) * LSEG, (2 * t + n + 1) * LSEG)
                        last = pe.matmul(AMB[one][n * LSEG:(n + 1) * LSEG, pair * VW:(pair + 1) * VW],
                                         sqk[par][part, pair, seg], MEM[par][part, 2 * t + n, pair, :], start=True, stop=True)
                last.then_inc(am_filled, 1)

            def turn_probabilities(t, g):
                pe.wait_ge(pb_ready, g + 1)
                for half in range(2):
                    if half == 1:
                        wait(pe, y_ready, g)
                    for i in range(PAIRS):
                        last = pe.transpose((LB, OB)[half][:, i * P:(i + 1) * P], PB[t % 2][:, half * PAIRS + i, :], ident[:, :])
                    last.then_inc(pbT_filled, 1)

            def weigh(t, g, par):
                pe.wait_ge(pbT_ready, (g + 1) * 2)
                for h in range(H):
                    last = pe.matmul(LB[:, h * DK:(h + 1) * DK], PBT[:, (h % 2) * PAIRS + h // 2, :],
                                     V[par][:, t, h, 0:DK], start=True, stop=True)
                last.then_inc(l_filled, 1)

            def ring_free(kind, i, n):
                at = ORDER.index((kind, i))
                if at >= 2:
                    before, j = ORDER[at - 2]
                    wait(pe, drained[before], n * COUNT[before] + j + 1)
                else:
                    wait(pe, drained["mem"], n * U)

            def item(kind, i, n, par):
                ring_free(kind, i, n)
                to = RING[ring(kind, i)]
                if kind == "hsT":
                    pe.wait_ge(hs_ready, n + 1)
                    for t in range(T):
                        last = pe.transpose(to[:, t * P:(t + 1) * P], HS[:, t, i * P:(i + 1) * P], ident[:, :])
                if kind == "qk":
                    if i == 0:
                        pe.wait_ge(drained["hsT"], (n + 1) * DC)
                    weight = w["la_q"] if i < PAIRS else w["la_k"]
                    pair = i % PAIRS
                    for c in range(DC):
                        last = pe.matmul(to, weight[:, c, pair * P:(pair + 1) * P], hsT[:, c, :],
                                         start=(c == 0), stop=(c == DC - 1))
                if kind == "v":
                    for c in range(DC):
                        last = pe.matmul(to, hsT[:, c, i * P:(i + 1) * P], w["la_v"][:, c, :],
                                         start=(c == 0), stop=(c == DC - 1))
                if kind == "sk":
                    if i == 0:
                        pe.wait_ge(sqk_ready, (n + 1) * QK)
                    for pair in range(PAIRS):
                        last = pe.transpose(to[:, pair * P:(pair + 1) * P],
                                            sqk[par][:, PAIRS + pair, i * P:(i + 1) * P], ident[:, :])
                if kind == "mem":
                    if i == 0:
                        pe.wait_ge(drained["v"], (n + 1) * T)
                        pe.wait_ge(drained["sk"], (n + 1) * T)
                    carry(to)
                    t, rows = i // 2, slice((i % 2) * LSEG, (i % 2 + 1) * LSEG)
                    for h in range(H):
                        pair, one = h // 2, h % 2
                        last = pe.matmul(to[one * DK:(one + 1) * DK, pair * VW:(pair + 1) * VW],
                                         sk[rows, t, h * DK:(h + 1) * DK], V[par][rows, t, h, :], start=True, stop=True)
                last.then_inc(filled[kind], 1)

            def turn(b, n, par):
                if b is not None:
                    pe.wait_ge(drained["mem"], (b + 1) * U)
                for slot in range(SLOTS):
                    if b is not None and slot < T:
                        score(slot, b * T + slot, par)
                        recall(slot, b * T + slot, par)
                    places = PLACES[2 * slot] if n is not None else []
                    for kind, i in places[:1]:
                        item(kind, i, n, 1 - par)
                    if b is not None and slot >= 2:
                        turn_out(b * T + (slot - 2))
                    for kind, i in places[1:]:
                        item(kind, i, n, 1 - par)
                    if b is not None and slot >= 2:
                        project_out(b * T + (slot - 2))
                    if b is not None and 1 <= slot <= T:
                        turn_probabilities(slot - 1, b * T + (slot - 1))
                    for kind, i in PLACES[2 * slot + 1] if n is not None else []:
                        item(kind, i, n, 1 - par)
                    if b is not None and 1 <= slot <= T:
                        weigh(slot - 1, b * T + (slot - 1), par)

            pe.wait_ge(init, INIT)
            pe.wait_ge(la_loaded, 80)
            run_turns(pe, turn)


def macaron(nc, x, Wq, Wk, Wv, betas, Wo, q_w, q_b, k_w, k_b, v_w, v_b, o_w, o_b,
            router_w, router_b, w1, b1, w2, b2, out):
    B, S, D = x.shape
    E, _, F = w1.shape
    H = 16
    LAT = k_w.shape[1]
    KPH, HD = LAT // H, D // H
    AH, ADK = betas.shape[1], betas.shape[3]
    LSEG = 64
    DC, FC = D // P, F // P
    TOKENS = B * S
    REG = region_rows(TOKENS)
    NT = 2 * TOKENS // P + E - 1
    assert LAT == P and AH * ADK == Wq.shape[1]

    with ExitStack() as ctx:
        def sb(name, shape, dt=F32):
            return ctx.enter_context(nc.sbuf_tensor(name, shape, dt))

        semaphores = {}

        def sem(name):
            if name not in semaphores:
                semaphores[name] = ctx.enter_context(nc.semaphore(name))
            return semaphores[name]

        bank = [ctx.enter_context(nc.psum_tensor(f"bank{i}", [P, 512], F32))[:, :] for i in range(8)]
        ident = sb("ident", [P, P])
        tri = sb("tri", [P, E, E])
        w = {
            "q_w": sb("q_w", [P, DC, LAT]), "k_w": sb("k_w", [P, DC, LAT]), "v_w": sb("v_w", [P, DC, LAT]),
            "q_bs": sb("q_bs", [P, 1]), "k_b": sb("k_b", [P, 1]), "v_b": sb("v_b", [P, LAT]),
            "o_w": sb("o_w", [P, D]), "o_b": sb("o_b", [P, DC]),
            "router_w": sb("router_w", [P, DC, E]), "router_b": sb("router_b", [P, E]),
            "o_b_row": sb("o_b_row", [P, D]),
            "ident_b": sb("ident_b", [P, P], BF16), "ones_b": sb("ones_b", [P, P], BF16),
            "before_b": sb("before_b", [P, P], BF16),
            "region": sb("region", [P, E]), "partition": sb("partition", [P, 1]),
            "rung": sb("rung", [P, B * S // P + 1]), "tile": sb("tile", [P, NT]),
        }
        x1 = nc.dram_tensor("x1", (B, S, D), F32, kind="Internal").ap()
        x2 = nc.dram_tensor("x2", (B, S, D), F32, kind="Internal").ap()
        xr = nc.dram_tensor("xr", (B, S, D), F32, kind="Internal").ap()
        xs = nc.dram_tensor("routed_rows", (E * REG, D), F32, kind="Internal").ap()
        ys = nc.dram_tensor("expert_rows", (NT * P, D), F32, kind="Internal").ap()
        routing = {"ROW": sb("ROW", [P, TOKENS // P, 2]), "IDX": sb("IDX", [P, TOKENS // P, 2], I32), "CW": sb("CW", [P, TOKENS // P, 2]),
                   "start_row": sb("start_row", [P, E]), "tables": sb("tables", [P, 2, NT], I32)}
        scratch = [nc.dram_tensor(n, s, BF16, kind="Internal").ap() for n, s in
                   (("q_parts", (3, P, S)), ("k_parts", (3, P, S)), ("m_parts", (4, 3 * H // 4, S)))]

        loaded, q_full_loaded, made, zeroed, diag = (
            sem("loaded"), sem("q_full_loaded"), sem("made"), sem("zeroed"), sem("diag"))

        w1_loaded, w2_loaded, b_loaded = sem("w1_loaded"), sem("w2_loaded"), sem("b_loaded")

        def load_and_make():
            with ExitStack() as inner:
                q_full = inner.enter_context(nc.sbuf_tensor("q_full", [P, DC, D], F32))
                ones = inner.enter_context(nc.sbuf_tensor("ones", [P, E, E], F32))
                RUNGS = TOKENS // P + 1
                counts = inner.enter_context(nc.sbuf_tensor("counts", [P, 1 + E + RUNGS + NT], I32))
                block = inner.enter_context(nc.Block())

                plain = [
                    (w["k_w"][:, :, :], k_w.rearrange("(c p) n -> p c n", p=P)),
                    (w["v_w"][:, :, :], v_w.rearrange("(c p) n -> p c n", p=P)),
                    (w["k_b"][:, :], k_b.rearrange("(p one) -> p one", one=1)),
                    (w["v_b"][:, :], v_b.partition_broadcast(P)),
                    (w["o_w"][:, :], o_w[0:LAT, :]),
                    (w["o_b"][:, 0:1], o_b[0:P].rearrange("(p one) -> p one", one=1)),
                    (w["o_b"][:, 1:2], o_b[P:2 * P].rearrange("(p one) -> p one", one=1)),
                    (w["router_w"][:, :, :], router_w.rearrange("(c p) n -> p c n", p=P)),
                    (w["router_b"][:, :], router_b.partition_broadcast(P)),
                    (w["o_b_row"][:, :], o_b.partition_broadcast(P)),
                ]
                QB = 16 * (len(plain) + H)

                @block.sync
                def _(sp):
                    sp.dma_start(q_full[:, :, :], q_w.rearrange("(c p) n -> p c n", p=P)).then_inc(q_full_loaded, 16)
                    for h in range(H):
                        sp.dma_start(w["q_bs"][h * KPH:(h + 1) * KPH, :],
                                     q_b[h * HD:h * HD + KPH].rearrange("(p one) -> p one", one=1)).then_inc(loaded, 16)
                    for to, source in plain:
                        sp.dma_start(to, source).then_inc(loaded, 16)

                @block.gpsimd
                def _(pool):
                    pool.memset(w["ones_b"][:, :], 1.0).then_inc(zeroed, 1)
                    pool.memset(ident[:, :], 0.0).then_inc(zeroed, 1)
                    pool.memset(ones[:, :, :], 1.0).then_inc(zeroed, 1)
                    pool.wait_ge(zeroed, 3)
                    pool.affine_select(out=ident[:, :], in_=ident[:, :], compare_op=ALU.not_equal, fill=1.0,
                                       base=0, pattern=[[-1, P]], channel_multiplier=1).then_inc(diag, 1)
                    pool.affine_select(out=tri[:, :, :], in_=ones[:, :, :], compare_op=ALU.is_gt, fill=0.0,
                                       base=0, pattern=[[1, E], [-1, E]], channel_multiplier=0).then_inc(diag, 1)
                    pool.affine_select(out=w["before_b"][:, :], in_=w["ones_b"][:, :], compare_op=ALU.is_gt, fill=0.0,
                                       base=0, pattern=[[1, P]], channel_multiplier=-1).then_inc(diag, 1)
                    pool.iota(counts[:, 0:1], pattern=[[0, 1]], base=0, channel_multiplier=1).then_inc(diag, 1)
                    pool.iota(counts[:, 1:1 + E], pattern=[[REG, E]], base=0, channel_multiplier=0).then_inc(diag, 1)
                    pool.iota(counts[:, 1 + E:1 + E + RUNGS], pattern=[[P, RUNGS]], base=0,
                              channel_multiplier=0).then_inc(diag, 1)
                    pool.iota(counts[:, 1 + E + RUNGS:], pattern=[[1, NT]], base=0, channel_multiplier=0).then_inc(diag, 1)

                @block.vector
                def _(dve):
                    dve.wait_ge(diag, 7)
                    dve.tensor_copy(w["ident_b"][:, :], ident[:, :]).then_inc(made, 1)
                    dve.tensor_copy(w["partition"][:, :], counts[:, 0:1]).then_inc(made, 1)
                    dve.tensor_copy(w["region"][:, :], counts[:, 1:1 + E]).then_inc(made, 1)
                    dve.tensor_copy(w["rung"][:, :], counts[:, 1 + E:1 + E + RUNGS]).then_inc(made, 1)
                    dve.tensor_copy(w["tile"][:, :], counts[:, 1 + E + RUNGS:]).then_inc(made, 1)
                    dve.wait_ge(q_full_loaded, 16)
                    for c in range(DC):
                        dve.tensor_copy(w["q_w"][:, c, :].rearrange("p (h k) -> p h k", k=KPH),
                                        q_full[:, c, :].rearrange("p (h x) -> p h x", x=HD)[:, :, 0:KPH]).then_inc(made, 1)
                    dve.wait_ge(loaded, QB)
                    dve.tensor_scalar(w["q_bs"][:, :], w["q_bs"][:, :], 1.0 / float(np.sqrt(KPH)), None,
                                      ALU.mult).then_inc(made, 1)
                    dve.wait_ge(made, 5 + DC + 1)

        dims = (B, S, D, H, HD, KPH, E, F)

        def attend_and_apply_experts(tag, nth, x_in):
            with nc.sbuf_tensor(f"{tag}_w1", [P, E * DC * F], F32) as room, \
                    nc.sbuf_tensor(f"{tag}_b1", [P, E * F], F32) as room_b1:
                w["w1"], w["b1"] = room, room_b1

                def load_w1(sp):
                    sp.dma_start(room[:, :].rearrange("p (e c f) -> p e c f", e=E, c=DC),
                                 w1.rearrange("e (c p) f -> p e c f", p=P)).then_inc(w1_loaded, 16)
                    sp.dma_start(room_b1[:, :], b1.rearrange("e f -> (e f)").partition_broadcast(P)).then_inc(b_loaded, 16)

                attend_and_route(nc, sem, tag, nth, x_in, xr, xs, bank, ident, tri, w, scratch, routing, dims, load_w1)
                tiles_of_experts(tag, nth)

        def tiles_of_experts(tag, nth):
            with ExitStack() as inner:
                w["w2"] = inner.enter_context(nc.sbuf_tensor(f"{tag}_w2", [P, E * FC * D], F32))
                w["b2"] = inner.enter_context(nc.sbuf_tensor(f"{tag}_b2", [P, E * D], F32))

                def load_w2(sp, part):
                    es = slice(part * E // 2, (part + 1) * E // 2)
                    sp.dma_start(w["w2"][:, :].rearrange("p (e c d) -> p e c d", e=E, c=FC)[:, es, :, :],
                                 w2.rearrange("e (c p) d -> p e c d", p=P)[:, es, :, :]).then_inc(w2_loaded, 16)

                def load(sp):
                    load_w2(sp, 0)
                    sp.dma_start(w["b2"][:, :], b2.rearrange("e d -> (e d)").partition_broadcast(P)).then_inc(w2_loaded, 16)

                tile_tables(nc, sem, tag + "t", nth, w, tri, routing, TOKENS, E, NT, load)
                experts(nc, sem, tag + "m", nth, xs, ys, bank, ident, w, (w1_loaded, w2_loaded, b_loaded),
                        lambda sp: load_w2(sp, 1), routing, dims, NT)


        load_and_make()
        attend_and_apply_experts("f1", 0, x)

        with ExitStack() as inner:
            HK = AH * ADK
            KC = HK // P
            la = {"la_q": [P, DC, HK], "la_k": [P, DC, HK], "la_v": [P, DC, HK], "la_o": [P, KC, D],
                  "gate": [P, HK], "omg": [P, HK]}
            la = {k: inner.enter_context(nc.sbuf_tensor(k, s, F32)) for k, s in la.items()}

            def load_la(sp, loaded):
                for k, source in (("la_q", Wq), ("la_k", Wk), ("la_v", Wv), ("la_o", Wo)):
                    sp.dma_start(la[k][:, :, :], source.rearrange("(c p) n -> p c n", p=P)).then_inc(loaded, 16)
                sp.dma_start(la["gate"][:, :], betas.rearrange("a h b v -> (a h b v)").partition_broadcast(P)) \
                  .then_inc(loaded, 16)

            attention_pass(nc, sem, "la", xr, ys, x1, x2, bank, ident, w["ident_b"], la, load_la, routing, B, S, D, AH, ADK, LSEG)

        attend_and_apply_experts("f2", 1, x2)
        combine(nc, sem, "fc", 0, xr, ys, out, routing, dims)


_INS = ["L0_attn_x", "L0_attn_Wq", "L0_attn_Wk", "L0_attn_Wv", "L0_attn_betas", "L0_attn_Wo",
        "L0_ffn_q_w", "L0_ffn_q_b", "L0_ffn_k_w", "L0_ffn_k_b", "L0_ffn_v_w", "L0_ffn_v_b",
        "L0_ffn_o_w", "L0_ffn_o_b", "L0_ffn_router_w", "L0_ffn_router_b",
        "L0_ffn_w1", "L0_ffn_b1", "L0_ffn_w2", "L0_ffn_b2"]


def kernel(**inputs):
    import concourse.bacc as bacc
    from concourse.bass_utils import run_bass_kernel_spmd

    nc = bacc.Bacc("TRN2", target_bir_lowering=False, num_devices=1)
    arrays, args = {}, []
    for name in _INS:
        a = np.asarray(inputs[name])
        a = np.ascontiguousarray(a)
        arrays[f"in_{name}"] = a
        args.append(nc.dram_tensor(f"in_{name}", a.shape, mybir.dt.from_np(a.dtype), kind="ExternalInput").ap())
    shape = inputs["L0_attn_x"].shape
    out = nc.dram_tensor("out", shape, F32, kind="ExternalOutput").ap()
    macaron(nc, *args, out)
    result = run_bass_kernel_spmd(nc, [arrays], core_ids=[0])
    return result.results[0]["out"]
```
